# Optimizing a Trainium2 kernel written in Bass

```python
import numpy as np
import jax
import jax.numpy as jnp

def _softmax(x, axis=-1):
    return jax.nn.softmax(x, axis=axis)

def _gelu(x):
    return jax.nn.gelu(x, approximate=True)

def _silu(x):
    return jax.nn.silu(x)

def _sigmoid(x):
    return jax.nn.sigmoid(x)

def _layernorm(x, axis=-1, eps=1e-05):
    m = jnp.mean(x, axis=axis, keepdims=True)
    v = jnp.var(x, axis=axis, keepdims=True)
    return (x - m) / jnp.sqrt(v + eps)

def _scatter_add(tgt, idx, src, axis=0):
    return tgt.at[idx].add(src)

def _segment_sum(src, seg, n):
    return jax.ops.segment_sum(src, seg, n)
kernel_name = 'mk_hybrid_d2_jaxref_r8_ec003d'

def setup_inputs(seed: int=0):
    np.random.seed(seed)
    _w = jnp.asarray

    def _L0_attn_a_setup():
        import jax, jax.numpy as jnp
        import numpy as np
        import math
        D_MODEL = 256
        D_STATE = 16
        DT_RANK = math.ceil(D_MODEL / 16)
        DT_MIN, DT_MAX, DT_INIT_FLOOR = (0.001, 0.1, 0.0001)

        def _selective_scan(u, delta, A, Bmat, Cmat, D):
            b, l, d = u.shape
            n = A.shape[1]

            def step(h, inp):
                u_t, delta_t, B_t, C_t = inp
                dA = jnp.exp(delta_t[:, :, None] * A)
                dBu = (delta_t * u_t)[:, :, None] * B_t[:, None, :]
                h = dA * h + dBu
                y_t = jnp.einsum('bdn,bn->bd', h, C_t)
                return (h, y_t)
            h0 = jnp.zeros((b, d, n), dtype=u.dtype)
            xs = (jnp.swapaxes(u, 0, 1), jnp.swapaxes(delta, 0, 1), jnp.swapaxes(Bmat, 0, 1), jnp.swapaxes(Cmat, 0, 1))
            _, ys = jax.lax.scan(step, h0, xs)
            y = jnp.swapaxes(ys, 0, 1)
            return y + u * D
        key = jax.random.key(seed)
        k1, k2, k3, k4 = jax.random.split(key, 4)
        B, L = (4, 256)
        hidden_states = jax.random.normal(k1, (B, L, D_MODEL), dtype=jnp.float32)
        fan_in = D_MODEL
        bound = 1.0 / math.sqrt(fan_in)
        x_proj_w = jax.random.uniform(k2, (DT_RANK + 2 * D_STATE, D_MODEL), minval=-bound, maxval=bound, dtype=jnp.float32)
        dt_init_std = DT_RANK ** (-0.5)
        dt_proj_w = jax.random.uniform(k3, (D_MODEL, DT_RANK), minval=-dt_init_std, maxval=dt_init_std, dtype=jnp.float32)
        dt = jnp.exp(jax.random.uniform(k4, (D_MODEL,), dtype=jnp.float32) * (math.log(DT_MAX) - math.log(DT_MIN)) + math.log(DT_MIN))
        dt = jnp.clip(dt, DT_INIT_FLOOR, None)
        dt_proj_b = dt + jnp.log(-jnp.expm1(-dt))
        A_log = jnp.log(jnp.broadcast_to(jnp.arange(1, D_STATE + 1, dtype=jnp.float32), (D_MODEL, D_STATE)))
        D = jnp.ones((D_MODEL,), dtype=jnp.float32)
        return {'hidden_states': hidden_states, 'x_proj_w': x_proj_w, 'dt_proj_w': dt_proj_w, 'dt_proj_b': dt_proj_b, 'A_log': A_log, 'D': D}
    _L0_attn_a_in = _L0_attn_a_setup()

    def _L0_attn_b_setup():
        import jax, jax.numpy as jnp
        import numpy as np
        DIM = 256
        DIM_HEAD = 128
        HEADS = 16
        EPS = 1e-05

        def _rotate_half(t):
            d2 = t.shape[-1] // 2
            x1, x2 = (t[..., :d2], t[..., d2:])
            return jnp.concatenate([-x2, x1], axis=-1)

        def _rotary_pos(n, dim_head, dtype):
            inv_freq = 1.0 / 10000.0 ** (jnp.arange(0, dim_head, 2, dtype=jnp.float32) / dim_head)
            freqs = jnp.arange(n, dtype=jnp.float32)[:, None] * inv_freq[None, :]
            return jnp.concatenate([freqs, freqs], axis=-1).astype(dtype)
        key = jax.random.key(seed)
        ks = jax.random.split(key, 4)
        b, n = (2, 256)
        x = jax.random.normal(ks[0], (b, n, DIM), dtype=jnp.float32)
        gamma = jnp.ones((DIM,), dtype=jnp.float32)
        Wq = jax.random.normal(ks[1], (DIM, HEADS * DIM_HEAD), dtype=jnp.float32) * DIM ** (-0.5)
        Wkv = jax.random.normal(ks[2], (DIM, 2 * DIM_HEAD), dtype=jnp.float32) * DIM ** (-0.5)
        Wo = jax.random.normal(ks[3], (HEADS * DIM_HEAD, DIM), dtype=jnp.float32) * (HEADS * DIM_HEAD) ** (-0.5)
        return {'x': x, 'gamma': gamma, 'Wq': Wq, 'Wkv': Wkv, 'Wo': Wo}
    _L0_attn_b_in = _L0_attn_b_setup()

    def _L0_ffn_setup():
        import jax, jax.numpy as jnp
        import numpy as np
        H = 256
        IM = 128
        E = 16
        K = 8
        N_SHARED = 2
        IS = IM * N_SHARED
        B, L = (1, 256)
        SCALE = 2.5
        W_INIT = 0.02
        key = jax.random.key(seed)
        ks = jax.random.split(key, 9)
        return {'hidden_states': jax.random.normal(ks[0], (B, L, H), jnp.float32), 'gate_w': jax.random.normal(ks[1], (E, H), jnp.float32) * W_INIT, 'Wg': jax.random.normal(ks[2], (E, H, IM), jnp.float32) * W_INIT, 'Wu': jax.random.normal(ks[3], (E, H, IM), jnp.float32) * W_INIT, 'Wd': jax.random.normal(ks[4], (E, IM, H), jnp.float32) * W_INIT, 'sWg': jax.random.normal(ks[5], (H, IS), jnp.float32) * W_INIT, 'sWu': jax.random.normal(ks[6], (H, IS), jnp.float32) * W_INIT, 'sWd': jax.random.normal(ks[7], (IS, H), jnp.float32) * W_INIT}
    _L0_ffn_in = _L0_ffn_setup()

    def _L1_attn_a_setup():
        import jax, jax.numpy as jnp
        import numpy as np
        import math
        HIDDEN = 256
        NUM_HEADS = 16
        NUM_KV_HEADS = 4
        HEAD_DIM = 128
        GROUPS = NUM_HEADS // NUM_KV_HEADS
        BATCH = 1
        SEQ = 512
        THETA = 10000.0

        def _rope(x):
            seq = x.shape[2]
            freqs = 1.0 / THETA ** (jnp.arange(0, HEAD_DIM, 2, dtype=jnp.float32) / HEAD_DIM)
            angles = jnp.arange(seq, dtype=jnp.float32)[:, None] * freqs[None, :]
            cos = jnp.cos(angles)[None, None]
            sin = jnp.sin(angles)[None, None]
            x1 = x[..., 0::2]
            x2 = x[..., 1::2]
            rot = jnp.stack([x1 * cos - x2 * sin, x1 * sin + x2 * cos], axis=-1)
            return rot.reshape(x.shape)
        key = jax.random.key(seed)
        kx, kq, kk, kv, ko = jax.random.split(key, 5)
        scale = 0.02
        x = jax.random.normal(kx, (BATCH, SEQ, HIDDEN), dtype=jnp.float32)
        Wq = jax.random.normal(kq, (NUM_HEADS * HEAD_DIM, HIDDEN), dtype=jnp.float32) * scale
        Wk = jax.random.normal(kk, (NUM_KV_HEADS * HEAD_DIM, HIDDEN), dtype=jnp.float32) * scale
        Wv = jax.random.normal(kv, (NUM_KV_HEADS * HEAD_DIM, HIDDEN), dtype=jnp.float32) * scale
        Wo = jax.random.normal(ko, (HIDDEN, NUM_HEADS * HEAD_DIM), dtype=jnp.float32) * scale
        return {'x': x, 'Wq': Wq, 'Wk': Wk, 'Wv': Wv, 'Wo': Wo}
    _L1_attn_a_in = _L1_attn_a_setup()

    def _L1_attn_b_setup():
        import jax, jax.numpy as jnp
        import numpy as np
        HIDDEN = 256
        NUM_HEADS = 16
        HEAD_DIM = 128
        WINDOW = 128
        ROPE_THETA = 10000.0
        B, L = (1, 512)

        def _apply_rotary(x, cos, sin):
            d2 = x.shape[-1] // 2
            x1, x2 = (x[..., :d2], x[..., d2:])
            return jnp.concatenate([x1 * cos - x2 * sin, x2 * cos + x1 * sin], axis=-1)
        key = jax.random.key(seed)
        k0, k1, k2, k3, k4 = jax.random.split(key, 5)
        s = 1.0 / np.sqrt(HIDDEN)
        return {'hidden_states': jax.random.normal(k0, (B, L, HIDDEN), dtype=jnp.float32), 'wq': jax.random.normal(k1, (HIDDEN, NUM_HEADS * HEAD_DIM), dtype=jnp.float32) * s, 'wk': jax.random.normal(k2, (HIDDEN, NUM_HEADS * HEAD_DIM), dtype=jnp.float32) * s, 'wv': jax.random.normal(k3, (HIDDEN, NUM_HEADS * HEAD_DIM), dtype=jnp.float32) * s, 'wo': jax.random.normal(k4, (NUM_HEADS * HEAD_DIM, HIDDEN), dtype=jnp.float32) * s}
    _L1_attn_b_in = _L1_attn_b_setup()

    def _L1_ffn_setup():
        import jax, jax.numpy as jnp
        import numpy as np
        E, K, H, I = (64, 6, 256, 176)
        NS = 2
        IS = NS * I
        CAP = 32
        T_TOKENS = (1, 128)
        SCALE = 0.02

        def _moe_infer(x, gate_w, w_gate, w_up, w_down):
            T = x.shape[0]
            TK = T * K
            logits = x @ gate_w.T
            scores = jax.nn.softmax(logits, axis=-1)
            topk_w, topk_i = jax.lax.top_k(scores, K)
            flat_i = topk_i.reshape(-1)
            flat_w = topk_w.reshape(-1)
            token_ids = jnp.arange(TK, dtype=jnp.int32) // K
            order = jnp.argsort(flat_i)
            sorted_e = flat_i[order]
            counts = jnp.bincount(flat_i, length=E)
            starts = jnp.concatenate([jnp.zeros((1,), counts.dtype), jnp.cumsum(counts)[:-1]])
            pos_sorted = jnp.arange(TK) - starts[sorted_e]
            pos = jnp.zeros((TK,), jnp.int32).at[order].set(pos_sorted.astype(jnp.int32))
            valid = pos < CAP
            slot = jnp.where(valid, pos, CAP)
            buf = jnp.zeros((E, CAP + 1, H), x.dtype).at[flat_i, slot].set(x[token_ids])
            g = jnp.einsum('ech,ehi->eci', buf, w_gate)
            u = jnp.einsum('ech,ehi->eci', buf, w_up)
            y = jnp.einsum('eci,eih->ech', jax.nn.silu(g) * u, w_down)
            out_slots = y[flat_i, slot] * (flat_w * valid)[:, None]
            return out_slots.reshape(T, K, H).sum(axis=1)
        key = jax.random.key(seed)
        ks = jax.random.split(key, 8)
        f32 = jnp.float32
        return {'hidden_states': jax.random.normal(ks[0], (*T_TOKENS, H), f32), 'gate_w': jax.random.normal(ks[1], (E, H), f32) * SCALE, 'w_gate': jax.random.normal(ks[2], (E, H, I), f32) * SCALE, 'w_up': jax.random.normal(ks[3], (E, H, I), f32) * SCALE, 'w_down': jax.random.normal(ks[4], (E, I, H), f32) * SCALE, 'sw_gate': jax.random.normal(ks[5], (H, IS), f32) * SCALE, 'sw_up': jax.random.normal(ks[6], (H, IS), f32) * SCALE, 'sw_down': jax.random.normal(ks[7], (IS, H), f32) * SCALE}
    _L1_ffn_in = _L1_ffn_setup()
    _d = {'L0_attn_a_hidden_states': _L0_attn_a_in['hidden_states'], 'L0_attn_a_x_proj_w': _L0_attn_a_in['x_proj_w'], 'L0_attn_a_dt_proj_w': _L0_attn_a_in['dt_proj_w'], 'L0_attn_a_dt_proj_b': _L0_attn_a_in['dt_proj_b'], 'L0_attn_a_A_log': _L0_attn_a_in['A_log'], 'L0_attn_a_D': _L0_attn_a_in['D'], 'L0_attn_b_gamma': _L0_attn_b_in['gamma'], 'L0_attn_b_Wq': _L0_attn_b_in['Wq'], 'L0_attn_b_Wkv': _L0_attn_b_in['Wkv'], 'L0_attn_b_Wo': _L0_attn_b_in['Wo'], 'L0_ffn_gate_w': _L0_ffn_in['gate_w'], 'L0_ffn_Wg': _L0_ffn_in['Wg'], 'L0_ffn_Wu': _L0_ffn_in['Wu'], 'L0_ffn_Wd': _L0_ffn_in['Wd'], 'L0_ffn_sWg': _L0_ffn_in['sWg'], 'L0_ffn_sWu': _L0_ffn_in['sWu'], 'L0_ffn_sWd': _L0_ffn_in['sWd'], 'L1_attn_a_Wq': _L1_attn_a_in['Wq'], 'L1_attn_a_Wk': _L1_attn_a_in['Wk'], 'L1_attn_a_Wv': _L1_attn_a_in['Wv'], 'L1_attn_a_Wo': _L1_attn_a_in['Wo'], 'L1_attn_b_wq': _L1_attn_b_in['wq'], 'L1_attn_b_wk': _L1_attn_b_in['wk'], 'L1_attn_b_wv': _L1_attn_b_in['wv'], 'L1_attn_b_wo': _L1_attn_b_in['wo'], 'L1_ffn_gate_w': _L1_ffn_in['gate_w'], 'L1_ffn_w_gate': _L1_ffn_in['w_gate'], 'L1_ffn_w_up': _L1_ffn_in['w_up'], 'L1_ffn_w_down': _L1_ffn_in['w_down'], 'L1_ffn_sw_gate': _L1_ffn_in['sw_gate'], 'L1_ffn_sw_up': _L1_ffn_in['sw_up'], 'L1_ffn_sw_down': _L1_ffn_in['sw_down']}
    _x0 = _d['L0_attn_a_hidden_states']
    _d['L0_attn_a_hidden_states'] = jax.random.normal(jax.random.fold_in(jax.random.key(seed), 1), (2, 512, 256), dtype=_x0.dtype)
    del _x0
    return _d

def reference(L0_attn_a_hidden_states, L0_attn_a_x_proj_w, L0_attn_a_dt_proj_w, L0_attn_a_dt_proj_b, L0_attn_a_A_log, L0_attn_a_D, L0_attn_b_gamma, L0_attn_b_Wq, L0_attn_b_Wkv, L0_attn_b_Wo, L0_ffn_gate_w, L0_ffn_Wg, L0_ffn_Wu, L0_ffn_Wd, L0_ffn_sWg, L0_ffn_sWu, L0_ffn_sWd, L1_attn_a_Wq, L1_attn_a_Wk, L1_attn_a_Wv, L1_attn_a_Wo, L1_attn_b_wq, L1_attn_b_wk, L1_attn_b_wv, L1_attn_b_wo, L1_ffn_gate_w, L1_ffn_w_gate, L1_ffn_w_up, L1_ffn_w_down, L1_ffn_sw_gate, L1_ffn_sw_up, L1_ffn_sw_down):

    def _L0_attn_a_ref(hidden_states, x_proj_w, dt_proj_w, dt_proj_b, A_log, D):
        import jax, jax.numpy as jnp
        import numpy as np
        import math
        D_MODEL = 256
        D_STATE = 16
        DT_RANK = math.ceil(D_MODEL / 16)
        DT_MIN, DT_MAX, DT_INIT_FLOOR = (0.001, 0.1, 0.0001)

        def _selective_scan(u, delta, A, Bmat, Cmat, D):
            b, l, d = u.shape
            n = A.shape[1]

            def step(h, inp):
                u_t, delta_t, B_t, C_t = inp
                dA = jnp.exp(delta_t[:, :, None] * A)
                dBu = (delta_t * u_t)[:, :, None] * B_t[:, None, :]
                h = dA * h + dBu
                y_t = jnp.einsum('bdn,bn->bd', h, C_t)
                return (h, y_t)
            h0 = jnp.zeros((b, d, n), dtype=u.dtype)
            xs = (jnp.swapaxes(u, 0, 1), jnp.swapaxes(delta, 0, 1), jnp.swapaxes(Bmat, 0, 1), jnp.swapaxes(Cmat, 0, 1))
            _, ys = jax.lax.scan(step, h0, xs)
            y = jnp.swapaxes(ys, 0, 1)
            return y + u * D
        A = -jnp.exp(A_log)
        x_dbl = hidden_states @ x_proj_w.T
        dt_r = x_dbl[..., :DT_RANK]
        Bmat = x_dbl[..., DT_RANK:DT_RANK + D_STATE]
        Cmat = x_dbl[..., DT_RANK + D_STATE:]
        dt = dt_r @ dt_proj_w.T
        delta = jax.nn.softplus(dt + dt_proj_b)
        return _selective_scan(hidden_states, delta, A, Bmat, Cmat, D)

    def _L0_attn_b_ref(x, gamma, Wq, Wkv, Wo):
        import jax, jax.numpy as jnp
        import numpy as np
        DIM = 256
        DIM_HEAD = 128
        HEADS = 16
        EPS = 1e-05

        def _rotate_half(t):
            d2 = t.shape[-1] // 2
            x1, x2 = (t[..., :d2], t[..., d2:])
            return jnp.concatenate([-x2, x1], axis=-1)

        def _rotary_pos(n, dim_head, dtype):
            inv_freq = 1.0 / 10000.0 ** (jnp.arange(0, dim_head, 2, dtype=jnp.float32) / dim_head)
            freqs = jnp.arange(n, dtype=jnp.float32)[:, None] * inv_freq[None, :]
            return jnp.concatenate([freqs, freqs], axis=-1).astype(dtype)
        b, n, dim = x.shape
        h, dh = (HEADS, DIM_HEAD)
        scale = dh ** (-0.5)
        mu = jnp.mean(x, axis=-1, keepdims=True)
        var = jnp.var(x, axis=-1, keepdims=True)
        xn = (x - mu) * jax.lax.rsqrt(var + EPS) * gamma
        q = (xn @ Wq).reshape(b, n, h, dh).transpose(0, 2, 1, 3)
        kv = xn @ Wkv
        k, v = (kv[..., :dh], kv[..., dh:])
        pos = _rotary_pos(n, dh, x.dtype)
        cos, sin = (jnp.cos(pos), jnp.sin(pos))
        q = q * cos + _rotate_half(q) * sin
        k = k * cos + _rotate_half(k) * sin
        q = q * scale
        sim = jnp.einsum('bhid,bjd->bhij', q, k)
        causal = jnp.triu(jnp.ones((n, n), dtype=bool), k=1)
        neg = -jnp.finfo(sim.dtype).max
        sim = jnp.where(causal, neg, sim)
        sim = sim - jax.lax.stop_gradient(jnp.max(sim, axis=-1, keepdims=True))
        attn = jax.nn.softmax(sim, axis=-1)
        out = jnp.einsum('bhij,bjd->bhid', attn, v)
        out = out.transpose(0, 2, 1, 3).reshape(b, n, h * dh)
        return out @ Wo

    def _L0_ffn_ref(hidden_states, gate_w, Wg, Wu, Wd, sWg, sWu, sWd):
        import jax, jax.numpy as jnp
        import numpy as np
        H = 256
        IM = 128
        E = 16
        K = 8
        N_SHARED = 2
        IS = IM * N_SHARED
        B, L = (1, 256)
        SCALE = 2.5
        W_INIT = 0.02
        orig_shape = hidden_states.shape
        h = hidden_states.reshape(-1, H)
        T = h.shape[0]
        shared = jax.nn.silu(h @ sWg) * (h @ sWu) @ sWd
        router_logits = h @ gate_w.T
        routing_weights = jax.nn.sigmoid(router_logits)
        topk_w, topk_idx = jax.lax.top_k(routing_weights, K)
        topk_w = topk_w / (jnp.sum(topk_w, axis=-1, keepdims=True) + 1e-06)
        topk_w = topk_w * SCALE
        comb = jnp.zeros((T, E), h.dtype).at[jnp.arange(T)[:, None], topk_idx].add(topk_w)
        g = jnp.einsum('th,ehi->eti', h, Wg)
        u = jnp.einsum('th,ehi->eti', h, Wu)
        eo = jnp.einsum('eti,eih->eth', jax.nn.silu(g) * u, Wd)
        routed = jnp.einsum('eth,te->th', eo, comb)
        return (shared + routed).reshape(orig_shape)

    def _L1_attn_a_ref(x, Wq, Wk, Wv, Wo):
        import jax, jax.numpy as jnp
        import numpy as np
        import math
        HIDDEN = 256
        NUM_HEADS = 16
        NUM_KV_HEADS = 4
        HEAD_DIM = 128
        GROUPS = NUM_HEADS // NUM_KV_HEADS
        BATCH = 1
        SEQ = 512
        THETA = 10000.0

        def _rope(x):
            seq = x.shape[2]
            freqs = 1.0 / THETA ** (jnp.arange(0, HEAD_DIM, 2, dtype=jnp.float32) / HEAD_DIM)
            angles = jnp.arange(seq, dtype=jnp.float32)[:, None] * freqs[None, :]
            cos = jnp.cos(angles)[None, None]
            sin = jnp.sin(angles)[None, None]
            x1 = x[..., 0::2]
            x2 = x[..., 1::2]
            rot = jnp.stack([x1 * cos - x2 * sin, x1 * sin + x2 * cos], axis=-1)
            return rot.reshape(x.shape)
        B, S, _ = x.shape
        q = (x @ Wq.T).reshape(B, S, NUM_HEADS, HEAD_DIM).transpose(0, 2, 1, 3)
        k = (x @ Wk.T).reshape(B, S, NUM_KV_HEADS, HEAD_DIM).transpose(0, 2, 1, 3)
        v = (x @ Wv.T).reshape(B, S, NUM_KV_HEADS, HEAD_DIM).transpose(0, 2, 1, 3)
        q = _rope(q)
        k = _rope(k)
        k = jnp.repeat(k, GROUPS, axis=1)
        v = jnp.repeat(v, GROUPS, axis=1)
        scale = 1.0 / math.sqrt(HEAD_DIM)
        scores = jnp.einsum('bhqd,bhkd->bhqk', q, k) * scale
        causal = jnp.triu(jnp.ones((S, S), dtype=bool), k=1)
        scores = jnp.where(causal[None, None], jnp.float32(-jnp.inf), scores)
        attn = jax.nn.softmax(scores, axis=-1)
        out = jnp.einsum('bhqk,bhkd->bhqd', attn, v)
        out = out.transpose(0, 2, 1, 3).reshape(B, S, NUM_HEADS * HEAD_DIM)
        return out @ Wo.T

    def _L1_attn_b_ref(hidden_states, wq, wk, wv, wo):
        import jax, jax.numpy as jnp
        import numpy as np
        HIDDEN = 256
        NUM_HEADS = 16
        HEAD_DIM = 128
        WINDOW = 128
        ROPE_THETA = 10000.0
        B, L = (1, 512)

        def _apply_rotary(x, cos, sin):
            d2 = x.shape[-1] // 2
            x1, x2 = (x[..., :d2], x[..., d2:])
            return jnp.concatenate([x1 * cos - x2 * sin, x2 * cos + x1 * sin], axis=-1)
        Bsz, Ln, _ = hidden_states.shape
        dtype = hidden_states.dtype
        scale = HEAD_DIM ** (-0.5)

        def split_heads(x):
            return x.reshape(Bsz, Ln, NUM_HEADS, HEAD_DIM).transpose(0, 2, 1, 3)
        q = split_heads(hidden_states @ wq)
        k = split_heads(hidden_states @ wk)
        v = split_heads(hidden_states @ wv)
        inv_freq = 1.0 / ROPE_THETA ** (jnp.arange(0, HEAD_DIM, 2, dtype=jnp.float32) / HEAD_DIM)
        pos = jnp.arange(Ln, dtype=jnp.float32)
        freqs = pos[:, None] * inv_freq[None, :]
        cos = jnp.cos(freqs).astype(dtype)
        sin = jnp.sin(freqs).astype(dtype)
        q = _apply_rotary(q, cos, sin)
        k = _apply_rotary(k, cos, sin)
        q_pos = jnp.arange(Ln)[:, None]
        k_pos = jnp.arange(Ln)[None, :]
        valid = (k_pos > q_pos - WINDOW) & (k_pos <= q_pos)
        neg = jnp.finfo(dtype).min
        attn = jnp.einsum('bhqd,bhkd->bhqk', q, k) * scale
        attn = jnp.where(valid, attn, neg)
        attn = jax.nn.softmax(attn, axis=-1)
        out = jnp.einsum('bhqk,bhkd->bhqd', attn, v)
        out = out.transpose(0, 2, 1, 3).reshape(Bsz, Ln, NUM_HEADS * HEAD_DIM)
        return out @ wo

    def _L1_ffn_ref(hidden_states, gate_w, w_gate, w_up, w_down, sw_gate, sw_up, sw_down):
        import jax, jax.numpy as jnp
        import numpy as np
        E, K, H, I = (64, 6, 256, 176)
        NS = 2
        IS = NS * I
        CAP = 32
        T_TOKENS = (1, 128)
        SCALE = 0.02

        def _moe_infer(x, gate_w, w_gate, w_up, w_down):
            T = x.shape[0]
            TK = T * K
            logits = x @ gate_w.T
            scores = jax.nn.softmax(logits, axis=-1)
            topk_w, topk_i = jax.lax.top_k(scores, K)
            flat_i = topk_i.reshape(-1)
            flat_w = topk_w.reshape(-1)
            token_ids = jnp.arange(TK, dtype=jnp.int32) // K
            order = jnp.argsort(flat_i)
            sorted_e = flat_i[order]
            counts = jnp.bincount(flat_i, length=E)
            starts = jnp.concatenate([jnp.zeros((1,), counts.dtype), jnp.cumsum(counts)[:-1]])
            pos_sorted = jnp.arange(TK) - starts[sorted_e]
            pos = jnp.zeros((TK,), jnp.int32).at[order].set(pos_sorted.astype(jnp.int32))
            valid = pos < CAP
            slot = jnp.where(valid, pos, CAP)
            buf = jnp.zeros((E, CAP + 1, H), x.dtype).at[flat_i, slot].set(x[token_ids])
            g = jnp.einsum('ech,ehi->eci', buf, w_gate)
            u = jnp.einsum('ech,ehi->eci', buf, w_up)
            y = jnp.einsum('eci,eih->ech', jax.nn.silu(g) * u, w_down)
            out_slots = y[flat_i, slot] * (flat_w * valid)[:, None]
            return out_slots.reshape(T, K, H).sum(axis=1)
        orig_shape = hidden_states.shape
        x = hidden_states.reshape(-1, orig_shape[-1])
        y = _moe_infer(x, gate_w, w_gate, w_up, w_down).reshape(orig_shape)
        shared = jax.nn.silu(hidden_states @ sw_gate) * (hidden_states @ sw_up) @ sw_down
        return y + shared
    x = L0_attn_a_hidden_states
    x = x + _L0_attn_a_ref(_layernorm(x, axis=-1), L0_attn_a_x_proj_w, L0_attn_a_dt_proj_w, L0_attn_a_dt_proj_b, L0_attn_a_A_log, L0_attn_a_D)
    x = x + _L0_ffn_ref(_layernorm(x, axis=-1), L0_ffn_gate_w, L0_ffn_Wg, L0_ffn_Wu, L0_ffn_Wd, L0_ffn_sWg, L0_ffn_sWu, L0_ffn_sWd)
    x = x + _L0_attn_b_ref(_layernorm(x, axis=-1), L0_attn_b_gamma, L0_attn_b_Wq, L0_attn_b_Wkv, L0_attn_b_Wo)
    x = x + _L0_ffn_ref(_layernorm(x, axis=-1), L0_ffn_gate_w, L0_ffn_Wg, L0_ffn_Wu, L0_ffn_Wd, L0_ffn_sWg, L0_ffn_sWu, L0_ffn_sWd)
    x = x + _L1_attn_a_ref(_layernorm(x, axis=-1), L1_attn_a_Wq, L1_attn_a_Wk, L1_attn_a_Wv, L1_attn_a_Wo)
    x = x + _L1_ffn_ref(_layernorm(x, axis=-1), L1_ffn_gate_w, L1_ffn_w_gate, L1_ffn_w_up, L1_ffn_w_down, L1_ffn_sw_gate, L1_ffn_sw_up, L1_ffn_sw_down)
    x = x + _L1_attn_b_ref(_layernorm(x, axis=-1), L1_attn_b_wq, L1_attn_b_wk, L1_attn_b_wv, L1_attn_b_wo)
    x = x + _L1_ffn_ref(_layernorm(x, axis=-1), L1_ffn_gate_w, L1_ffn_w_gate, L1_ffn_w_up, L1_ffn_w_down, L1_ffn_sw_gate, L1_ffn_sw_up, L1_ffn_sw_down)
    return x

_drawn_inputs = setup_inputs


def setup_inputs(seed=0):
    import zlib

    import numpy as np

    out = dict(_drawn_inputs(seed))
    spreads = {'L0_attn_a_D': (1.0, 0.2), 'L0_attn_b_gamma': (1.0, 0.2)}
    factors = {'L0_ffn_gate_w': 7.507,
     'L0_ffn_Wg': 5.267,
     'L0_ffn_Wu': 5.208,
     'L0_ffn_Wd': 5.215,
     'L0_ffn_sWg': 3.284,
     'L0_ffn_sWu': 3.235,
     'L0_ffn_sWd': 3.242,
     'L1_attn_a_Wq': 8.0,
     'L1_attn_a_Wk': 8.0,
     'L1_ffn_gate_w': 8.0,
     'L1_ffn_w_gate': 8.0,
     'L1_ffn_w_up': 8.0,
     'L1_ffn_w_down': 8.0,
     'L1_ffn_sw_gate': 3.033,
     'L1_ffn_sw_up': 2.991,
     'L1_ffn_sw_down': 2.994}
    for name, (base, spread) in spreads.items():
        noise = np.random.default_rng([zlib.crc32(name.encode()), seed]).standard_normal(out[name].shape)
        drawn = base * np.exp(spread * noise) if base else spread * noise
        out[name] = jnp.asarray(drawn.astype(out[name].dtype))
    for name, factor in factors.items():
        out[name] = (out[name] * factor).astype(out[name].dtype)
    return out
```

```python
from contextlib import ExitStack

import concourse.bass as bass
from concourse import mybir

F32 = mybir.dt.float32
BF16 = mybir.dt.bfloat16
ALU = mybir.AluOpType
ACT = mybir.ActivationFunctionType
AX = mybir.AxisListType

P = 128
T, H = 1024, 256
SEQ = 512
NSEQ = T // SEQ
NT, NC = T // P, H // P
EPS = 1e-5

HEADS = 16
N_STATE, DT_RANK = 16, 16
XROWS = 3 * 2 * N_STATE + DT_RANK

NE0, TOP0, FF0 = 16, 8, 128
NU0 = NE0 + 2
ROUTED_SCALE = 2.5

NE1, TOP1, FF1 = 64, 6, 176
CAP = 32
HF1 = FF1 // 2
GE = P // CAP
NG1 = NE1 // GE
NSH = 2 * FF1 // HF1
NEG = -1e30


class Count:

    def __init__(self, nc, name, prime=0):
        self.sem = nc.alloc_semaphore(f"{name}_{nc.next_id()}")
        self.prime = prime


def sbuf(nc, name, shape, dtype):
    return nc.sbuf_tensor(f"{name}_{nc.next_id()}", shape, dtype)


def psum(nc, name, shape, dtype):
    return nc.psum_tensor(f"{name}_{nc.next_id()}", shape, dtype)


def wait(eng, count, n, i=0, per=0):
    if isinstance(i, int):
        n += i * per
        if n > 0:
            eng.wait_ge(count.sem, n + count.prime)
    else:
        assert n + count.prime > 0, (count.sem, n)
        eng.wait_ge(count.sem, i * per + (n + count.prime))


def finish(nc, counts):
    nc.clear_and_free_semaphores([c.sem for c in counts])
    nc.all_engine_barrier(sem_only=True)


def layer_norm(nc, g, gamma=None, again=False):
    rounds = 2 if again else 1
    stats, moved, rooted, normed, turned, kept_v, kept_a = counts = [
        Count(nc, n) for n in ("stats", "moments", "rooted", "normed", "turned", "kept_v", "kept_a")]
    with (
        sbuf(nc, "bn", [P, NT, 6], F32) as bn,
        sbuf(nc, "mv", [P, NT, 2], F32) as mv,
        sbuf(nc, "std", [P, NT], F32) as std,
        sbuf(nc, "rstd", [P, NT], F32) as rstd,
        psum(nc, "turn", [P, NC, T], F32) as turn,
        nc.Block() as block,
    ):
        @block.vector
        def _(dve):
            for r in range(rounds):
                src = g.xn if r else g.x
                if r:
                    dve.wait_ge(normed.sem, NT * r)
                for t in range(NT):
                    dve.bn_stats(bn[:, t, :], src[:, t, :]).then_inc(stats.sem, 1)
                for t in range(NT):
                    dve.wait_ge(stats.sem, NT * r + t + 1)
                    dve.bn_aggr(mv[:, t, :], bn[:, t, :]).then_inc(moved.sem, 1)
                dve.wait_ge(rooted.sem, r + 1)
                dve.reciprocal(rstd[:, :], std[:, :]).then_inc(moved.sem, 1)
                dve.wait_ge(moved.sem, (NT + 1) * (r + 1))
                for t in range(NT):
                    dve.tensor_scalar(g.xn[:, t, :], src[:, t, :], mv[:, t, 0:1], rstd[:, t:t + 1],
                                      ALU.subtract, ALU.mult).then_inc(normed.sem, 1)
            for c in range(NC):
                dve.wait_ge(turned.sem, c * NT + NT // 2)
                src = turn[:, c, 0:SEQ]
                if gamma is None:
                    dve.tensor_copy(g.xt[:, c, 0:SEQ], src)
                else:
                    dve.tensor_scalar(g.xt[:, c, 0:SEQ], src, gamma[:, c:c + 1], None, ALU.mult)

        @block.scalar
        def _(act):
            for r in range(rounds):
                act.wait_ge(moved.sem, (NT + 1) * r + NT)
                act.activation(std[:, :], mv[:, :, 1], ACT.Sqrt, bias=g.eps[:, 0:1]).then_inc(rooted.sem, 1)
            for c in range(NC):
                act.wait_ge(turned.sem, (c + 1) * NT)
                src = turn[:, c, SEQ:T]
                if gamma is None:
                    act.activation(g.xt[:, c, SEQ:T], src, ACT.Copy)
                else:
                    act.activation(g.xt[:, c, SEQ:T], src, ACT.Copy, scale=gamma[:, c:c + 1])

        @block.tensor
        def _(pe):
            for c in range(NC):
                for t in range(NT):
                    pe.wait_ge(normed.sem, NT * (rounds - 1) + t + 1)
                    pe.transpose(turn[:, c, t * P:(t + 1) * P], g.xn[:, t, c * P:(c + 1) * P],
                                 g.ident[:, :]).then_inc(turned.sem, 1)
    finish(nc, counts)


def selective_scan(nc, g, d):
    c = {n: Count(nc, n, p) for n, p in (
        ("loaded", 0), ("projected", 0), ("rows", 0), ("split", 0), ("dt", 0), ("soft_a", 0), ("soft_v", 0),
        ("ready", 0), ("spread", 0), ("copied", 2), ("decay", 0), ("driven", 0), ("state", 4),
        ("read", 4), ("summed", 4), ("gated", 0), ("turned", 0), ("zeroed", 0), ("selected", 0), ("added", 0))}
    HALF = 2 * N_STATE
    with (
        sbuf(nc, "xw", [P, NC, XROWS], F32) as xw,
        sbuf(nc, "dtw", [XROWS, H], F32) as dtw,
        sbuf(nc, "vecs", [P, 2 * NC + NC * N_STATE], F32) as vecs,
        sbuf(nc, "pick1", [3 * HALF, HALF], F32) as pick1,
        sbuf(nc, "pick", [3 * HALF, HALF, P], BF16) as pick,
        sbuf(nc, "rows", [XROWS, T], F32) as rows,
        sbuf(nc, "rest", [3 * HALF, T], F32) as rest,
        sbuf(nc, "part", [3 * HALF, T], BF16) as part,
        sbuf(nc, "stack", [3 * HALF, T], BF16) as stack,
        sbuf(nc, "nega", [P, NC, N_STATE], F32) as nega,
        sbuf(nc, "delta", [P, NC, T], F32) as delta,
        sbuf(nc, "du", [P, NC, T], F32) as du,
        sbuf(nc, "decay", [P, 2, NC, T], F32) as decay,
        sbuf(nc, "drive", [P, 2, NC, T], F32) as drive,
        sbuf(nc, "state", [P, 2, NC, T], F32) as state,
        sbuf(nc, "bs", [P, 2, T], F32) as bs,
        sbuf(nc, "cs", [P, 2, T], F32) as cs,
        psum(nc, "acc", [P, NC, T], F32) as acc,
        psum(nc, "wide", [P, 2, T], F32) as wide,
        nc.Block() as block,
    ):
        bias, dvec, alog = vecs[:, 0:NC], vecs[:, NC:2 * NC], vecs[:, 2 * NC:].rearrange("p (c n) -> p c n", c=NC)
        z, e, lg = decay[:, 0], decay[:, 1], drive[:, 0]
        r1, c1 = drive[:, 1], state[:, 0]
        term = drive

        @block.sync
        def _(sp):
            sp.dma_start(xw[:, :, :], d["xw"]).then_inc(c["loaded"].sem, 16)
            sp.dma_start(dtw[:, :], d["dtw"]).then_inc(c["loaded"].sem, 16)
            sp.dma_start(vecs[:, :], d["vecs"]).then_inc(c["loaded"].sem, 16)
            sp.dma_start(pick1[:, :], d["pick"]).then_inc(c["loaded"].sem, 16)

        @block.gpsimd
        def _(pool):
            pool.wait_ge(c["loaded"].sem, 64)
            pool.tensor_copy(pick[:, :, :], pick1[:, :].unsqueeze(2).broadcast_to([3 * HALF, HALF, P])) \
                .then_inc(c["selected"].sem, 1)
            pool.sem_inc(c["read"].sem, c["read"].prime)
            with pool.Fori(0, N_STATE // 2) as i:
                for k in range(2):
                    for dc in range(NC):
                        wait(pool, c["state"], 2 * k + dc + 1, i, 4)
                        wait(pool, c["copied"], 2 * (k + 1), i, 4)
                        pool.tensor_tensor(term[:, k, dc, :], state[:, k, dc, :], cs[:, k, :], ALU.mult) \
                            .then_inc(c["read"].sem, 1)

        @block.tensor
        def _(pe):
            pe.wait_ge(c["loaded"].sem, 64)
            for s in range(NSEQ):
                for kc in range(NC):
                    last = pe.matmul(acc[0:XROWS, 0, s * SEQ:(s + 1) * SEQ], xw[:, kc, :],
                                     g.xt[:, kc, s * SEQ:(s + 1) * SEQ], start=(kc == 0), stop=(kc == NC - 1))
                last.then_inc(c["projected"].sem, 1)
            pe.wait_ge(c["rows"].sem, 2)
            for dc in range(NC):
                for s in range(NSEQ):
                    pe.matmul(wide[:, dc, s * SEQ:(s + 1) * SEQ], dtw[:, dc * P:(dc + 1) * P],
                              rows[:, s * SEQ:(s + 1) * SEQ], start=True, stop=True).then_inc(c["dt"].sem, 1)
            for dc in range(NC):
                for s in range(NSEQ):
                    pe.matmul(acc[:, dc, s * SEQ:(s + 1) * SEQ], g.zeros[:, 0:P], g.zeros[:, :],
                              start=True, stop=True)
            pe.sem_inc(c["summed"].sem, c["summed"].prime)
            pe.wait_ge(c["split"].sem, 1)
            pe.wait_ge(c["selected"].sem, 1)

            def spread(i, k):
                for which in range(2):
                    wait(pe, c["copied"], 2 * k - 1 + which, i, 4)
                    for s in range(NSEQ):
                        lhs = pick[:, bass.ds(2 * i + (k + which * N_STATE), 1), :].rearrange("p o m -> p (o m)")
                        last = pe.matmul(wide[:, which, s * SEQ:(s + 1) * SEQ], lhs,
                                         stack[:, s * SEQ:(s + 1) * SEQ], start=True, stop=True)
                    last.then_inc(c["spread"].sem, 1)

            with pe.Fori(0, N_STATE // 2) as i:
                for k in range(2):
                    if k == 0:
                        pe.wait_ge(c["soft_a"].sem, 1)
                    spread(i, k)
                    for dc in range(NC):
                        wait(pe, c["read"], 2 * k + dc + 1, i, 4)
                        for s in range(NSEQ):
                            last = pe.matmul(acc[:, dc, s * SEQ:(s + 1) * SEQ], g.ident[:, :],
                                             term[:, k, dc, s * SEQ:(s + 1) * SEQ], start=False, stop=True,
                                             skip_group_check=True)
                        last.then_inc(c["summed"].sem, 1)
            for t in range(NT):
                for dc in range(NC):
                    if dc == 0:
                        pe.wait_ge(c["gated"].sem, NSEQ * NC)
                    last = pe.transpose(wide[:, t // 4, (t % 4) * H + dc * P:(t % 4) * H + (dc + 1) * P],
                                        state[:, 0, dc, t * P:(t + 1) * P], g.ident[:, :])
                last.then_inc(c["turned"].sem, 1)

        @block.scalar
        def _(act):
            for s in range(NSEQ):
                act.wait_ge(c["projected"].sem, s + 1)
                act.activation(rows[:, s * SEQ:(s + 1) * SEQ], acc[0:XROWS, 0, s * SEQ:(s + 1) * SEQ],
                               ACT.Copy).then_inc(c["rows"].sem, 1)
            act.wait_ge(c["loaded"].sem, 64)
            for dc in range(NC):
                act.wait_ge(c["dt"].sem, 2 * dc + 2)
                last = act.activation(z[:, dc, :], wide[:, dc, :], ACT.Identity, bias=bias[:, dc:dc + 1])
            last.then_inc(c["soft_a"].sem, 1)
            act.wait_ge(c["soft_a"].sem, 1)
            act.activation(c1[:, :, :], z[:, :, :], ACT.Abs).then_inc(c["soft_a"].sem, 1)
            act.activation(nega[:, :, :], alog, ACT.Exp).then_inc(c["soft_a"].sem, 1)
            act.wait_ge(c["soft_a"].sem, 3)
            act.activation(e[:, :, :], c1[:, :, :], ACT.Exp, scale=-1.0).then_inc(c["soft_a"].sem, 1)
            act.wait_ge(c["soft_a"].sem, 4)
            act.activation(lg[:, :, :], e[:, :, :], ACT.Ln, bias=g.one[:, 0:1]).then_inc(c["soft_a"].sem, 1)
            act.wait_ge(c["ready"].sem, 1)
            act.sem_inc(c["copied"].sem, c["copied"].prime)
            with act.Fori(0, N_STATE // 2) as i:
                for k in range(2):
                    for dc in range(NC):
                        wait(act, c["state"], 2 * k + dc - 3, i, 4)
                        act.activation(decay[:, k, dc, :], delta[:, dc, :], ACT.Exp,
                                       scale=nega[:, dc, bass.ds(2 * i + k, 1)]).then_inc(c["decay"].sem, 1)
                    for which, to in enumerate((bs, cs)):
                        wait(act, c["spread"], 2 * k + which + 1, i, 4)
                        if which == 0:
                            wait(act, c["state"], 2 * k - 2, i, 4)
                        else:
                            wait(act, c["read"], 2 * k - 2, i, 4)
                        act.activation(to[:, k, :], wide[:, which, :], ACT.Copy).then_inc(c["copied"].sem, 1)

        @block.vector
        def _(dve):
            n = [0]

            def link(op):
                n[0] += 1
                op.then_inc(c["soft_v"].sem, 1)
                dve.wait_ge(c["soft_v"].sem, n[0])

            A3 = 3 * HALF
            dve.wait_ge(c["rows"].sem, 2)
            link(dve.tensor_copy(part[:, :], rows[0:A3, :]))
            dve.tensor_copy(stack[0:HALF, :], part[0:HALF, :])
            link(dve.tensor_tensor(rest[:, :], rows[0:A3, :], part[:, :], ALU.subtract))
            link(dve.tensor_copy(part[:, :], rest[:, :]))
            dve.tensor_copy(stack[HALF:2 * HALF, :], part[HALF:2 * HALF, :])
            link(dve.tensor_tensor(rest[:, :], rest[:, :], part[:, :], ALU.subtract))
            dve.tensor_copy(stack[2 * HALF:A3, :], rest[2 * HALF:A3, :]).then_inc(c["split"].sem, 1)
            dve.wait_ge(c["soft_a"].sem, 5)
            link(dve.tensor_scalar(nega[:, :, :], nega[:, :, :], -1.0, None, ALU.mult))
            link(dve.tensor_scalar(r1[:, :, :], e[:, :, :], 1.0, None, ALU.add))
            link(dve.tensor_scalar(c1[:, :, :], r1[:, :, :], 1.0, None, ALU.subtract))
            link(dve.tensor_tensor(c1[:, :, :], e[:, :, :], c1[:, :, :], ALU.subtract))
            link(dve.reciprocal(r1[:, :, :], r1[:, :, :]))
            link(dve.tensor_tensor(c1[:, :, :], c1[:, :, :], r1[:, :, :], ALU.mult))
            link(dve.tensor_tensor(c1[:, :, :], c1[:, :, :], lg[:, :, :], ALU.add))
            link(dve.scalar_tensor_tensor(delta[:, :, :].rearrange("p c t -> p (c t)"), z[:, :, :].rearrange("p c t -> p (c t)"),
                                          0.0, c1[:, :, :].rearrange("p c t -> p (c t)"), ALU.max, ALU.add))
            dve.tensor_tensor(du[:, :, :], delta[:, :, :], g.xt[:, :, :], ALU.mult).then_inc(c["ready"].sem, 1)
            dve.wait_ge(c["ready"].sem, 1)
            dve.sem_inc(c["state"].sem, c["state"].prime)
            with dve.Fori(0, N_STATE // 2) as i:
                for k in range(2):
                    wait(dve, c["decay"], 2 * (k + 1), i, 4)
                    dve.memset(decay[:, k, :, 0:T:SEQ], 0.0).then_inc(c["zeroed"].sem, 1)
                    wait(dve, c["copied"], 2 * k + 1, i, 4)
                    for dc in range(NC):
                        wait(dve, c["summed"], 2 * k + dc - 3, i, 4)
                        dve.tensor_tensor(drive[:, k, dc, :], du[:, dc, :], bs[:, k, :], ALU.mult) \
                            .then_inc(c["driven"].sem, 1)
                    wait(dve, c["zeroed"], k + 1, i, 2)
                    for dc in range(NC):
                        wait(dve, c["driven"], 2 * k + dc + 1, i, 4)
                        wait(dve, c["read"], 2 * k + dc - 3, i, 4)
                        dve.tensor_tensor_scan(state[:, k, dc, :], decay[:, k, dc, :], drive[:, k, dc, :], 0.0,
                                               ALU.mult, ALU.add).then_inc(c["state"].sem, 1)
            for dc in range(NC):
                wait(dve, c["summed"], 2 * N_STATE - NC + dc + 1)
                wait(dve, c["read"], 2 * N_STATE)
                for s in range(NSEQ):
                    cut = slice(s * SEQ, (s + 1) * SEQ)
                    dve.scalar_tensor_tensor(state[:, 0, dc, cut], g.xt[:, dc, cut], dvec[:, dc:dc + 1],
                                             acc[:, dc, cut], ALU.mult, ALU.add).then_inc(c["gated"].sem, 1)
            for t in range(0, NT, 2):
                dve.wait_ge(c["turned"].sem, t + 2)
                x2 = g.x[:, t:t + 2, :].rearrange("p a h -> p (a h)")
                dve.tensor_tensor(x2, x2, wide[:, t // 4, (t % 4) * H:(t % 4 + 2) * H], ALU.add)
    finish(nc, c.values())


def mixture(nc, g, d):
    c = {n: Count(nc, n, p) for n, p in (
        ("loaded", 0), ("w_even", 0), ("w_odd", 0), ("logits", 0), ("gates", 0), ("own", 0), ("weighed", 0),
        ("inner", 0), ("silu", 0), ("prod", 4), ("down", 4), ("added", 4))}
    full = (c["w_even"], c["w_odd"])
    LAST = NU0 // 2 - 1
    with (
        sbuf(nc, "router", [P, NC, NE0], F32) as router,
        sbuf(nc, "w", [P, 2, 2 * 2 * FF0 + H], F32) as w,
        sbuf(nc, "score", [P, NT, NE0], F32) as score,
        sbuf(nc, "left", [P, NT, NE0], F32) as left,
        sbuf(nc, "top", [P, NT, 8], F32) as top,
        sbuf(nc, "total", [P, NT], F32) as total,
        sbuf(nc, "weight", [P, NT, NU0], F32) as weight,
        sbuf(nc, "silu", [P, NSEQ, SEQ], F32) as silu,
        sbuf(nc, "inner", [P, 2, T], F32) as inner,
        psum(nc, "gate", [P, NSEQ, SEQ], F32) as gate,
        psum(nc, "up", [P, NSEQ, SEQ], F32) as up,
        psum(nc, "outs", [P, NT, H], F32) as outs,
        nc.Block() as block,
    ):
        def part(k, which, kc):
            return w[:, k, (which * NC + kc) * FF0:(which * NC + kc + 1) * FF0]

        @block.sync
        def _(sp):
            sp.dma_start(router[:, :, :], d["router0"]).then_inc(c["loaded"].sem, 16)
            with sp.Fori(0, NU0 // 2) as i:
                for k in range(2):
                    wait(sp, c["down"], 4 * 0 + 2 * k - 2, i, 4)
                    sp.dma_start(w[:, k, :], d["w0"][bass.ds(2 * i + k, 1)].rearrange("o p n -> p (o n)")) \
                        .then_inc(full[k].sem, 16)

        @block.tensor
        def _(pe):
            pe.sem_inc(c["down"].sem, c["down"].prime)
            pe.wait_ge(c["loaded"].sem, 16)
            for t in range(NT):
                for kc in range(NC):
                    last = pe.matmul(outs[:, 0, t * NE0:(t + 1) * NE0], g.xt[:, kc, t * P:(t + 1) * P],
                                     router[:, kc, :], start=(kc == 0), stop=(kc == NC - 1))
            last.then_inc(c["logits"].sem, 1)

            def gate_up(i, n):
                k = n % 2
                wait(pe, full[k], 16 * (n // 2) + 16, i, 16)
                for s in range(NSEQ):
                    wait(pe, c["prod"], 2 * n - 1 + s, i, 4)
                    for which, to in enumerate((gate, up)):
                        for kc in range(NC):
                            last = pe.matmul(to[:, s, :], part(k, which, kc), g.xt[:, kc, s * SEQ:(s + 1) * SEQ],
                                             start=(kc == 0), stop=(kc == NC - 1))
                    last.then_inc(c["inner"].sem, 1)

            def down(i, n):
                k = n % 2
                for t in range(NT):
                    if t % 4 == 0:
                        wait(pe, c["prod"], 2 * n + t // 4 + 1, i, 4)
                    if t % 2 == 0:
                        wait(pe, c["added"], 4 * n - 3 + t // 2, i, 8)
                    last = pe.matmul(outs[:, t, :], inner[:, k, t * P:(t + 1) * P], w[:, k, 4 * FF0:],
                                     start=True, stop=True)
                    if t % 4 == 3:
                        last.then_inc(c["down"].sem, 1)

            gate_up(0, 0)
            pe.wait_ge(c["gates"].sem, 1)
            with pe.Fori(0, LAST) as i:
                for n in range(2):
                    gate_up(i, n + 1)
                    down(i, n)
            gate_up(LAST, 1)
            down(LAST, 0)
            down(LAST, 1)

        @block.scalar
        def _(act):
            act.wait_ge(c["logits"].sem, 1)
            act.activation(score[:, :, :].rearrange("p t e -> p (t e)"), outs[:, 0, 0:NT * NE0],
                           ACT.Sigmoid).then_inc(c["gates"].sem, 1)
            with act.Fori(0, NU0 // 2) as i:
                for n in range(2):
                    for s in range(NSEQ):
                        wait(act, c["inner"], 2 * n + s + 1, i, 4)
                        wait(act, c["prod"], 2 * n - 1 + s, i, 4)
                        act.activation(silu[:, s, :], gate[:, s, :], ACT.Silu).then_inc(c["silu"].sem, 1)

        @block.vector
        def _(dve):
            dve.sem_inc(c["prod"].sem, c["prod"].prime)
            dve.sem_inc(c["added"].sem, c["added"].prime)

            def product(i, n):
                for s in range(NSEQ):
                    wait(dve, c["silu"], 2 * n + s + 1, i, 4)
                    wait(dve, c["down"], 2 * n - 3 + s, i, 4)
                    dve.tensor_tensor(inner[:, n % 2, s * SEQ:(s + 1) * SEQ], silu[:, s, :], up[:, s, :], ALU.mult) \
                        .then_inc(c["prod"].sem, 1)

            def add(i, n):
                for t in range(NT):
                    if t % 4 == 0:
                        wait(dve, c["down"], 2 * n + t // 4 + 1, i, 4)
                    if t % 2 == 0:
                        wait(dve, c["added"], 4 * n - 3 + t // 2, i, 8)
                    e = bass.ds(2 * i + n, 1)
                    last = dve.scalar_tensor_tensor(g.x[:, t, :], outs[:, t, :], weight[:, t, e],
                                                    g.x[:, t, :], ALU.mult, ALU.add)
                    if t % 2 == 1:
                        last.then_inc(c["added"].sem, 1)

            own = [0]

            def link(op):
                own[0] += 1
                op.then_inc(c["own"].sem, 1)
                dve.wait_ge(c["own"].sem, own[0])

            dve.memset(weight[:, :, NE0:], 1.0)
            dve.wait_ge(c["gates"].sem, 1)
            for t in range(NT):
                op = dve.max(top[:, t, :], score[:, t, :])
                if t == NT - 1:
                    link(op)
            for t in range(NT):
                op = dve.match_replace(left[:, t, :], top[:, t, :], score[:, t, :], -1.0)
                if t == NT - 1:
                    link(op)
            link(dve.scalar_tensor_tensor(left[:, :, :], left[:, :, :], 0.0, score[:, :, :], ALU.is_lt, ALU.mult))
            link(dve.reduce_sum(total[:, :], left[:, :, :], axis=AX.X))
            link(dve.tensor_scalar(total[:, :], total[:, :], 1e-6, None, ALU.add))
            link(dve.reciprocal(total[:, :], total[:, :]))
            link(dve.tensor_scalar(total[:, :], total[:, :], ROUTED_SCALE, None, ALU.mult))
            link(dve.tensor_tensor(weight[:, :, 0:NE0], left[:, :, :],
                                   total[:, :].unsqueeze(2).broadcast_to([P, NT, NE0]), ALU.mult))
            product(0, 0)
            with dve.Fori(0, LAST) as i:
                for n in range(2):
                    product(i, n + 1)
                    add(i, n)
            product(LAST, 1)
            add(LAST, 0)
            add(LAST, 1)
    finish(nc, c.values())


def attention(nc, g, d, name, kv_every, window):
    UNITS = HEADS * NSEQ
    U = 4 if kv_every == 4 else 2
    BODY = U * NSEQ
    LOOPS = HEADS // U - 1
    KVSLOTS = 2 if kv_every == 1 else 1
    NQ = SEQ // P
    groups = [[0, 1], [2, 3]] if window else [[0, 1], [2], [3]]
    NG = len(groups)
    keys = [list(range(max(0, t - 1) if window else 0, t + 1)) for t in range(NQ)]
    cols, psum_col, width = [], [], []
    for gr in groups:
        at = 0
        for t in gr:
            cols.append(sum(len(keys[s]) for s in range(t)) * P)
            psum_col.append(at)
            at += len(keys[t]) * P
        width.append(at)
    WIDTH = sum(width)

    def has_kv(m):
        return (m // NSEQ) % kv_every == 0

    def before(m, kind):
        if m < 0 and kv_every < HEADS:
            return before(m + BODY, kind) - before(BODY, kind)
        if m < 0:
            return m + NSEQ if kind == "rope" else NSEQ
        kv = sum(has_kv(j) for j in range(m))
        return kv if kind == "v" else m + kv

    per_rope = BODY if kv_every == HEADS else before(BODY, "rope")
    per_v = 0 if kv_every == HEADS else before(BODY, "v")

    c = {n: Count(nc, n, p) for n, p in (
        ("loaded", 0), ("wo", 0), ("wq_even", 0), ("wq_odd", 0), ("kv_even", 0), ("kv_odd", 0), ("ready", 0), ("turns", 0),
        ("proj", 8), ("swapped", 4), ("cosed", 6), ("sined", 4), ("rotated", 6),
        ("vproj", 4), ("vkept", 4), ("scores", 8), ("peak", 0), ("expd", 8), ("recip", 0), ("normed", 0),
        ("turned", 8), ("pt_v", 8), ("pt_a", 8), ("values", 6), ("okept", 4), ("out", 0))}
    wq_full, kv_full = (c["wq_even"], c["wq_odd"]), (c["kv_even"], c["kv_odd"])
    VBANK = window

    with (
        sbuf(nc, "wo", [P, HEADS, H], F32) as wo,
        sbuf(nc, "wq", [P, 2, NC, P], F32) as wq,
        sbuf(nc, "wkv", [P, KVSLOTS, 2, NC, P], F32) as wkv,
        sbuf(nc, "ropes", [P, 2, 2, SEQ], F32) as ropes,
        sbuf(nc, "mask1", [P, 2, P], F32) as mask1,
        sbuf(nc, "mask", [P, 2, P], BF16) as mask,
        sbuf(nc, "q", [P, NSEQ, SEQ], F32) as q,
        sbuf(nc, "k", [P, NSEQ, SEQ], F32) as k,
        sbuf(nc, "v", [P, NSEQ, NQ, P], F32) as v,
        sbuf(nc, "swap", [P, 2, SEQ], F32) as swap,
        sbuf(nc, "cosed", [P, 2, SEQ], F32) as cosed,
        sbuf(nc, "prob", [P, NSEQ, WIDTH], F32) as prob,
        sbuf(nc, "pt", [P, NSEQ, NQ, SEQ], F32) as pt,
        sbuf(nc, "peak", [P, NSEQ, NQ], F32) as peak,
        sbuf(nc, "sums", [P, NSEQ, NQ], F32) as sums,
        sbuf(nc, "recip", [P, NSEQ, NQ], F32) as recip,
        sbuf(nc, "o", [P, HEADS, T], F32) as o,
        psum(nc, "banks", [P, 8, SEQ], F32) as banks,
        nc.Block() as block,
    ):
        s_bank = [banks[:, j, :] for j in range(NG)]
        t_bank = [banks[:, 3 + j, :] for j in range(2)]
        p_bank = [banks[:, 5 + j, :] for j in range(2)]
        o_bank = banks[:, 7, :]
        v_bank = banks[:, 2, :] if VBANK else o_bank
        mover = ["v", "a"] if window else ["v", "v", "a"]

        def turned_by(n, gi):
            own = [j for j in range(NG) if mover[j] == mover[gi]]
            return c["pt_" + mover[gi]], n * len(own) + own.index(gi) + 1, BODY * len(own)

        @block.sync
        def _(sp):
            sp.dma_start(ropes[:, 0], d["rope_q"]).then_inc(c["loaded"].sem, 16)
            sp.dma_start(ropes[:, 1], d["rope_k"]).then_inc(c["loaded"].sem, 16)
            sp.dma_start(mask1[:, :, :], d["mask"].rearrange("p (a n) -> p a n", a=2)).then_inc(c["loaded"].sem, 16)

            def load(i, h):
                at = bass.ds(i * U + h, 1) if not isinstance(i, int) else slice(i * U + h, i * U + h + 1)
                wait(sp, c["proj"], before(NSEQ * h - 3, "rope") + 1, i, per_rope)
                sp.dma_start(wq[:, h % 2], d[name + "_q"][at].rearrange("o p c n -> p (o c) n")) \
                    .then_inc(wq_full[h % 2].sem, 16)
                if has_kv(NSEQ * h) and kv_every < HEADS:
                    kvh = h // kv_every
                    at = bass.ds(i * (U // kv_every) + kvh, 1)
                    wait(sp, c["vproj"], NSEQ * (kvh + 1 - KVSLOTS), i, per_v)
                    sp.dma_start(wkv[:, kvh % KVSLOTS].rearrange("p a c n -> p (a c) n"),
                                 d[name + "_kv"][at].rearrange("o p a c n -> p (o a c) n")) \
                        .then_inc(kv_full[kvh % KVSLOTS].sem, 16)

            if kv_every == HEADS:
                sp.dma_start(wkv[:, 0].rearrange("p a c n -> p (a c) n"),
                             d[name + "_kv"][0:1].rearrange("o p a c n -> p (o a c) n")).then_inc(kv_full[0].sem, 16)
            with sp.Fori(0, HEADS // U) as i:
                for h in range(U):
                    load(i, h)
            sp.dma_start(wo[:, :, :], d[name + "_o"]).then_inc(c["wo"].sem, 16)

        @block.tensor
        def _(pe):
            for n in ("proj", "vproj", "scores", "turned", "values"):
                pe.sem_inc(c[n].sem, c[n].prime)
            pe.wait_ge(c["ready"].sem, 1)

            def rope_unit(i, m, which):
                s = m % NSEQ
                r = before(m, "rope") + which
                wait(pe, c["cosed"], r - 1, i, per_rope)
                if which == 0:
                    h = m // NSEQ
                    wait(pe, wq_full[h % 2], 16 * (h // 2) + 16, i, 16 * U // 2)
                    w = wq[:, h % 2]
                else:
                    kvh = m // NSEQ // kv_every
                    wait(pe, kv_full[kvh % KVSLOTS], 16 * (kvh // KVSLOTS) + 16, i, 16 * (U // kv_every) // KVSLOTS)
                    w = wkv[:, kvh % KVSLOTS, 0]
                for kc in range(NC):
                    last = pe.matmul(p_bank[r % 2], w[:, kc, :], g.xt[:, kc, s * SEQ:(s + 1) * SEQ],
                                     start=(kc == 0), stop=(kc == NC - 1))
                last.then_inc(c["proj"].sem, 1)

            def value_unit(i, m):
                s = m % NSEQ
                kvh = m // NSEQ // kv_every
                wait(pe, kv_full[kvh % KVSLOTS], 16 * (kvh // KVSLOTS) + 16, i, 16 * (U // kv_every) // KVSLOTS)
                wait(pe, c["vkept"], before(m, "v"), i, per_v)
                if not VBANK:
                    wait(pe, c["okept"], m - 1, i, BODY)
                for t in range(NQ):
                    for kc in range(NC):
                        last = pe.matmul(v_bank[:, t * P:(t + 1) * P],
                                         g.xt[:, kc, s * SEQ + t * P:s * SEQ + (t + 1) * P],
                                         wkv[:, kvh % KVSLOTS, 1, kc, :], start=(kc == 0), stop=(kc == NC - 1))
                last.then_inc(c["vproj"].sem, 1)

            def score(i, m, gi):
                s = m % NSEQ
                if gi == 0:
                    r = before(m + 1, "rope") if m >= 0 else 0
                    wait(pe, c["rotated"], r, i, per_rope)
                wait(pe, c["expd"], NG * (m - 1) + gi + 1, i, NG * BODY)
                for t in groups[gi]:
                    out = s_bank[gi][:, psum_col[t]:psum_col[t] + len(keys[t]) * P]
                    pe.matmul(out, q[:, s, t * P:(t + 1) * P],
                              k[:, s, keys[t][0] * P:(keys[t][-1] + 1) * P], start=True, stop=False)
                    lo = 0 if window and len(keys[t]) == 2 else 1
                    last = pe.matmul(out[:, (len(keys[t]) - 2 + lo) * P:], g.identb[:, :],
                                     mask[:, lo:, :].rearrange("p a n -> p (a n)"), start=False, stop=True)
                last.then_inc(c["scores"].sem, 1)

            def turn(i, n, gi):
                s = n % NSEQ
                wait(pe, c["normed"], NG * n + gi + 1, i, NG * BODY)
                j = NG * n + gi - 2
                cnt, at, per = turned_by(j // NG, j % NG)
                wait(pe, cnt, at, i, per)
                at = 0
                for t in groups[gi]:
                    for x in range(len(keys[t])):
                        last = pe.transpose(t_bank[(NG * n + gi) % 2][:, at:at + P],
                                            prob[:, s, cols[t] + x * P:cols[t] + (x + 1) * P], g.ident[:, :])
                        at += P
                last.then_inc(c["turned"].sem, 1)

            def sum_values(i, n):
                s = n % NSEQ
                for e in ("v", "a"):
                    own = [j for j in range(NG) if mover[j] == e]
                    wait(pe, c["pt_" + e], (n + 1) * len(own), i, BODY * len(own))
                wait(pe, c["okept"], n, i, BODY)
                wait(pe, c["vkept"], before(n + 1, "v"), i, per_v)
                if not VBANK:
                    m = min(n + 2, UNITS - i * BODY) if isinstance(i, int) else n + 2
                    wait(pe, c["vkept"], before(m, "v"), i, per_v)
                order = [0, 2, 1, 3] if window else list(range(NQ))
                for j, x in enumerate(order):
                    to = min(x + 2, NQ) * P if window else SEQ
                    last = pe.matmul(o_bank[:, x * P:to], v[:, s, x, :], pt[:, s, x, x * P:to],
                                     start=(j == 0), stop=(j == NQ - 1))
                last.then_inc(c["values"].sem, 1)

            def slot(i, n):
                static = isinstance(i, int)
                live = lambda m: not static or 0 <= i * BODY + m < UNITS
                kv = lambda m: has_kv(m) and (kv_every < HEADS or static and i * BODY + m < NSEQ)
                for gi in range(NG):
                    if live(n + 1):
                        score(i, n + 1, gi)
                    if live(n):
                        turn(i, n, gi)
                if live(n + 3):
                    rope_unit(i, n + 3, 0)
                    if kv(n + 3):
                        rope_unit(i, n + 3, 1)
                if live(n):
                    sum_values(i, n)
                if live(n + 2) and kv(n + 2):
                    value_unit(i, n + 2)

            for n in range(-3, 0):
                slot(0, n)
            with pe.Fori(0, LOOPS) as i:
                for n in range(BODY):
                    slot(i, n)
            for n in range(BODY):
                slot(LOOPS, n)
            pe.wait_ge(c["wo"].sem, 16)
            wait(pe, c["okept"], UNITS)
            for t in range(NT):
                for h in range(HEADS):
                    last = pe.matmul(banks[:, t // 2, (t % 2) * H:(t % 2 + 1) * H], o[:, h, t * P:(t + 1) * P],
                                     wo[:, h, :], start=(h == 0), stop=(h == HEADS - 1))
                last.then_inc(c["out"].sem, 1)

        def move_turned(eng, i, n, gi):
            s = n % NSEQ
            wait(eng, c["turned"], NG * n + gi + 1, i, NG * BODY)
            wait(eng, c["values"], n - 1, i, BODY)
            at = 0
            for t in groups[gi]:
                m = len(keys[t])
                src = t_bank[(NG * n + gi) % 2][:, at:at + m * P].rearrange("p (k q) -> p k q", q=P)
                dst = pt[:, s, keys[t][0]:keys[t][-1] + 1, t * P:(t + 1) * P]
                if mover[gi] == "v":
                    last = eng.tensor_copy(dst, src)
                else:
                    last = eng.activation(dst, src, ACT.Copy)
                at += m * P
            last.then_inc(c["pt_" + mover[gi]].sem, 1)

        @block.scalar
        def _(act):
            for n in ("swapped", "expd", "pt_a", "okept", "vkept"):
                act.sem_inc(c[n].sem, c[n].prime)

            def swap_halves(i, m, which):
                r = before(m, "rope") + which
                wait(act, c["proj"], r + 1, i, per_rope)
                wait(act, c["rotated"], r - 1, i, per_rope)
                act.activation(swap[0:P // 2, r % 2, :], p_bank[r % 2][P // 2:P, :], ACT.Copy)
                act.activation(swap[P // 2:P, r % 2, :], p_bank[r % 2][0:P // 2, :], ACT.Copy) \
                    .then_inc(c["swapped"].sem, 1)

            def exps(i, m, gi):
                s = m % NSEQ
                wait(act, c["peak"], NG * m + gi + 1, i, NG * BODY)
                wait(act, c["turned"], NG * (m - 2) + gi + 1, i, NG * BODY)
                for t in groups[gi]:
                    n = len(keys[t]) * P
                    last = act.activation(prob[:, s, cols[t]:cols[t] + n], s_bank[gi][:, psum_col[t]:psum_col[t] + n],
                                          ACT.Exp, bias=peak[:, s, t:t + 1], accum_out=sums[:, s, t:t + 1])
                last.then_inc(c["expd"].sem, 1)

            def slot(i, n):
                static = isinstance(i, int)
                live = lambda m: not static or 0 <= i * BODY + m < UNITS
                kv = lambda m: has_kv(m) and (kv_every < HEADS or static and i * BODY + m < NSEQ)
                for gi in range(NG):
                    if gi == NG - 1 and live(n):
                        move_turned(act, i, n, NG - 1)
                    if live(n + 1):
                        exps(i, n + 1, gi)
                if live(n + 3):
                    swap_halves(i, n + 3, 0)
                    if kv(n + 3):
                        swap_halves(i, n + 3, 1)
                if live(n):
                    wait(act, c["values"], n + 1, i, BODY)
                    h = n // NSEQ
                    s = n % NSEQ
                    at = bass.ds(i * U + h, 1) if not static else slice(i * U + h, i * U + h + 1)
                    act.activation(o[:, at, s * SEQ:(s + 1) * SEQ].rearrange("p a n -> p (a n)"), o_bank,
                                   ACT.Copy).then_inc(c["okept"].sem, 1)
                if live(n + 2) and kv(n + 2):
                    m = n + 2
                    wait(act, c["vproj"], before(m, "v") + 1, i, per_v)
                    wait(act, c["values"], m - 1, i, BODY)
                    act.activation(v[:, m % NSEQ].rearrange("p t n -> p (t n)"), v_bank, ACT.Copy) \
                        .then_inc(c["vkept"].sem, 1)

            for n in range(-3, 0):
                slot(0, n)
            with act.Fori(0, LOOPS) as i:
                for n in range(BODY):
                    slot(i, n)
            for n in range(BODY):
                slot(LOOPS, n)

        @block.vector
        def _(dve):
            dve.wait_ge(c["loaded"].sem, 48)
            dve.tensor_scalar(mask[:, :, :], mask1[:, :, :], NEG, None, ALU.mult) \
                .then_inc(c["ready"].sem, 1)
            for n in ("cosed", "sined", "pt_v"):
                dve.sem_inc(c[n].sem, c[n].prime)

            def peaks(i, m, gi):
                s = m % NSEQ
                wait(dve, c["scores"], NG * m + gi + 1, i, NG * BODY)
                wait(dve, c["expd"], NG * (m - 2) + gi + 1, i, NG * BODY)
                for t in groups[gi]:
                    last = dve.reduce_max(peak[:, s, t:t + 1],
                                          s_bank[gi][:, psum_col[t]:psum_col[t] + len(keys[t]) * P],
                                          axis=AX.X, negate=True)
                last.then_inc(c["peak"].sem, 1)

            def recips(i, m, gi):
                s = m % NSEQ
                wait(dve, c["expd"], NG * m + gi + 1, i, NG * BODY)
                cut = slice(groups[gi][0], groups[gi][-1] + 1)
                dve.reciprocal(recip[:, s, cut], sums[:, s, cut]).then_inc(c["recip"].sem, 1)

            def rotate(i, m, which):
                r = before(m, "rope") + which
                wait(dve, c["swapped"], r + 1, i, per_rope)
                wait(dve, c["rotated"], r - 1, i, per_rope)
                dve.tensor_tensor(cosed[:, r % 2, :], p_bank[r % 2], ropes[:, which, 0, :], ALU.mult) \
                    .then_inc(c["cosed"].sem, 1)
                dve.tensor_tensor(swap[:, r % 2, :], swap[:, r % 2, :], ropes[:, which, 1, :], ALU.mult) \
                    .then_inc(c["sined"].sem, 1)

            def slot(i, n):
                static = isinstance(i, int)
                live = lambda m: not static or 0 <= i * BODY + m < UNITS
                kv = lambda m: has_kv(m) and (kv_every < HEADS or static and i * BODY + m < NSEQ)
                for gi in range(NG):
                    if live(n + 1):
                        peaks(i, n + 1, gi)
                        if gi:
                            recips(i, n + 1, gi - 1)
                    if live(n) and mover[gi] == "v":
                        move_turned(dve, i, n, gi)
                if live(n + 1):
                    recips(i, n + 1, NG - 1)
                if live(n + 3):
                    rotate(i, n + 3, 0)
                    if kv(n + 3):
                        rotate(i, n + 3, 1)

            for n in range(-3, 0):
                slot(0, n)
            with dve.Fori(0, LOOPS) as i:
                for n in range(BODY):
                    slot(i, n)
            for n in range(BODY):
                slot(LOOPS, n)
            for t in range(0, NT, 2):
                dve.wait_ge(c["out"].sem, t + 2)
                x2 = g.x[:, t:t + 2, :].rearrange("p a h -> p (a h)")
                dve.tensor_tensor(x2, x2, banks[:, t // 2, :], ALU.add)

        @block.gpsimd
        def _(pool):
            pool.sem_inc(c["rotated"].sem, c["rotated"].prime)

            def norms(i, m, gi):
                s = m % NSEQ
                wait(pool, c["recip"], NG * m + gi + 1, i, NG * BODY)
                pool.sem_inc(c["turns"].sem, 1)
                for t in groups[gi]:
                    part = prob[:, s, cols[t]:cols[t] + len(keys[t]) * P]
                    last = pool.tensor_scalar(part, part, recip[:, s, t:t + 1], None, ALU.mult)
                last.then_inc(c["normed"].sem, 1)

            def rotated(i, m, which):
                s = m % NSEQ
                r = before(m, "rope") + which
                wait(pool, c["sined"], r + 1, i, per_rope)
                wait(pool, c["cosed"], r + 1, i, per_rope)
                wait(pool, c["scores"], NG * (m - 1), i, NG * BODY)
                pool.tensor_tensor((k if which else q)[:, s, :], cosed[:, r % 2, :], swap[:, r % 2, :], ALU.add) \
                    .then_inc(c["rotated"].sem, 1)

            def slot(i, n):
                static = isinstance(i, int)
                live = lambda m: not static or 0 <= i * BODY + m < UNITS
                kv = lambda m: has_kv(m) and (kv_every < HEADS or static and i * BODY + m < NSEQ)
                if live(n + 1):
                    for gi in range(NG):
                        norms(i, n + 1, gi)
                if live(n + 3):
                    rotated(i, n + 3, 0)
                    if kv(n + 3):
                        rotated(i, n + 3, 1)

            for n in range(-3, 0):
                slot(0, n)
            with pool.Fori(0, LOOPS) as i:
                for n in range(BODY):
                    slot(i, n)
            for n in range(BODY):
                slot(LOOPS, n)
    finish(nc, c.values())


def capacity_mixture(nc, g, d):
    c = {n: Count(nc, n, p) for n, p in (
        ("loaded", 0), ("own_v", 0), ("logits", 0), ("shared_w", 0), ("peak", 0), ("expd", 0), ("masked", 0),
        ("places", 0), ("sparts", 0), ("routed", 0), ("sinner", 0), ("ssilu", 0), ("sprod", 0), ("based", 0),
        ("gu_even", 0), ("gu_odd", 0), ("d_even", 0), ("d_odd", 0),
        ("picked", 4), ("gathered", 4), ("buffered", 4), ("sloted", 4), ("spread0", 4), ("spread1", 4),
        ("kept0", 4), ("kept1", 4), ("inner", 4), ("silu", 4), ("acted", 4), ("turned", 4), ("moved", 4),
        ("down", 4), ("split", 4), ("summed", 4), ("chain", 0), ("parted", 0))}
    gu_full, d_full = (c["gu_even"], c["gu_odd"]), (c["d_even"], c["d_odd"])
    SENTINEL = 2.0
    BODY = 2
    LOOPS = NG1 // BODY - 1
    with ExitStack() as ctx:
        def sb(name, shape, dtype):
            return ctx.enter_context(sbuf(nc, name, shape, dtype))

        router = sb("router", [P, NC, NE1], F32)
        ranks1 = sb("ranks", [P, 2 * P], F32)
        ranks = sb("ranks_b", [P, 2 * P], BF16)
        slot1 = sb("slot1", [P, CAP], F32)
        own = sb("own", [P, GE * 3], F32)
        peak = sb("peak", [P, NT], F32)
        sums = sb("sums", [P, NT], F32)
        score = sb("score", [P, NT, NE1 + 2], F32)
        left = sb("left", [P, NT, NE1 + 2], F32)
        top = sb("top", [P, NT, 8], F32)
        maskb = sb("maskb", [P, NT, NE1], BF16)
        prior = sb("prior", [P, NT, NE1], BF16)
        place = sb("place", [P, NT, NE1], F32)
        wrest = sb("wrest", [P, NT, NE1], F32)
        wpart = sb("wpart", [P, NT, NE1], BF16)
        wparts = sb("wparts", [P, NT, NE1, 3], BF16)
        xrest = sb("xrest", [P, NT, H], F32)
        xparts = sb("xparts", [P, 3, NT, H], BF16)
        shgu = sb("shgu", [P, 2, NC, 2 * FF1], F32)
        shd = sb("shd", [HF1, NSH, H], F32)
        shsilu = sb("shsilu", [HF1, 2, SEQ], F32)
        shinner = sb("shinner", [HF1, NSH, T], F32)
        wgu = sb("wgu", [P, 2, GE, NC, 2 * FF1], F32)
        wd = sb("wd", [HF1, 2, GE, 2, H], F32)
        pick = sb("pick", [P, 2, NT, P], BF16)
        pickt = sb("pickt", [P, 2, T], BF16)
        buf = sb("buf", [P, 2, NC, P], F32)
        wtmp = sb("wtmp", [P, 2, GE * 3], F32)
        wslot = sb("wslot", [P, 2], F32)
        silu = sb("silu", [P, FF1], F32)
        acted = sb("acted", [P, FF1], F32)
        actt = sb("actt", [HF1, 2, P], F32)
        y = sb("y", [P, H], F32)
        yrest = sb("yrest", [P, H], F32)
        yparts = sb("yparts", [P, 2, 3, H], BF16)
        acc = ctx.enter_context(psum(nc, "acc", [P, NT, H], F32))
        banks = ctx.enter_context(psum(nc, "banks", [P, 4, SEQ], F32))
        block = ctx.enter_context(nc.Block())
        b_gather, b_weight = banks[:, 0, 0:NC * P], banks[:, 0, NC * P:NC * P + GE * 3]
        b_spread, b_inner = banks[:, 1, :], banks[:, 2, 0:2 * FF1]
        b_turn, b_out = banks[0:HF1, 3, 0:2 * P], banks[:, 3, H:2 * H]
        wparts_g = wparts[:, :, :, :].rearrange("p t (n e) c -> p t n (e c)", e=GE)
        b_sh = acc[:, :, :].rearrange("p (b s) h -> p b (s h)", s=2)

        @block.sync
        def _(sp):
            for to, name in ((router[:, :, :], "router1"), (ranks1[:, :], "before"), (slot1[:, :], "slot1"),
                             (own[:, :], "own")):
                sp.dma_start(to, d[name]).then_inc(c["loaded"].sem, 16)
            sp.dma_start(shgu[:, :, :, :], d["shared1_gu"].rearrange("p a c n -> p a c n")).then_inc(c["shared_w"].sem, 16)
            sp.dma_start(shd[:, :, :], d["shared1_d"]).then_inc(c["shared_w"].sem, 16)
            with sp.Fori(0, NG1 // BODY) as i:
                for k in range(BODY):
                    at = bass.ds(BODY * i + k, 1)
                    wait(sp, c["inner"], k - 1, i, BODY)
                    sp.dma_start(wgu[:, k], d["w1_gu"][at].rearrange("o p e c n -> p (o e) c n")) \
                        .then_inc(gu_full[k].sem, 16)
                    wait(sp, c["down"], k - 1, i, BODY)
                    sp.dma_start(wd[:, k], d["w1_d"][at].rearrange("o p e c n -> p (o e) c n")) \
                        .then_inc(d_full[k].sem, 16)

        def live(i, m):
            return not isinstance(i, int) or 0 <= i * BODY + m < NG1

        @block.tensor
        def _(pe):
            for n in ("inner", "down", "gathered", "spread0", "spread1", "turned", "summed"):
                pe.sem_inc(c[n].sem, c[n].prime)
            pe.wait_ge(c["loaded"].sem, 64)
            for t in range(NT):
                for kc in range(NC):
                    last = pe.matmul(banks[:, 0, t * NE1:(t + 1) * NE1], g.xt[:, kc, t * P:(t + 1) * P],
                                     router[:, kc, :], start=(kc == 0), stop=(kc == NC - 1))
            last.then_inc(c["logits"].sem, 1)
            def count_places():
                pe.wait_ge(c["masked"].sem, 1)
                for t in range(NT):
                    pe.matmul(banks[:, 1, t * NE1:(t + 1) * NE1], ranks[:, 0:P], maskb[:, t, :], start=True, stop=False)
                    last = pe.matmul(banks[:, 1, t * NE1:(t + 1) * NE1], ranks[:, P:], prior[:, t, :],
                                     start=False, stop=True)
                last.then_inc(c["places"].sem, 1)

            pe.wait_ge(c["shared_w"].sem, 32)
            for j in range(NSH):
                for s in range(NSEQ):
                    n = j * NSEQ + s
                    if n == 4:
                        count_places()
                    wait(pe, c["sprod"], n - 1)
                    for which in range(2):
                        for kc in range(NC):
                            last = pe.matmul(b_sh[0:HF1, (n % 2) * 2 + which, :],
                                             shgu[:, which, kc, j * HF1:(j + 1) * HF1],
                                             g.xt[:, kc, s * SEQ:(s + 1) * SEQ], start=(kc == 0), stop=(kc == NC - 1))
                    last.then_inc(c["sinner"].sem, 1)
            wait(pe, c["sprod"], NSH * NSEQ)
            for t in range(NT):
                for j in range(NSH):
                    pe.matmul(acc[:, t, :], shinner[:, j, t * P:(t + 1) * P], shd[:, j, :],
                              start=(j == 0 and t % 2 == 0), stop=True, skip_group_check=True)
            pe.wait_ge(c["parted"].sem, 1)

            def gather(i, m):
                k = m % 2
                wait(pe, c["picked"], m + 1, i, BODY)
                wait(pe, c["buffered"], m, i, BODY)
                wait(pe, c["sloted"], m, i, BODY)
                for hc in range(NC):
                    for t in range(NT):
                        for part in range(3):
                            pe.matmul(b_gather[:, hc * P:(hc + 1) * P], xparts[:, part, t, hc * P:(hc + 1) * P],
                                      pick[:, k, t, :], start=(t == 0 and part == 0),
                                      stop=(t == NT - 1 and part == 2))
                at = bass.ds(BODY * i + m, 1) if not isinstance(i, int) else slice(BODY * i + m, BODY * i + m + 1)
                for t in range(NT):
                    last = pe.matmul(b_weight, pick[:, k, t, :], wparts_g[:, t, at, :].rearrange("p o w -> p (o w)"),
                                     start=(t == 0), stop=(t == NT - 1))
                last.then_inc(c["gathered"].sem, 1)

            def spread(i, m, half):
                k = m % 2
                wait(pe, c["kept1" if half == 0 else "kept0"], m + half, i, BODY)
                for j in range(4):
                    t = 4 * half + j
                    last = pe.matmul(b_spread[:, j * P:(j + 1) * P], pick[:, k, t, :], g.identb[:, :],
                                     start=True, stop=True)
                last.then_inc(c[f"spread{half}"].sem, 1)

            def inner(i, n):
                k = n % 2
                wait(pe, gu_full[k], 16 * (n // 2) + 16, i, 16)
                wait(pe, c["buffered"], n + 1, i, BODY)
                wait(pe, c["acted"], n, i, BODY)
                for kc in range(NC):
                    for e in range(GE):
                        last = pe.matmul(b_inner[e * CAP:(e + 1) * CAP, :], buf[:, k, kc, e * CAP:(e + 1) * CAP],
                                         wgu[:, k, e, kc, :], start=(kc == 0), stop=(kc == NC - 1),
                                         tile_position=(0, e * CAP))
                last.then_inc(c["inner"].sem, 1)

            def turn(i, n):
                wait(pe, c["acted"], n + 1, i, BODY)
                wait(pe, c["split"], n, i, BODY)
                for j in range(2):
                    last = pe.transpose(b_turn[:, j * P:(j + 1) * P], acted[:, j * HF1:(j + 1) * HF1], g.ident[:, :])
                last.then_inc(c["turned"].sem, 1)

            def down(i, n):
                k = n % 2
                wait(pe, d_full[k], 16 * (n // 2) + 16, i, 16)
                wait(pe, c["moved"], n + 1, i, BODY)
                for j in range(2):
                    for e in range(GE):
                        last = pe.matmul(b_out[e * CAP:(e + 1) * CAP, :], actt[:, j, e * CAP:(e + 1) * CAP],
                                         wd[:, k, e, j, :], start=(j == 0), stop=(j == 1),
                                         tile_position=(0, e * CAP))
                last.then_inc(c["down"].sem, 1)

            def sum_up(i, n):
                k = n % 2
                wait(pe, c["split"], n + 1, i, BODY)
                wait(pe, c["kept0"], n + 1, i, BODY)
                wait(pe, c["kept1"], n + 1, i, BODY)
                for t in range(NT):
                    for part in range(3):
                        last = pe.matmul(acc[:, t, :], pickt[:, k, t * P:(t + 1) * P], yparts[:, k, part, :],
                                         start=False, stop=True, skip_group_check=True)
                last.then_inc(c["summed"].sem, 1)

            def slot(i, n):
                if live(i, n + 1):
                    gather(i, n + 1)
                if live(i, n):
                    inner(i, n)
                if live(i, n - 1):
                    sum_up(i, n - 1)
                if live(i, n + 1):
                    spread(i, n + 1, 0)
                if live(i, n):
                    turn(i, n)
                if live(i, n + 1):
                    spread(i, n + 1, 1)
                if live(i, n):
                    down(i, n)

            slot(0, -1)
            slot(0, 0)
            slot(0, 1)
            with pe.Fori(1, LOOPS) as i:
                for n in range(BODY):
                    slot(i, n)
            for n in range(BODY + 1):
                slot(LOOPS, n)

        @block.scalar
        def _(act):
            for n in ("buffered", "silu", "moved", "kept1"):
                act.sem_inc(c[n].sem, c[n].prime)
            act.wait_ge(c["peak"].sem, 1)
            for t in range(NT):
                last = act.activation(score[:, t, 0:NE1], banks[:, 0, t * NE1:(t + 1) * NE1], ACT.Exp,
                                      bias=peak[:, t:t + 1], accum_out=sums[:, t:t + 1])
            last.then_inc(c["expd"].sem, 1)
            for n in range(NSH * NSEQ):
                act.wait_ge(c["sinner"].sem, n + 1)
                wait(act, c["sprod"], n - 1)
                act.activation(shsilu[:, n % 2, :], b_sh[0:HF1, (n % 2) * 2, :], ACT.Silu).then_inc(c["ssilu"].sem, 1)

            def slot(i, n):
                if live(i, n + 1):
                    m = n + 1
                    wait(act, c["gathered"], m + 1, i, BODY)
                    wait(act, c["inner"], m - 1, i, BODY)
                    act.activation(buf[:, m % 2].rearrange("p c s -> p (c s)"), b_gather, ACT.Copy) \
                        .then_inc(c["buffered"].sem, 1)
                if live(i, n):
                    wait(act, c["inner"], n + 1, i, BODY)
                    wait(act, c["acted"], n, i, BODY)
                    act.activation(silu[:, :], b_inner[:, 0:FF1], ACT.Silu).then_inc(c["silu"].sem, 1)
                    wait(act, c["turned"], n + 1, i, BODY)
                    wait(act, c["down"], n, i, BODY)
                    act.activation(actt[:, :, :].rearrange("p c s -> p (c s)"), b_turn, ACT.Copy) \
                        .then_inc(c["moved"].sem, 1)
                if live(i, n + 1):
                    m = n + 1
                    wait(act, c["spread1"], m + 1, i, BODY)
                    wait(act, c["summed"], m - 1, i, BODY)
                    act.activation(pickt[:, m % 2, SEQ:T], b_spread, ACT.Copy).then_inc(c["kept1"].sem, 1)

            slot(0, -1)
            slot(0, 0)
            slot(0, 1)
            with act.Fori(1, LOOPS) as i:
                for n in range(BODY):
                    slot(i, n)
            for n in range(BODY):
                slot(LOOPS, n)

        @block.vector
        def _(dve):
            for n in ("picked", "sloted", "kept0", "acted", "split"):
                dve.sem_inc(c[n].sem, c[n].prime)
            done = [0]

            def link(op):
                done[0] += 1
                op.then_inc(c["own_v"].sem, 1)
                dve.wait_ge(c["own_v"].sem, done[0])

            dve.memset(score[:, :, NE1:], SENTINEL)
            dve.memset(prior[:, 0, :], 0.0)
            dve.wait_ge(c["loaded"].sem, 64)
            dve.tensor_copy(ranks[:, :], ranks1[:, :])
            dve.wait_ge(c["logits"].sem, 1)
            dve.reduce_max(peak[:, :], banks[:, 0, :].rearrange("p (t e) -> p t e", t=NT), axis=AX.X, negate=True) \
                .then_inc(c["peak"].sem, 1)
            dve.wait_ge(c["expd"].sem, 1)
            link(dve.reciprocal(sums[:, :], sums[:, :]))
            link(dve.tensor_tensor(score[:, :, 0:NE1], score[:, :, 0:NE1],
                                   sums[:, :].unsqueeze(2).broadcast_to([P, NT, NE1]), ALU.mult))
            for t in range(NT):
                op = dve.max(top[:, t, :], score[:, t, 0:NE1])
            link(op)
            link(dve.memset(top[:, :, TOP1:], SENTINEL))
            for t in range(NT):
                op = dve.match_replace(left[:, t, :], top[:, t, :], score[:, t, :], -1.0)
            link(op)
            dve.tensor_scalar(maskb[:, :, :], left[:, :, 0:NE1], 0.0, None, ALU.is_lt)
            link(dve.scalar_tensor_tensor(wrest[:, :, :], left[:, :, 0:NE1], 0.0, score[:, :, 0:NE1],
                                          ALU.is_lt, ALU.mult))
            for t in range(1, NT):
                op = dve.tensor_tensor(prior[:, t, :], prior[:, t - 1, :], maskb[:, t - 1, :], ALU.add)
                if t < NT - 1:
                    link(op)
            op.then_inc(c["masked"].sem, 1)

            def shared_product(n):
                j, s = n // NSEQ, n % NSEQ
                dve.wait_ge(c["ssilu"].sem, n + 1)
                dve.tensor_tensor(shinner[:, j, s * SEQ:(s + 1) * SEQ], shsilu[:, n % 2, :],
                                  b_sh[0:HF1, (n % 2) * 2 + 1, :], ALU.mult).then_inc(c["sprod"].sem, 1)

            shared_product(0)
            shared_product(1)
            link(dve.tensor_copy(wpart[:, :, :], wrest[:, :, :]))
            dve.tensor_copy(wparts[:, :, :, 0], wpart[:, :, :])
            link(dve.tensor_tensor(wrest[:, :, :], wrest[:, :, :], wpart[:, :, :], ALU.subtract))
            shared_product(2)
            link(dve.tensor_copy(wpart[:, :, :], wrest[:, :, :]))
            dve.tensor_copy(wparts[:, :, :, 1], wpart[:, :, :])
            link(dve.tensor_tensor(wrest[:, :, :], wrest[:, :, :], wpart[:, :, :], ALU.subtract))
            dve.tensor_copy(wparts[:, :, :, 2], wrest[:, :, :])
            shared_product(3)
            dve.wait_ge(c["places"].sem, 1)
            link(dve.tensor_scalar(place[:, :, :].rearrange("p t e -> p (t e)"), banks[:, 1, :], 1.0, 2.0 * CAP,
                                   ALU.add, ALU.min))
            link(dve.tensor_tensor(place[:, :, :], place[:, :, :], maskb[:, :, :], ALU.mult))
            shared_product(4)
            for part in range(3):
                src = xrest if part else g.xn
                link(dve.tensor_copy(xparts[:, part], src[:, :, :]))
                if part < 2:
                    op = dve.tensor_tensor(xrest[:, :, :], src[:, :, :], xparts[:, part], ALU.subtract)
                    link(op)
                shared_product(5 + part)
            dve.sem_inc(c["parted"].sem, 1)

            def picks(i, m):
                wait(dve, c["spread1"], m - 1, i, BODY)
                at = bass.ds((BODY * i + m) * GE, GE) if not isinstance(i, int) \
                    else slice((BODY * i + m) * GE, (BODY * i + m + 1) * GE)
                dve.tensor_tensor(pick[:, m % 2].rearrange("p t (e s) -> p t e s", s=CAP),
                                  place[:, :, at].unsqueeze(3).broadcast_to([P, NT, GE, CAP]),
                                  slot1[:, :].unsqueeze(1).unsqueeze(1).broadcast_to([P, NT, GE, CAP]),
                                  ALU.is_equal).then_inc(c["picked"].sem, 1)

            chained = [0]

            def slot(i, n):
                if live(i, n + 1):
                    m = n + 1
                    wait(dve, c["gathered"], m + 1, i, BODY)
                    wait(dve, c["buffered"], m + 1, i, BODY)
                    wait(dve, c["split"], m - 1, i, BODY)
                    dve.tensor_tensor_reduce(out=wtmp[:, m % 2, :], in0=b_weight, in1=own[:, :], scale=1.0, scalar=0.0,
                                             op0=ALU.mult, op1=ALU.add, accum_out=wslot[:, m % 2:m % 2 + 1]) \
                        .then_inc(c["sloted"].sem, 1)
                if live(i, n):
                    wait(dve, c["silu"], n + 1, i, BODY)
                    wait(dve, c["turned"], n, i, BODY)
                    dve.tensor_tensor(acted[:, :], silu[:, :], b_inner[:, FF1:2 * FF1], ALU.mult) \
                        .then_inc(c["acted"].sem, 1)
                if live(i, n + 1):
                    m = n + 1
                    wait(dve, c["spread0"], m + 1, i, BODY)
                    wait(dve, c["summed"], m - 1, i, BODY)
                    dve.tensor_copy(pickt[:, m % 2, 0:SEQ], b_spread).then_inc(c["kept0"].sem, 1)
                if live(i, n + 2):
                    picks(i, n + 2)
                if live(i, n):
                    k = n % 2
                    wait(dve, c["down"], n + 1, i, BODY)
                    wait(dve, c["sloted"], n + 1, i, BODY)
                    wait(dve, c["summed"], n - 1, i, BODY)
                    at = 4 * n if isinstance(i, int) else 4 * n
                    dve.tensor_scalar(y[:, :], b_out, wslot[:, k:k + 1], None, ALU.mult).then_inc(c["chain"].sem, 1)
                    wait(dve, c["chain"], at + 1, i, 4 * BODY)
                    dve.tensor_copy(yparts[:, k, 0, :], y[:, :]).then_inc(c["chain"].sem, 1)
                    wait(dve, c["chain"], at + 2, i, 4 * BODY)
                    dve.tensor_tensor(y[:, :], y[:, :], yparts[:, k, 0, :], ALU.subtract).then_inc(c["chain"].sem, 1)
                    wait(dve, c["chain"], at + 3, i, 4 * BODY)
                    dve.tensor_copy(yparts[:, k, 1, :], y[:, :]).then_inc(c["chain"].sem, 1)
                    wait(dve, c["chain"], at + 4, i, 4 * BODY)
                    dve.tensor_tensor(yparts[:, k, 2, :], y[:, :], yparts[:, k, 1, :], ALU.subtract) \
                        .then_inc(c["split"].sem, 1)

            picks(0, 0)
            slot(0, -1)
            slot(0, 0)
            slot(0, 1)
            with dve.Fori(1, LOOPS) as i:
                for n in range(BODY):
                    slot(i, n)
            for n in range(BODY):
                slot(LOOPS, n)
            wait(dve, c["summed"], NG1)
            for t in range(0, NT, 2):
                x2 = g.x[:, t:t + 2, :].rearrange("p a h -> p (a h)")
                dve.tensor_tensor(x2, x2, acc[:, t:t + 2, :].rearrange("p a h -> p (a h)"), ALU.add)
    finish(nc, c.values())


class Shared:
    pass


def hybrid_layers_kernel(nc, ins, out):
    g = Shared()
    with (
        nc.sbuf_tensor("x", [P, NT, H], F32) as g.x,
        nc.sbuf_tensor("xn", [P, NT, H], F32) as g.xn,
        nc.sbuf_tensor("xt", [P, NC, T], F32) as g.xt,
        nc.sbuf_tensor("ident", [P, P], F32) as g.ident,
        nc.sbuf_tensor("identb", [P, P], BF16) as g.identb,
        nc.sbuf_tensor("zeros", [P, SEQ], BF16) as g.zeros,
        nc.sbuf_tensor("eps", [P, 1], F32) as g.eps,
        nc.sbuf_tensor("one", [P, 1], F32) as g.one,
        nc.sbuf_tensor("gamma", [P, NC], F32) as g.gamma,
    ):
        loaded, = counts = [Count(nc, "loaded")]
        with nc.Block() as block:
            @block.sync
            def _(sp):
                sp.dma_start(g.x[:, :, :], ins["x"]).then_inc(loaded.sem, 16)
                sp.dma_start(g.ident[:, :], ins["ident"]).then_inc(loaded.sem, 16)
                sp.dma_start(g.gamma[:, :], ins["gamma"]).then_inc(loaded.sem, 16)
                sp.wait_ge(loaded.sem, 48)

            @block.vector
            def _(dve):
                dve.memset(g.zeros[:, :], 0.0)
                dve.memset(g.eps[:, :], EPS)
                dve.memset(g.one[:, :], 1.0)
                dve.wait_ge(loaded.sem, 48)
                dve.tensor_copy(g.identb[:, :], g.ident[:, :])
        finish(nc, counts)

        stages(nc, g, ins)

        stored, = counts = [Count(nc, "stored")]
        with nc.Block() as block:
            @block.sync
            def _(sp):
                sp.dma_start(out, g.x[:, :, :]).then_inc(stored.sem, 16)
                sp.wait_ge(stored.sem, 16)


def stages(nc, g, ins):
    layer_norm(nc, g)
    selective_scan(nc, g, ins)
    layer_norm(nc, g)
    mixture(nc, g, ins)
    layer_norm(nc, g, gamma=g.gamma, again=True)
    attention(nc, g, ins, "mqa", kv_every=HEADS, window=False)
    layer_norm(nc, g)
    mixture(nc, g, ins)
    layer_norm(nc, g)
    attention(nc, g, ins, "gqa", kv_every=4, window=False)
    layer_norm(nc, g)
    capacity_mixture(nc, g, ins)
    layer_norm(nc, g)
    attention(nc, g, ins, "mha", kv_every=1, window=True)
    layer_norm(nc, g)
    capacity_mixture(nc, g, ins)


def kernel(**inputs):
    import numpy as np
    import concourse.bacc as bacc
    from concourse.bass_utils import run_bass_kernel_spmd

    a = {k: np.asarray(v) for k, v in inputs.items()}

    def chunks(w):
        w = w.reshape(*w.shape[:-2], -1, P, w.shape[-1])
        return np.moveaxis(w, -3, -2)

    def heads(w):
        return np.moveaxis(chunks(w).reshape(P, NC, -1, P), 2, 0)

    def tokens(x):
        return x.reshape(NT, P, H).transpose(1, 0, 2)

    arrays = {}
    arrays["x"] = tokens(a["L0_attn_a_hidden_states"].reshape(T, H))
    arrays["ident"] = np.eye(P, dtype=np.float32)
    arrays["gamma"] = a["L0_attn_b_gamma"].reshape(NC, P).T

    w = a["L0_attn_a_x_proj_w"].T
    bc, dt = w[:, DT_RANK:], w[:, :DT_RANK]
    arrays["xw"] = chunks(np.concatenate([bc, bc, bc, dt], 1))
    dtw = np.zeros((XROWS, H), np.float32)
    dtw[XROWS - DT_RANK:] = a["L0_attn_a_dt_proj_w"].T
    arrays["dtw"] = dtw
    arrays["vecs"] = np.concatenate([
        a["L0_attn_a_dt_proj_b"].reshape(NC, P).T, a["L0_attn_a_D"].reshape(NC, P).T,
        a["L0_attn_a_A_log"].reshape(NC, P, N_STATE).transpose(1, 0, 2).reshape(P, -1)], 1)
    arrays["pick"] = np.tile(np.eye(2 * N_STATE, dtype=np.float32), (3, 1))

    gate, up, down = (a["L0_ffn_" + n] for n in ("Wg", "Wu", "Wd"))
    sgate, sup, sdown = (a["L0_ffn_s" + n] for n in ("Wg", "Wu", "Wd"))
    gate = np.concatenate([gate, sgate.reshape(H, 2, FF0).transpose(1, 0, 2)])
    up = np.concatenate([up, sup.reshape(H, 2, FF0).transpose(1, 0, 2)])
    down = np.concatenate([down, sdown.reshape(2, FF0, H)])
    arrays["w0"] = np.concatenate([chunks(gate).reshape(NU0, P, -1), chunks(up).reshape(NU0, P, -1), down], 2)
    arrays["router0"] = chunks(a["L0_ffn_gate_w"].T)

    inv = 1.0 / np.float32(10000.0) ** (np.arange(0, P, 2, dtype=np.float32) / np.float32(P))
    angle = np.arange(SEQ, dtype=np.float32)[None, :] * inv.astype(np.float32)[:, None]
    cos, sin = np.cos(angle), np.sin(angle)
    rope = np.stack([np.concatenate([cos, cos]), np.concatenate([-sin, sin])], 1)
    arrays["rope_k"] = rope
    arrays["rope_q"] = rope * np.float32(P ** -0.5)
    q, k = np.arange(P)[:, None], np.arange(P)[None, :]
    arrays["mask"] = np.concatenate([np.where(k > q, 0, 1), np.where(k > q, 1, 0)], 1).astype(np.float32)
    pairs = np.concatenate([np.arange(0, P, 2), np.arange(1, P, 2)])

    def unpaired(w):
        return w.T.reshape(H, -1, P)[:, :, pairs].reshape(H, -1)

    kv = a["L0_attn_b_Wkv"]
    weights = {
        "mqa": (a["L0_attn_b_Wq"], kv[:, :P], kv[:, P:], a["L0_attn_b_Wo"]),
        "gqa": (unpaired(a["L1_attn_a_Wq"]), unpaired(a["L1_attn_a_Wk"]), a["L1_attn_a_Wv"].T, a["L1_attn_a_Wo"].T),
        "mha": tuple(a["L1_attn_b_" + n] for n in ("wq", "wk", "wv", "wo")),
    }
    for n, (wq, wk, wv, wo) in weights.items():
        arrays[n + "_q"] = heads(wq)
        arrays[n + "_kv"] = np.stack([heads(wk), heads(wv)], 2)
        arrays[n + "_o"] = wo.reshape(HEADS, P, H).transpose(1, 0, 2)

    gu = chunks(np.concatenate([a["L1_ffn_w_gate"], a["L1_ffn_w_up"]], 2))
    arrays["w1_gu"] = gu.reshape(NG1, GE, P, NC, 2 * FF1).transpose(0, 2, 1, 3, 4)
    arrays["w1_d"] = a["L1_ffn_w_down"].reshape(NG1, GE, 2, HF1, H).transpose(0, 3, 1, 2, 4)
    arrays["shared1_gu"] = np.stack([chunks(a["L1_ffn_sw_gate"]), chunks(a["L1_ffn_sw_up"])], 1)
    arrays["shared1_d"] = a["L1_ffn_sw_down"].reshape(NSH, HF1, H).transpose(1, 0, 2)
    arrays["router1"] = chunks(a["L1_ffn_gate_w"].T)
    t = np.arange(P)
    arrays["before"] = np.concatenate([(t[:, None] < t[None, :]).astype(np.float32), np.ones((P, P), np.float32)], 1)
    arrays["slot1"] = np.tile(np.arange(1, CAP + 1, dtype=np.float32), (P, 1))
    arrays["own"] = np.repeat((t[:, None] // CAP == np.arange(GE)[None, :]).astype(np.float32)[:, None, :], 3, 1) \
        .transpose(0, 2, 1).reshape(P, GE * 3)

    nc = bacc.Bacc("TRN2", target_bir_lowering=False, num_devices=1)
    sent, ins = {}, {}
    for name, v in arrays.items():
        v = np.ascontiguousarray(v, dtype=np.float32)
        sent["in_" + name] = v
        ins[name] = nc.dram_tensor("in_" + name, v.shape, F32, kind="ExternalInput").ap()
    out = nc.dram_tensor("out", (P, NT, H), F32, kind="ExternalOutput").ap()
    hybrid_layers_kernel(nc, ins, out)
    r = run_bass_kernel_spmd(nc, [sent], core_ids=[0])
    got = r.results[0]["out"]
    return got.transpose(1, 0, 2).reshape(NSEQ, SEQ, H)
```

```python
from contextlib import ExitStack

import concourse.bass as bass
from concourse import mybir

F32 = mybir.dt.float32
BF16 = mybir.dt.bfloat16
F32R = mybir.dt.float32r
ALU = mybir.AluOpType
ACT = mybir.ActivationFunctionType
AX = mybir.AxisListType

P = 128
T, H = 1024, 256
SEQ = 512
NSEQ = T // SEQ
NT, NC = T // P, H // P
EPS = 1e-5

HEADS = 16
N_STATE, DT_RANK = 16, 16
XROWS = 3 * 2 * N_STATE + DT_RANK

NE0, TOP0, FF0 = 16, 8, 128
NU0 = NE0 + 2
ROUTED_SCALE = 2.5

NE1, TOP1, FF1 = 64, 6, 176
CAP = 32
HF1 = FF1 // 2
GE = P // CAP
NG1 = NE1 // GE
NSH = 2 * FF1 // HF1
NEG = -1e30


class Count:

    def __init__(self, nc, name, prime=0):
        self.sem = nc.alloc_semaphore(f"{name}_{nc.next_id()}")
        self.prime = prime


def sbuf(nc, name, shape, dtype):
    return nc.sbuf_tensor(f"{name}_{nc.next_id()}", shape, dtype)


def psum(nc, name, shape, dtype):
    return nc.psum_tensor(f"{name}_{nc.next_id()}", shape, dtype)


def wait(eng, count, n, i=0, per=0):
    if isinstance(i, int):
        n += i * per
        if n > 0:
            eng.wait_ge(count.sem, n + count.prime)
    else:
        assert n + count.prime > 0, (count.sem, n)
        eng.wait_ge(count.sem, i * per + (n + count.prime))


def finish(nc, counts):
    nc.clear_and_free_semaphores([c.sem for c in counts])
    nc.all_engine_barrier(sem_only=True)


def layer_norm(nc, g, gamma=None, again=False, split=False):
    rounds = 2 if again else 1
    stats, moved, rooted, normed, turned, kept_v, kept_a, high = counts = [
        Count(nc, n) for n in ("stats", "moments", "rooted", "normed", "turned", "kept_v", "kept_a", "high")]
    with (
        sbuf(nc, "bn", [P, NT, 6], F32) as bn,
        sbuf(nc, "mv", [P, NT, 2], F32) as mv,
        sbuf(nc, "std", [P, NT], F32) as std,
        sbuf(nc, "rstd", [P, NT], F32) as rstd,
        psum(nc, "turn", [P, NC, T], F32) as turn,
        nc.Block() as block,
    ):
        @block.vector
        def _(dve):
            for r in range(rounds):
                src = g.xn if r else g.x
                if r:
                    dve.wait_ge(normed.sem, NT * r)
                for t in range(NT):
                    dve.bn_stats(bn[:, t, :], src[:, t, :]).then_inc(stats.sem, 1)
                for t in range(NT):
                    dve.wait_ge(stats.sem, NT * r + t + 1)
                    dve.bn_aggr(mv[:, t, :], bn[:, t, :]).then_inc(moved.sem, 1)
                dve.wait_ge(rooted.sem, r + 1)
                dve.reciprocal(rstd[:, :], std[:, :]).then_inc(moved.sem, 1)
                dve.wait_ge(moved.sem, (NT + 1) * (r + 1))
                for t in range(NT):
                    dve.tensor_scalar(g.xn[:, t, :], src[:, t, :], mv[:, t, 0:1], rstd[:, t:t + 1],
                                      ALU.subtract, ALU.mult).then_inc(normed.sem, 1)
            for c in range(NC):
                dve.wait_ge(turned.sem, c * NT + NT // 2)
                src = turn[:, c, 0:SEQ]
                if gamma is None:
                    op = dve.tensor_copy(g.xt[:, c, 0:SEQ], src)
                else:
                    op = dve.tensor_scalar(g.xt[:, c, 0:SEQ], src, gamma[:, c:c + 1], None, ALU.mult)
                op.then_inc(kept_v.sem, 1)
            for j in range(NC * NSEQ if split else 0):
                dve.wait_ge(high.sem, j + 1)
                c, cut = j // NSEQ, slice(j % NSEQ * SEQ, (j % NSEQ + 1) * SEQ)
                dve.tensor_tensor(g.xl[:, c, cut], g.xt[:, c, cut], g.xh[:, c, cut].bitcast(F32), ALU.subtract)

        @block.scalar
        def _(act):
            for r in range(rounds):
                act.wait_ge(moved.sem, (NT + 1) * r + NT)
                act.activation(std[:, :], mv[:, :, 1], ACT.Sqrt, bias=g.eps[:, 0:1]).then_inc(rooted.sem, 1)
            for c in range(NC):
                act.wait_ge(turned.sem, (c + 1) * NT)
                src = turn[:, c, SEQ:T]
                if gamma is None:
                    op = act.activation(g.xt[:, c, SEQ:T], src, ACT.Copy)
                else:
                    op = act.activation(g.xt[:, c, SEQ:T], src, ACT.Copy, scale=gamma[:, c:c + 1])
                op.then_inc(kept_a.sem, 1)
                for s in range(NSEQ if split else 0):
                    act.wait_ge((kept_v, kept_a)[s].sem, c + 1)
                    cut = slice(s * SEQ, (s + 1) * SEQ)
                    act.activation(g.xh[:, c, cut], g.xt[:, c, cut], ACT.Copy).then_inc(high.sem, 1)

        @block.tensor
        def _(pe):
            for c in range(NC):
                for t in range(NT):
                    pe.wait_ge(normed.sem, NT * (rounds - 1) + t + 1)
                    pe.transpose(turn[:, c, t * P:(t + 1) * P], g.xn[:, t, c * P:(c + 1) * P],
                                 g.ident[:, :]).then_inc(turned.sem, 1)
    finish(nc, counts)


def selective_scan(nc, g, d):
    c = {n: Count(nc, n, p) for n, p in (
        ("loaded", 0), ("projected", 0), ("rows", 0), ("split", 0), ("dt", 0), ("soft_a", 0), ("soft_v", 0),
        ("ready", 0), ("spread", 0), ("copied", 2), ("decay", 0), ("driven", 0), ("state", 4),
        ("read", 4), ("summed", 4), ("gated", 0), ("turned", 0), ("zeroed", 0), ("selected", 0), ("added", 0))}
    HALF = 2 * N_STATE
    with (
        sbuf(nc, "xw", [P, NC, XROWS], F32) as xw,
        sbuf(nc, "dtw", [XROWS, H], F32) as dtw,
        sbuf(nc, "vecs", [P, 2 * NC + NC * N_STATE], F32) as vecs,
        sbuf(nc, "pick1", [3 * HALF, HALF], F32) as pick1,
        sbuf(nc, "pick", [3 * HALF, HALF, P], BF16) as pick,
        sbuf(nc, "rows", [XROWS, T], F32) as rows,
        sbuf(nc, "rest", [3 * HALF, T], F32) as rest,
        sbuf(nc, "part", [3 * HALF, T], BF16) as part,
        sbuf(nc, "stack", [3 * HALF, T], BF16) as stack,
        sbuf(nc, "nega", [P, NC, N_STATE], F32) as nega,
        sbuf(nc, "delta", [P, NC, T], F32) as delta,
        sbuf(nc, "du", [P, NC, T], F32) as du,
        sbuf(nc, "decay", [P, 2, NC, T], F32) as decay,
        sbuf(nc, "drive", [P, 2, NC, T], F32) as drive,
        sbuf(nc, "state", [P, 2, NC, T], F32) as state,
        sbuf(nc, "bs", [P, 2, T], F32) as bs,
        sbuf(nc, "cs", [P, 2, T], F32) as cs,
        psum(nc, "acc", [P, NC, T], F32) as acc,
        psum(nc, "wide", [P, 2, T], F32) as wide,
        nc.Block() as block,
    ):
        bias, dvec, alog = vecs[:, 0:NC], vecs[:, NC:2 * NC], vecs[:, 2 * NC:].rearrange("p (c n) -> p c n", c=NC)
        z, e, lg = decay[:, 0], decay[:, 1], drive[:, 0]
        r1, c1 = drive[:, 1], state[:, 0]
        term = drive

        @block.sync
        def _(sp):
            sp.dma_start(xw[:, :, :], d["xw"]).then_inc(c["loaded"].sem, 16)
            sp.dma_start(dtw[:, :], d["dtw"]).then_inc(c["loaded"].sem, 16)
            sp.dma_start(vecs[:, :], d["vecs"]).then_inc(c["loaded"].sem, 16)
            sp.dma_start(pick1[:, :], d["pick"]).then_inc(c["loaded"].sem, 16)

        @block.gpsimd
        def _(pool):
            pool.wait_ge(c["loaded"].sem, 64)
            pool.tensor_copy(pick[:, :, :], pick1[:, :].unsqueeze(2).broadcast_to([3 * HALF, HALF, P])) \
                .then_inc(c["selected"].sem, 1)
            pool.sem_inc(c["read"].sem, c["read"].prime)
            with pool.Fori(0, N_STATE // 2) as i:
                for k in range(2):
                    for dc in range(NC):
                        wait(pool, c["state"], 2 * k + dc + 1, i, 4)
                        wait(pool, c["copied"], 2 * (k + 1), i, 4)
                        pool.tensor_tensor(term[:, k, dc, :], state[:, k, dc, :], cs[:, k, :], ALU.mult) \
                            .then_inc(c["read"].sem, 1)

        @block.tensor
        def _(pe):
            pe.wait_ge(c["loaded"].sem, 64)
            for s in range(NSEQ):
                for kc in range(NC):
                    last = pe.matmul(acc[0:XROWS, 0, s * SEQ:(s + 1) * SEQ], xw[:, kc, :],
                                     g.xt[:, kc, s * SEQ:(s + 1) * SEQ], start=(kc == 0), stop=(kc == NC - 1))
                last.then_inc(c["projected"].sem, 1)
            pe.wait_ge(c["rows"].sem, 2)
            for dc in range(NC):
                for s in range(NSEQ):
                    pe.matmul(wide[:, dc, s * SEQ:(s + 1) * SEQ], dtw[:, dc * P:(dc + 1) * P],
                              rows[:, s * SEQ:(s + 1) * SEQ], start=True, stop=True).then_inc(c["dt"].sem, 1)
            for dc in range(NC):
                for s in range(NSEQ):
                    pe.matmul(acc[:, dc, s * SEQ:(s + 1) * SEQ], g.zeros[:, 0:P], g.zeros[:, :],
                              start=True, stop=True)
            pe.sem_inc(c["summed"].sem, c["summed"].prime)
            pe.wait_ge(c["split"].sem, 1)
            pe.wait_ge(c["selected"].sem, 1)

            def spread(i, k):
                for which in range(2):
                    wait(pe, c["copied"], 2 * k - 1 + which, i, 4)
                    for s in range(NSEQ):
                        lhs = pick[:, bass.ds(2 * i + (k + which * N_STATE), 1), :].rearrange("p o m -> p (o m)")
                        last = pe.matmul(wide[:, which, s * SEQ:(s + 1) * SEQ], lhs,
                                         stack[:, s * SEQ:(s + 1) * SEQ], start=True, stop=True)
                    last.then_inc(c["spread"].sem, 1)

            with pe.Fori(0, N_STATE // 2) as i:
                for k in range(2):
                    if k == 0:
                        pe.wait_ge(c["soft_a"].sem, 1)
                    spread(i, k)
                    for dc in range(NC):
                        wait(pe, c["read"], 2 * k + dc + 1, i, 4)
                        for s in range(NSEQ):
                            last = pe.matmul(acc[:, dc, s * SEQ:(s + 1) * SEQ], g.ident[:, :],
                                             term[:, k, dc, s * SEQ:(s + 1) * SEQ], start=False, stop=True,
                                             skip_group_check=True)
                        last.then_inc(c["summed"].sem, 1)
            for t in range(NT):
                for dc in range(NC):
                    if dc == 0:
                        pe.wait_ge(c["gated"].sem, NSEQ * NC)
                    last = pe.transpose(wide[:, t // 4, (t % 4) * H + dc * P:(t % 4) * H + (dc + 1) * P],
                                        state[:, 0, dc, t * P:(t + 1) * P], g.ident[:, :])
                last.then_inc(c["turned"].sem, 1)

        @block.scalar
        def _(act):
            for s in range(NSEQ):
                act.wait_ge(c["projected"].sem, s + 1)
                act.activation(rows[:, s * SEQ:(s + 1) * SEQ], acc[0:XROWS, 0, s * SEQ:(s + 1) * SEQ],
                               ACT.Copy).then_inc(c["rows"].sem, 1)
            act.wait_ge(c["loaded"].sem, 64)
            for dc in range(NC):
                act.wait_ge(c["dt"].sem, 2 * dc + 2)
                last = act.activation(z[:, dc, :], wide[:, dc, :], ACT.Identity, bias=bias[:, dc:dc + 1])
            last.then_inc(c["soft_a"].sem, 1)
            act.wait_ge(c["soft_a"].sem, 1)
            act.activation(c1[:, :, :], z[:, :, :], ACT.Abs).then_inc(c["soft_a"].sem, 1)
            act.activation(nega[:, :, :], alog, ACT.Exp).then_inc(c["soft_a"].sem, 1)
            act.wait_ge(c["soft_a"].sem, 3)
            act.activation(e[:, :, :], c1[:, :, :], ACT.Exp, scale=-1.0).then_inc(c["soft_a"].sem, 1)
            act.wait_ge(c["soft_a"].sem, 4)
            act.activation(lg[:, :, :], e[:, :, :], ACT.Ln, bias=g.one[:, 0:1]).then_inc(c["soft_a"].sem, 1)
            act.wait_ge(c["ready"].sem, 1)
            act.sem_inc(c["copied"].sem, c["copied"].prime)
            with act.Fori(0, N_STATE // 2) as i:
                for k in range(2):
                    for dc in range(NC):
                        wait(act, c["state"], 2 * k + dc - 3, i, 4)
                        act.activation(decay[:, k, dc, :], delta[:, dc, :], ACT.Exp,
                                       scale=nega[:, dc, bass.ds(2 * i + k, 1)]).then_inc(c["decay"].sem, 1)
                    for which, to in enumerate((bs, cs)):
                        wait(act, c["spread"], 2 * k + which + 1, i, 4)
                        if which == 0:
                            wait(act, c["state"], 2 * k - 2, i, 4)
                        else:
                            wait(act, c["read"], 2 * k - 2, i, 4)
                        act.activation(to[:, k, :], wide[:, which, :], ACT.Copy).then_inc(c["copied"].sem, 1)

        @block.vector
        def _(dve):
            n = [0]

            def link(op):
                n[0] += 1
                op.then_inc(c["soft_v"].sem, 1)
                dve.wait_ge(c["soft_v"].sem, n[0])

            A3 = 3 * HALF
            dve.wait_ge(c["rows"].sem, 2)
            link(dve.tensor_copy(part[:, :], rows[0:A3, :]))
            dve.tensor_copy(stack[0:HALF, :], part[0:HALF, :])
            link(dve.tensor_tensor(rest[:, :], rows[0:A3, :], part[:, :], ALU.subtract))
            link(dve.tensor_copy(part[:, :], rest[:, :]))
            dve.tensor_copy(stack[HALF:2 * HALF, :], part[HALF:2 * HALF, :])
            link(dve.tensor_tensor(rest[:, :], rest[:, :], part[:, :], ALU.subtract))
            dve.tensor_copy(stack[2 * HALF:A3, :], rest[2 * HALF:A3, :]).then_inc(c["split"].sem, 1)
            dve.wait_ge(c["soft_a"].sem, 5)
            link(dve.tensor_scalar(nega[:, :, :], nega[:, :, :], -1.0, None, ALU.mult))
            link(dve.tensor_scalar(r1[:, :, :], e[:, :, :], 1.0, None, ALU.add))
            link(dve.tensor_scalar(c1[:, :, :], r1[:, :, :], 1.0, None, ALU.subtract))
            link(dve.tensor_tensor(c1[:, :, :], e[:, :, :], c1[:, :, :], ALU.subtract))
            link(dve.reciprocal(r1[:, :, :], r1[:, :, :]))
            link(dve.tensor_tensor(c1[:, :, :], c1[:, :, :], r1[:, :, :], ALU.mult))
            link(dve.tensor_tensor(c1[:, :, :], c1[:, :, :], lg[:, :, :], ALU.add))
            link(dve.scalar_tensor_tensor(delta[:, :, :].rearrange("p c t -> p (c t)"), z[:, :, :].rearrange("p c t -> p (c t)"),
                                          0.0, c1[:, :, :].rearrange("p c t -> p (c t)"), ALU.max, ALU.add))
            dve.tensor_tensor(du[:, :, :], delta[:, :, :], g.xt[:, :, :], ALU.mult).then_inc(c["ready"].sem, 1)
            dve.wait_ge(c["ready"].sem, 1)
            dve.sem_inc(c["state"].sem, c["state"].prime)
            with dve.Fori(0, N_STATE // 2) as i:
                for k in range(2):
                    wait(dve, c["decay"], 2 * (k + 1), i, 4)
                    dve.memset(decay[:, k, :, 0:T:SEQ], 0.0).then_inc(c["zeroed"].sem, 1)
                    wait(dve, c["copied"], 2 * k + 1, i, 4)
                    for dc in range(NC):
                        wait(dve, c["summed"], 2 * k + dc - 3, i, 4)
                        dve.tensor_tensor(drive[:, k, dc, :], du[:, dc, :], bs[:, k, :], ALU.mult) \
                            .then_inc(c["driven"].sem, 1)
                    wait(dve, c["zeroed"], k + 1, i, 2)
                    for dc in range(NC):
                        wait(dve, c["driven"], 2 * k + dc + 1, i, 4)
                        wait(dve, c["read"], 2 * k + dc - 3, i, 4)
                        dve.tensor_tensor_scan(state[:, k, dc, :], decay[:, k, dc, :], drive[:, k, dc, :], 0.0,
                                               ALU.mult, ALU.add).then_inc(c["state"].sem, 1)
            for dc in range(NC):
                wait(dve, c["summed"], 2 * N_STATE - NC + dc + 1)
                wait(dve, c["read"], 2 * N_STATE)
                for s in range(NSEQ):
                    cut = slice(s * SEQ, (s + 1) * SEQ)
                    dve.scalar_tensor_tensor(state[:, 0, dc, cut], g.xt[:, dc, cut], dvec[:, dc:dc + 1],
                                             acc[:, dc, cut], ALU.mult, ALU.add).then_inc(c["gated"].sem, 1)
            for t in range(0, NT, 2):
                dve.wait_ge(c["turned"].sem, t + 2)
                x2 = g.x[:, t:t + 2, :].rearrange("p a h -> p (a h)")
                dve.tensor_tensor(x2, x2, wide[:, t // 4, (t % 4) * H:(t % 4 + 2) * H], ALU.add)
    finish(nc, c.values())


def mixture(nc, g, d):
    c = {n: Count(nc, n, p) for n, p in (
        ("loaded", 0), ("gu_even", 0), ("gu_odd", 0), ("d_even", 0), ("d_odd", 0), ("logits", 0), ("gates", 0),
        ("own", 0), ("gu_high", 2), ("gu_low", 2), ("d_high", 2), ("d_low", 2),
        ("inner", 4), ("silu", 4), ("prod", 4), ("high", 4), ("low", 4), ("down", 4), ("added", 4))}
    gu_full, d_full = (c["gu_even"], c["gu_odd"]), (c["d_even"], c["d_odd"])
    GU = 2 * NC * FF0
    LAST = NU0 // 2 - 1
    with (
        sbuf(nc, "router", [P, NC, NE0], F32) as router,
        sbuf(nc, "gu", [P, 2, GU], F32) as gu,
        sbuf(nc, "gu_hi", [P, 2, GU], F32R) as gu_hi,
        sbuf(nc, "gu_lo", [P, 2, GU], F32R) as gu_lo,
        sbuf(nc, "wd", [P, 2, H], F32) as wd,
        sbuf(nc, "wd_hi", [P, 2, H], F32R) as wd_hi,
        sbuf(nc, "wd_lo", [P, 2, H], F32R) as wd_lo,
        sbuf(nc, "score", [P, NT, NE0], F32) as score,
        sbuf(nc, "left", [P, NT, NE0], F32) as left,
        sbuf(nc, "top", [P, NT, 8], F32) as top,
        sbuf(nc, "total", [P, NT], F32) as total,
        sbuf(nc, "weight", [P, NT, NU0], F32) as weight,
        sbuf(nc, "silu", [P, NSEQ, SEQ], F32) as silu,
        sbuf(nc, "inner", [P, NSEQ, SEQ], F32) as inner,
        sbuf(nc, "inner_hi", [P, 2, T], F32R) as inner_hi,
        sbuf(nc, "inner_lo", [P, 2, T], F32R) as inner_lo,
        psum(nc, "gate", [P, NSEQ, SEQ], F32) as gate,
        psum(nc, "up", [P, NSEQ, SEQ], F32) as up,
        psum(nc, "outs", [P, NT, H], F32) as outs,
        nc.Block() as block,
    ):
        @block.sync
        def _(sp):
            sp.dma_start(router[:, :, :], d["router0"]).then_inc(c["loaded"].sem, 16)
            with sp.Fori(0, NU0 // 2) as i:
                for k in range(2):
                    src = d["w0"][bass.ds(2 * i + k, 1)].rearrange("o p n -> p (o n)")
                    wait(sp, c["gu_low"], k - 1, i, 2)
                    sp.dma_start(gu[:, k, :], src[:, 0:GU]).then_inc(gu_full[k].sem, 16)
                    wait(sp, c["d_low"], k - 1, i, 2)
                    sp.dma_start(wd[:, k, :], src[:, GU:]).then_inc(d_full[k].sem, 16)

        @block.tensor
        def _(pe):
            pe.sem_inc(c["down"].sem, c["down"].prime)
            pe.sem_inc(c["inner"].sem, c["inner"].prime)
            pe.wait_ge(c["loaded"].sem, 16)
            for t in range(NT):
                for kc in range(NC):
                    last = pe.matmul(outs[:, 0, t * NE0:(t + 1) * NE0], g.xt[:, kc, t * P:(t + 1) * P],
                                     router[:, kc, :], start=(kc == 0), stop=(kc == NC - 1))
            last.then_inc(c["logits"].sem, 1)

            def gate_up(i, n):
                k = n % 2
                wait(pe, c["gu_low"], n + 1, i, 2)
                for s in range(NSEQ):
                    wait(pe, c["prod"], 2 * n - 1 + s, i, 4)
                    cut = slice(s * SEQ, (s + 1) * SEQ)
                    for which, to in enumerate((gate, up)):
                        for kc in range(NC):
                            col = slice((which * NC + kc) * FF0, (which * NC + kc + 1) * FF0)
                            pe.matmul(to[:, s, :], gu_hi[:, k, col], g.xh[:, kc, cut], start=(kc == 0), stop=False)
                            pe.matmul(to[:, s, :], gu_hi[:, k, col], g.xl[:, kc, cut], start=False, stop=False)
                            last = pe.matmul(to[:, s, :], gu_lo[:, k, col], g.xh[:, kc, cut],
                                             start=False, stop=(kc == NC - 1))
                    last.then_inc(c["inner"].sem, 1)

            def down(i, n):
                k = n % 2
                wait(pe, c["d_low"], n + 1, i, 2)
                for t in range(NT):
                    if t % 4 == 0:
                        wait(pe, c["low"], 2 * n + t // 4 + 1, i, 4)
                    if t % 2 == 0:
                        wait(pe, c["added"], 4 * n - 3 + t // 2, i, 8)
                    cut = slice(t * P, (t + 1) * P)
                    pe.matmul(outs[:, t, :], inner_hi[:, k, cut], wd_hi[:, k, :], start=True, stop=False)
                    pe.matmul(outs[:, t, :], inner_hi[:, k, cut], wd_lo[:, k, :], start=False, stop=False)
                    last = pe.matmul(outs[:, t, :], inner_lo[:, k, cut], wd_hi[:, k, :], start=False, stop=True)
                    if t % 4 == 3:
                        last.then_inc(c["down"].sem, 1)

            gate_up(0, 0)
            pe.wait_ge(c["gates"].sem, 1)
            with pe.Fori(0, LAST) as i:
                for n in range(2):
                    gate_up(i, n + 1)
                    down(i, n)
            gate_up(LAST, 1)
            down(LAST, 0)
            down(LAST, 1)

        @block.scalar
        def _(act):
            for n in ("silu", "high", "gu_high", "d_high"):
                act.sem_inc(c[n].sem, c[n].prime)

            def split_gu(i, n):
                wait(act, gu_full[n % 2], 16 * (n // 2) + 16, i, 16)
                wait(act, c["inner"], 2 * n - 2, i, 4)
                act.activation(gu_hi[:, n % 2, :], gu[:, n % 2, :], ACT.Copy).then_inc(c["gu_high"].sem, 1)

            def split_d(i, n):
                wait(act, d_full[n % 2], 16 * (n // 2) + 16, i, 16)
                wait(act, c["down"], 2 * n - 2, i, 4)
                act.activation(wd_hi[:, n % 2, :], wd[:, n % 2, :], ACT.Copy).then_inc(c["d_high"].sem, 1)

            def inner_values(i, n):
                for s in range(NSEQ):
                    wait(act, c["inner"], 2 * n + s + 1, i, 4)
                    wait(act, c["prod"], 2 * n - 1 + s, i, 4)
                    act.activation(silu[:, s, :], gate[:, s, :], ACT.Silu).then_inc(c["silu"].sem, 1)
                for s in range(NSEQ):
                    wait(act, c["prod"], 2 * n + s + 1, i, 4)
                    wait(act, c["down"], 2 * n - 3 + s, i, 4)
                    act.activation(inner_hi[:, n % 2, s * SEQ:(s + 1) * SEQ], inner[:, s, :], ACT.Copy) \
                        .then_inc(c["high"].sem, 1)

            split_gu(0, 0)
            act.wait_ge(c["logits"].sem, 1)
            act.activation(score[:, :, :].rearrange("p t e -> p (t e)"), outs[:, 0, 0:NT * NE0],
                           ACT.Sigmoid).then_inc(c["gates"].sem, 1)
            split_gu(0, 1)
            split_d(0, 0)
            inner_values(0, 0)
            with act.Fori(0, LAST) as i:
                for n in range(2):
                    split_gu(i, n + 2)
                    split_d(i, n + 1)
                    inner_values(i, n + 1)
            split_d(LAST, 1)
            inner_values(LAST, 1)

        @block.gpsimd
        def _(pool):
            pool.sem_inc(c["gu_low"].sem, c["gu_low"].prime)
            pool.sem_inc(c["d_low"].sem, c["d_low"].prime)

            def split_gu(i, n):
                wait(pool, c["gu_high"], n + 1, i, 2)
                pool.tensor_tensor(gu_lo[:, n % 2, :], gu[:, n % 2, :], gu_hi[:, n % 2, :].bitcast(F32),
                                   ALU.subtract).then_inc(c["gu_low"].sem, 1)

            def split_d(i, n):
                wait(pool, c["d_high"], n + 1, i, 2)
                pool.tensor_tensor(wd_lo[:, n % 2, :], wd[:, n % 2, :], wd_hi[:, n % 2, :].bitcast(F32),
                                   ALU.subtract).then_inc(c["d_low"].sem, 1)

            split_gu(0, 0)
            split_gu(0, 1)
            split_d(0, 0)
            with pool.Fori(0, LAST) as i:
                for n in range(2):
                    split_gu(i, n + 2)
                    split_d(i, n + 1)
            split_d(LAST, 1)

        @block.vector
        def _(dve):
            for n in ("prod", "low", "added"):
                dve.sem_inc(c[n].sem, c[n].prime)

            def inner_values(i, n):
                for s in range(NSEQ):
                    wait(dve, c["silu"], 2 * n + s + 1, i, 4)
                    wait(dve, c["low"], 2 * n - 1 + s, i, 4)
                    dve.tensor_tensor(inner[:, s, :], silu[:, s, :], up[:, s, :], ALU.mult) \
                        .then_inc(c["prod"].sem, 1)

            def inner_low(i, n, s):
                wait(dve, c["high"], 2 * n + s + 1, i, 4)
                cut = slice(s * SEQ, (s + 1) * SEQ)
                dve.tensor_tensor(inner_lo[:, n % 2, cut], inner[:, s, :], inner_hi[:, n % 2, cut].bitcast(F32),
                                  ALU.subtract).then_inc(c["low"].sem, 1)

            def add(i, n, half):
                for t in range(4 * half, 4 * half + 4):
                    if t % 4 == 0:
                        wait(dve, c["down"], 2 * n + t // 4 + 1, i, 4)
                    if t % 2 == 0:
                        wait(dve, c["added"], 4 * n - 3 + t // 2, i, 8)
                    e = bass.ds(2 * i + n, 1)
                    last = dve.scalar_tensor_tensor(g.x[:, t, :], outs[:, t, :], weight[:, t, e],
                                                    g.x[:, t, :], ALU.mult, ALU.add)
                    if t % 2 == 1:
                        last.then_inc(c["added"].sem, 1)

            own = [0]

            def link(op):
                own[0] += 1
                op.then_inc(c["own"].sem, 1)
                dve.wait_ge(c["own"].sem, own[0])

            dve.memset(weight[:, :, NE0:], 1.0)
            dve.wait_ge(c["gates"].sem, 1)
            for t in range(NT):
                op = dve.max(top[:, t, :], score[:, t, :])
                if t == NT - 1:
                    link(op)
            for t in range(NT):
                op = dve.match_replace(left[:, t, :], top[:, t, :], score[:, t, :], -1.0)
                if t == NT - 1:
                    link(op)
            link(dve.scalar_tensor_tensor(left[:, :, :], left[:, :, :], 0.0, score[:, :, :], ALU.is_lt, ALU.mult))
            link(dve.reduce_sum(total[:, :], left[:, :, :], axis=AX.X))
            link(dve.tensor_scalar(total[:, :], total[:, :], 1e-6, None, ALU.add))
            link(dve.reciprocal(total[:, :], total[:, :]))
            link(dve.tensor_scalar(total[:, :], total[:, :], ROUTED_SCALE, None, ALU.mult))
            link(dve.tensor_tensor(weight[:, :, 0:NE0], left[:, :, :],
                                   total[:, :].unsqueeze(2).broadcast_to([P, NT, NE0]), ALU.mult))
            inner_values(0, 0)
            inner_low(0, 0, 0)
            inner_low(0, 0, 1)
            with dve.Fori(0, LAST) as i:
                for n in range(2):
                    inner_values(i, n + 1)
                    inner_low(i, n + 1, 0)
                    inner_low(i, n + 1, 1)
                    add(i, n, 0)
                    add(i, n, 1)
            inner_values(LAST, 1)
            inner_low(LAST, 1, 0)
            inner_low(LAST, 1, 1)
            for n in range(2):
                add(LAST, n, 0)
                add(LAST, n, 1)
    finish(nc, c.values())


def attention(nc, g, d, name, kv_every, window):
    UNITS = HEADS * NSEQ
    U = 4 if kv_every == 4 else 2
    BODY = U * NSEQ
    LOOPS = HEADS // U - 1
    KVSLOTS = 2 if kv_every == 1 else 1
    NQ = SEQ // P
    groups = [[0, 1], [2, 3]] if window else [[0, 1], [2], [3]]
    NG = len(groups)
    keys = [list(range(max(0, t - 1) if window else 0, t + 1)) for t in range(NQ)]
    cols, psum_col, width = [], [], []
    for gr in groups:
        at = 0
        for t in gr:
            cols.append(sum(len(keys[s]) for s in range(t)) * P)
            psum_col.append(at)
            at += len(keys[t]) * P
        width.append(at)
    WIDTH = sum(width)

    def has_kv(m):
        return (m // NSEQ) % kv_every == 0

    def before(m, kind):
        if m < 0 and kv_every < HEADS:
            return before(m + BODY, kind) - before(BODY, kind)
        if m < 0:
            return m + NSEQ if kind == "rope" else NSEQ
        kv = sum(has_kv(j) for j in range(m))
        return kv if kind == "v" else m + kv

    per_rope = BODY if kv_every == HEADS else before(BODY, "rope")
    per_v = 0 if kv_every == HEADS else before(BODY, "v")

    c = {n: Count(nc, n, p) for n, p in (
        ("loaded", 0), ("wo", 0), ("wq_even", 0), ("wq_odd", 0), ("kv_even", 0), ("kv_odd", 0), ("ready", 0), ("turns", 0),
        ("wq_high", 2), ("wq_low", 2), ("wk_high", 2), ("wk_low", 2),
        ("proj", 8), ("swapped", 4), ("cosed", 6), ("sined", 4), ("rotated", 6),
        ("vproj", 4), ("vkept", 4), ("scores", 8), ("peak", 0), ("expd", 8), ("recip", 0), ("normed", 0),
        ("turned", 8), ("pt_v", 8), ("pt_a", 8), ("values", 6), ("okept", 4), ("out", 0))}
    wq_full, kv_full = (c["wq_even"], c["wq_odd"]), (c["kv_even"], c["kv_odd"])
    VBANK = window

    with ExitStack() as ctx:
        def sb(name, shape, dtype):
            return ctx.enter_context(sbuf(nc, name, shape, dtype))

        wo = sb("wo", [P, HEADS, H], F32)
        wq = sb("wq", [P, 2, NC, P], F32)
        wkv = sb("wkv", [P, KVSLOTS, 2, NC, P], F32)
        wq_hi = sb("wq_hi", [P, 2, NC, P], F32R)
        wq_lo = sb("wq_lo", [P, 2, NC, P], F32R)
        wk_hi = sb("wk_hi", [P, KVSLOTS, NC, P], F32R)
        wk_lo = sb("wk_lo", [P, KVSLOTS, NC, P], F32R)
        ropes = sb("ropes", [P, 2, 2, SEQ], F32)
        mask1 = sb("mask1", [P, 2, P], F32)
        mask = sb("mask", [P, 2, P], BF16)
        q = sb("q", [P, NSEQ, SEQ], F32)
        k = sb("k", [P, NSEQ, SEQ], F32)
        v = sb("v", [P, NSEQ, NQ, P], F32)
        swap = sb("swap", [P, 2, SEQ], F32)
        cosed = sb("cosed", [P, 2, SEQ], F32)
        prob = sb("prob", [P, NSEQ, WIDTH], F32)
        pt = sb("pt", [P, NSEQ, NQ, SEQ], F32)
        peak = sb("peak", [P, NSEQ, NQ], F32)
        sums = sb("sums", [P, NSEQ, NQ], F32)
        recip = sb("recip", [P, NSEQ, NQ], F32)
        o = sb("o", [P, HEADS, T], F32)
        banks = ctx.enter_context(psum(nc, "banks", [P, 8, SEQ], F32))
        block = ctx.enter_context(nc.Block())

        s_bank = [banks[:, j, :] for j in range(NG)]
        t_bank = [banks[:, 3 + j, :] for j in range(2)]
        p_bank = [banks[:, 5 + j, :] for j in range(2)]
        o_bank = banks[:, 7, :]
        v_bank = banks[:, 2, :] if VBANK else o_bank
        mover = ["v", "a"] if window else ["v", "v", "a"]

        def turned_by(n, gi):
            own = [j for j in range(NG) if mover[j] == mover[gi]]
            return c["pt_" + mover[gi]], n * len(own) + own.index(gi) + 1, BODY * len(own)

        @block.sync
        def _(sp):
            sp.dma_start(ropes[:, 0], d["rope_q"]).then_inc(c["loaded"].sem, 16)
            sp.dma_start(ropes[:, 1], d["rope_k"]).then_inc(c["loaded"].sem, 16)
            sp.dma_start(mask1[:, :, :], d["mask"].rearrange("p (a n) -> p a n", a=2)).then_inc(c["loaded"].sem, 16)

            def load(i, h):
                at = bass.ds(i * U + h, 1) if not isinstance(i, int) else slice(i * U + h, i * U + h + 1)
                wait(sp, c["wq_low"], h - 1, i, U)
                sp.dma_start(wq[:, h % 2], d[name + "_q"][at].rearrange("o p c n -> p (o c) n")) \
                    .then_inc(wq_full[h % 2].sem, 16)
                if has_kv(NSEQ * h) and kv_every < HEADS:
                    kvh = h // kv_every
                    at = bass.ds(i * (U // kv_every) + kvh, 1)
                    wait(sp, c["vproj"], NSEQ * (kvh + 1 - KVSLOTS), i, per_v)
                    sp.dma_start(wkv[:, kvh % KVSLOTS].rearrange("p a c n -> p (a c) n"),
                                 d[name + "_kv"][at].rearrange("o p a c n -> p (o a c) n")) \
                        .then_inc(kv_full[kvh % KVSLOTS].sem, 16)

            if kv_every == HEADS:
                sp.dma_start(wkv[:, 0].rearrange("p a c n -> p (a c) n"),
                             d[name + "_kv"][0:1].rearrange("o p a c n -> p (o a c) n")).then_inc(kv_full[0].sem, 16)
            with sp.Fori(0, HEADS // U) as i:
                for h in range(U):
                    load(i, h)
            sp.dma_start(wo[:, :, :], d[name + "_o"]).then_inc(c["wo"].sem, 16)

        @block.tensor
        def _(pe):
            for n in ("proj", "vproj", "scores", "turned", "values"):
                pe.sem_inc(c[n].sem, c[n].prime)
            pe.wait_ge(c["ready"].sem, 1)

            def rope_unit(i, m, which):
                s = m % NSEQ
                r = before(m, "rope") + which
                wait(pe, c["cosed"], r - 1, i, per_rope)
                if which == 0:
                    h = m // NSEQ
                    wait(pe, c["wq_low"], h + 1, i, U)
                    hi, lo = wq_hi[:, h % 2], wq_lo[:, h % 2]
                else:
                    kvh = m // NSEQ // kv_every
                    wait(pe, c["wk_low"], kvh + 1, i, U // kv_every)
                    hi, lo = wk_hi[:, kvh % KVSLOTS], wk_lo[:, kvh % KVSLOTS]
                cut = slice(s * SEQ, (s + 1) * SEQ)
                for kc in range(NC):
                    pe.matmul(p_bank[r % 2], hi[:, kc, :], g.xh[:, kc, cut], start=(kc == 0), stop=False)
                    pe.matmul(p_bank[r % 2], hi[:, kc, :], g.xl[:, kc, cut], start=False, stop=False)
                    last = pe.matmul(p_bank[r % 2], lo[:, kc, :], g.xh[:, kc, cut], start=False, stop=(kc == NC - 1))
                last.then_inc(c["proj"].sem, 1)

            def value_unit(i, m):
                s = m % NSEQ
                kvh = m // NSEQ // kv_every
                wait(pe, kv_full[kvh % KVSLOTS], 16 * (kvh // KVSLOTS) + 16, i, 16 * (U // kv_every) // KVSLOTS)
                wait(pe, c["vkept"], before(m, "v"), i, per_v)
                if not VBANK:
                    wait(pe, c["okept"], m - 1, i, BODY)
                for t in range(NQ):
                    for kc in range(NC):
                        last = pe.matmul(v_bank[:, t * P:(t + 1) * P],
                                         g.xt[:, kc, s * SEQ + t * P:s * SEQ + (t + 1) * P],
                                         wkv[:, kvh % KVSLOTS, 1, kc, :], start=(kc == 0), stop=(kc == NC - 1))
                last.then_inc(c["vproj"].sem, 1)

            def score(i, m, gi):
                s = m % NSEQ
                if gi == 0:
                    r = before(m + 1, "rope") if m >= 0 else 0
                    wait(pe, c["rotated"], r, i, per_rope)
                wait(pe, c["expd"], NG * (m - 1) + gi + 1, i, NG * BODY)
                for t in groups[gi]:
                    out = s_bank[gi][:, psum_col[t]:psum_col[t] + len(keys[t]) * P]
                    pe.matmul(out, q[:, s, t * P:(t + 1) * P],
                              k[:, s, keys[t][0] * P:(keys[t][-1] + 1) * P], start=True, stop=False)
                    lo = 0 if window and len(keys[t]) == 2 else 1
                    last = pe.matmul(out[:, (len(keys[t]) - 2 + lo) * P:], g.identb[:, :],
                                     mask[:, lo:, :].rearrange("p a n -> p (a n)"), start=False, stop=True)
                last.then_inc(c["scores"].sem, 1)

            def turn(i, n, gi):
                s = n % NSEQ
                wait(pe, c["normed"], NG * n + gi + 1, i, NG * BODY)
                j = NG * n + gi - 2
                cnt, at, per = turned_by(j // NG, j % NG)
                wait(pe, cnt, at, i, per)
                at = 0
                for t in groups[gi]:
                    for x in range(len(keys[t])):
                        last = pe.transpose(t_bank[(NG * n + gi) % 2][:, at:at + P],
                                            prob[:, s, cols[t] + x * P:cols[t] + (x + 1) * P], g.ident[:, :])
                        at += P
                last.then_inc(c["turned"].sem, 1)

            def sum_values(i, n):
                s = n % NSEQ
                for e in ("v", "a"):
                    own = [j for j in range(NG) if mover[j] == e]
                    wait(pe, c["pt_" + e], (n + 1) * len(own), i, BODY * len(own))
                wait(pe, c["okept"], n, i, BODY)
                wait(pe, c["vkept"], before(n + 1, "v"), i, per_v)
                if not VBANK:
                    m = min(n + 2, UNITS - i * BODY) if isinstance(i, int) else n + 2
                    wait(pe, c["vkept"], before(m, "v"), i, per_v)
                order = [0, 2, 1, 3] if window else list(range(NQ))
                for j, x in enumerate(order):
                    to = min(x + 2, NQ) * P if window else SEQ
                    last = pe.matmul(o_bank[:, x * P:to], v[:, s, x, :], pt[:, s, x, x * P:to],
                                     start=(j == 0), stop=(j == NQ - 1))
                last.then_inc(c["values"].sem, 1)

            def slot(i, n):
                static = isinstance(i, int)
                live = lambda m: not static or 0 <= i * BODY + m < UNITS
                kv = lambda m: has_kv(m) and (kv_every < HEADS or static and i * BODY + m < NSEQ)
                for gi in range(NG):
                    if live(n + 1):
                        score(i, n + 1, gi)
                    if live(n):
                        turn(i, n, gi)
                if live(n + 3):
                    rope_unit(i, n + 3, 0)
                    if kv(n + 3):
                        rope_unit(i, n + 3, 1)
                if live(n):
                    sum_values(i, n)
                if live(n + 2) and kv(n + 2):
                    value_unit(i, n + 2)

            for n in range(-3, 0):
                slot(0, n)
            with pe.Fori(0, LOOPS) as i:
                for n in range(BODY):
                    slot(i, n)
            for n in range(BODY):
                slot(LOOPS, n)
            pe.wait_ge(c["wo"].sem, 16)
            wait(pe, c["okept"], UNITS)
            for t in range(NT):
                for h in range(HEADS):
                    last = pe.matmul(banks[:, t // 2, (t % 2) * H:(t % 2 + 1) * H], o[:, h, t * P:(t + 1) * P],
                                     wo[:, h, :], start=(h == 0), stop=(h == HEADS - 1))
                last.then_inc(c["out"].sem, 1)

        def move_turned(eng, i, n, gi):
            s = n % NSEQ
            wait(eng, c["turned"], NG * n + gi + 1, i, NG * BODY)
            wait(eng, c["values"], n - 1, i, BODY)
            at = 0
            for t in groups[gi]:
                m = len(keys[t])
                src = t_bank[(NG * n + gi) % 2][:, at:at + m * P].rearrange("p (k q) -> p k q", q=P)
                dst = pt[:, s, keys[t][0]:keys[t][-1] + 1, t * P:(t + 1) * P]
                if mover[gi] == "v":
                    last = eng.tensor_copy(dst, src)
                else:
                    last = eng.activation(dst, src, ACT.Copy)
                at += m * P
            last.then_inc(c["pt_" + mover[gi]].sem, 1)

        @block.scalar
        def _(act):
            for n in ("swapped", "expd", "pt_a", "okept", "vkept", "wq_high", "wk_high"):
                act.sem_inc(c[n].sem, c[n].prime)

            def weights_high(i, m):
                h = m // NSEQ
                wait(act, wq_full[h % 2], 16 * (h // 2) + 16, i, 16 * U // 2)
                wait(act, c["proj"], before(m - 3, "rope") + 1, i, per_rope)
                act.activation(wq_hi[:, h % 2], wq[:, h % 2], ACT.Copy).then_inc(c["wq_high"].sem, 1)
                if has_kv(m) and (kv_every < HEADS or m == 0):
                    kvh = h // kv_every
                    wait(act, kv_full[kvh % KVSLOTS], 16 * (kvh // KVSLOTS) + 16, i, 16 * (U // kv_every) // KVSLOTS)
                    wait(act, c["proj"], before((kvh - KVSLOTS) * kv_every * NSEQ + 1, "rope") + 2, i, per_rope)
                    act.activation(wk_hi[:, kvh % KVSLOTS], wkv[:, kvh % KVSLOTS, 0], ACT.Copy) \
                        .then_inc(c["wk_high"].sem, 1)

            def swap_halves(i, m, which):
                r = before(m, "rope") + which
                wait(act, c["proj"], r + 1, i, per_rope)
                wait(act, c["rotated"], r - 1, i, per_rope)
                act.activation(swap[0:P // 2, r % 2, :], p_bank[r % 2][P // 2:P, :], ACT.Copy)
                act.activation(swap[P // 2:P, r % 2, :], p_bank[r % 2][0:P // 2, :], ACT.Copy) \
                    .then_inc(c["swapped"].sem, 1)

            def exps(i, m, gi):
                s = m % NSEQ
                wait(act, c["peak"], NG * m + gi + 1, i, NG * BODY)
                wait(act, c["turned"], NG * (m - 2) + gi + 1, i, NG * BODY)
                for t in groups[gi]:
                    n = len(keys[t]) * P
                    last = act.activation(prob[:, s, cols[t]:cols[t] + n], s_bank[gi][:, psum_col[t]:psum_col[t] + n],
                                          ACT.Exp, bias=peak[:, s, t:t + 1], accum_out=sums[:, s, t:t + 1])
                last.then_inc(c["expd"].sem, 1)

            def slot(i, n):
                static = isinstance(i, int)
                live = lambda m: not static or 0 <= i * BODY + m < UNITS
                kv = lambda m: has_kv(m) and (kv_every < HEADS or static and i * BODY + m < NSEQ)
                if n % NSEQ == 0 and live(n + 4):
                    weights_high(i, n + 4)
                for gi in range(NG):
                    if gi == NG - 1 and live(n):
                        move_turned(act, i, n, NG - 1)
                    if live(n + 1):
                        exps(i, n + 1, gi)
                if live(n + 3):
                    swap_halves(i, n + 3, 0)
                    if kv(n + 3):
                        swap_halves(i, n + 3, 1)
                if live(n):
                    wait(act, c["values"], n + 1, i, BODY)
                    h = n // NSEQ
                    s = n % NSEQ
                    at = bass.ds(i * U + h, 1) if not static else slice(i * U + h, i * U + h + 1)
                    act.activation(o[:, at, s * SEQ:(s + 1) * SEQ].rearrange("p a n -> p (a n)"), o_bank,
                                   ACT.Copy).then_inc(c["okept"].sem, 1)
                if live(n + 2) and kv(n + 2):
                    m = n + 2
                    wait(act, c["vproj"], before(m, "v") + 1, i, per_v)
                    wait(act, c["values"], m - 1, i, BODY)
                    act.activation(v[:, m % NSEQ].rearrange("p t n -> p (t n)"), v_bank, ACT.Copy) \
                        .then_inc(c["vkept"].sem, 1)

            weights_high(0, 0)
            for n in range(-3, 0):
                slot(0, n)
            with act.Fori(0, LOOPS) as i:
                for n in range(BODY):
                    slot(i, n)
            for n in range(BODY):
                slot(LOOPS, n)

        @block.vector
        def _(dve):
            dve.wait_ge(c["loaded"].sem, 48)
            dve.tensor_scalar(mask[:, :, :], mask1[:, :, :], NEG, None, ALU.mult) \
                .then_inc(c["ready"].sem, 1)
            for n in ("cosed", "sined", "pt_v"):
                dve.sem_inc(c[n].sem, c[n].prime)

            def peaks(i, m, gi):
                s = m % NSEQ
                wait(dve, c["scores"], NG * m + gi + 1, i, NG * BODY)
                wait(dve, c["expd"], NG * (m - 2) + gi + 1, i, NG * BODY)
                for t in groups[gi]:
                    last = dve.reduce_max(peak[:, s, t:t + 1],
                                          s_bank[gi][:, psum_col[t]:psum_col[t] + len(keys[t]) * P],
                                          axis=AX.X, negate=True)
                last.then_inc(c["peak"].sem, 1)

            def recips(i, m, gi):
                s = m % NSEQ
                wait(dve, c["expd"], NG * m + gi + 1, i, NG * BODY)
                cut = slice(groups[gi][0], groups[gi][-1] + 1)
                dve.reciprocal(recip[:, s, cut], sums[:, s, cut]).then_inc(c["recip"].sem, 1)

            def rotate(i, m, which):
                r = before(m, "rope") + which
                wait(dve, c["swapped"], r + 1, i, per_rope)
                wait(dve, c["rotated"], r - 1, i, per_rope)
                dve.tensor_tensor(cosed[:, r % 2, :], p_bank[r % 2], ropes[:, which, 0, :], ALU.mult) \
                    .then_inc(c["cosed"].sem, 1)
                dve.tensor_tensor(swap[:, r % 2, :], swap[:, r % 2, :], ropes[:, which, 1, :], ALU.mult) \
                    .then_inc(c["sined"].sem, 1)

            def slot(i, n):
                static = isinstance(i, int)
                live = lambda m: not static or 0 <= i * BODY + m < UNITS
                kv = lambda m: has_kv(m) and (kv_every < HEADS or static and i * BODY + m < NSEQ)
                for gi in range(NG):
                    if live(n + 1):
                        peaks(i, n + 1, gi)
                        if gi:
                            recips(i, n + 1, gi - 1)
                    if live(n) and mover[gi] == "v":
                        move_turned(dve, i, n, gi)
                if live(n + 1):
                    recips(i, n + 1, NG - 1)
                if live(n + 3):
                    rotate(i, n + 3, 0)
                    if kv(n + 3):
                        rotate(i, n + 3, 1)

            for n in range(-3, 0):
                slot(0, n)
            with dve.Fori(0, LOOPS) as i:
                for n in range(BODY):
                    slot(i, n)
            for n in range(BODY):
                slot(LOOPS, n)
            for t in range(0, NT, 2):
                dve.wait_ge(c["out"].sem, t + 2)
                x2 = g.x[:, t:t + 2, :].rearrange("p a h -> p (a h)")
                dve.tensor_tensor(x2, x2, banks[:, t // 2, :], ALU.add)

        @block.gpsimd
        def _(pool):
            for n in ("rotated", "wq_low", "wk_low"):
                pool.sem_inc(c[n].sem, c[n].prime)

            def weights_low(i, m):
                h = m // NSEQ
                wait(pool, c["wq_high"], h + 1, i, U)
                pool.tensor_tensor(wq_lo[:, h % 2], wq[:, h % 2], wq_hi[:, h % 2].bitcast(F32), ALU.subtract) \
                    .then_inc(c["wq_low"].sem, 1)
                if has_kv(m) and (kv_every < HEADS or m == 0):
                    kvh = h // kv_every
                    k = kvh % KVSLOTS
                    wait(pool, c["wk_high"], kvh + 1, i, U // kv_every)
                    pool.tensor_tensor(wk_lo[:, k], wkv[:, k, 0], wk_hi[:, k].bitcast(F32), ALU.subtract) \
                        .then_inc(c["wk_low"].sem, 1)

            def norms(i, m, gi):
                s = m % NSEQ
                wait(pool, c["recip"], NG * m + gi + 1, i, NG * BODY)
                pool.sem_inc(c["turns"].sem, 1)
                for t in groups[gi]:
                    part = prob[:, s, cols[t]:cols[t] + len(keys[t]) * P]
                    last = pool.tensor_scalar(part, part, recip[:, s, t:t + 1], None, ALU.mult)
                last.then_inc(c["normed"].sem, 1)

            def rotated(i, m, which):
                s = m % NSEQ
                r = before(m, "rope") + which
                wait(pool, c["sined"], r + 1, i, per_rope)
                wait(pool, c["cosed"], r + 1, i, per_rope)
                wait(pool, c["scores"], NG * (m - 1), i, NG * BODY)
                pool.tensor_tensor((k if which else q)[:, s, :], cosed[:, r % 2, :], swap[:, r % 2, :], ALU.add) \
                    .then_inc(c["rotated"].sem, 1)

            def slot(i, n):
                static = isinstance(i, int)
                live = lambda m: not static or 0 <= i * BODY + m < UNITS
                kv = lambda m: has_kv(m) and (kv_every < HEADS or static and i * BODY + m < NSEQ)
                if n % NSEQ == 0 and live(n + 4):
                    weights_low(i, n + 4)
                if live(n + 1):
                    for gi in range(NG):
                        norms(i, n + 1, gi)
                if live(n + 3):
                    rotated(i, n + 3, 0)
                    if kv(n + 3):
                        rotated(i, n + 3, 1)

            weights_low(0, 0)
            for n in range(-3, 0):
                slot(0, n)
            with pool.Fori(0, LOOPS) as i:
                for n in range(BODY):
                    slot(i, n)
            for n in range(BODY):
                slot(LOOPS, n)
    finish(nc, c.values())


def capacity_mixture(nc, g, d):
    c = {n: Count(nc, n, p) for n, p in (
        ("loaded", 0), ("own_v", 0), ("logits", 0), ("shared_w", 0), ("peak", 0), ("expd", 0), ("masked", 0),
        ("places", 0), ("sparts", 0), ("routed", 0), ("sinner", 0), ("ssilu", 0), ("sprod", 0), ("based", 0),
        ("gu_even", 0), ("gu_odd", 0), ("d_even", 0), ("d_odd", 0),
        ("picked", 4), ("gathered", 4), ("buffered", 4), ("sloted", 4), ("spread0", 4), ("spread1", 4),
        ("kept0", 4), ("kept1", 4), ("inner", 4), ("silu", 4), ("acted", 4), ("turned", 4), ("moved", 4),
        ("down", 4), ("split", 4), ("summed", 4), ("chain", 0), ("parted", 0))}
    gu_full, d_full = (c["gu_even"], c["gu_odd"]), (c["d_even"], c["d_odd"])
    SENTINEL = 2.0
    BODY = 2
    LOOPS = NG1 // BODY - 1
    with ExitStack() as ctx:
        def sb(name, shape, dtype):
            return ctx.enter_context(sbuf(nc, name, shape, dtype))

        router = sb("router", [P, NC, NE1], F32)
        ranks1 = sb("ranks", [P, 2 * P], F32)
        ranks = sb("ranks_b", [P, 2 * P], BF16)
        slot1 = sb("slot1", [P, CAP], F32)
        own = sb("own", [P, GE * 3], F32)
        peak = sb("peak", [P, NT], F32)
        sums = sb("sums", [P, NT], F32)
        score = sb("score", [P, NT, NE1 + 2], F32)
        left = sb("left", [P, NT, NE1 + 2], F32)
        top = sb("top", [P, NT, 8], F32)
        maskb = sb("maskb", [P, NT, NE1], BF16)
        prior = sb("prior", [P, NT, NE1], BF16)
        place = sb("place", [P, NT, NE1], F32)
        wrest = sb("wrest", [P, NT, NE1], F32)
        wpart = sb("wpart", [P, NT, NE1], BF16)
        wparts = sb("wparts", [P, NT, NE1, 3], BF16)
        xrest = sb("xrest", [P, NT, H], F32)
        xparts = sb("xparts", [P, 3, NT, H], BF16)
        shgu = sb("shgu", [P, 2, NC, 2 * FF1], F32)
        shd = sb("shd", [HF1, NSH, H], F32)
        shsilu = sb("shsilu", [HF1, 2, SEQ], F32)
        shinner = sb("shinner", [HF1, NSH, T], F32)
        wgu = sb("wgu", [P, 2, GE, NC, 2 * FF1], F32)
        wd = sb("wd", [HF1, 2, GE, 2, H], F32)
        pick = sb("pick", [P, 2, NT, P], BF16)
        pickt = sb("pickt", [P, 2, T], BF16)
        buf = sb("buf", [P, 2, NC, P], F32)
        wtmp = sb("wtmp", [P, 2, GE * 3], F32)
        wslot = sb("wslot", [P, 2], F32)
        silu = sb("silu", [P, FF1], F32)
        acted = sb("acted", [P, FF1], F32)
        actt = sb("actt", [HF1, 2, P], F32)
        y = sb("y", [P, H], F32)
        yrest = sb("yrest", [P, H], F32)
        yparts = sb("yparts", [P, 2, 3, H], BF16)
        acc = ctx.enter_context(psum(nc, "acc", [P, NT, H], F32))
        banks = ctx.enter_context(psum(nc, "banks", [P, 4, SEQ], F32))
        block = ctx.enter_context(nc.Block())
        b_gather, b_weight = banks[:, 0, 0:NC * P], banks[:, 0, NC * P:NC * P + GE * 3]
        b_spread, b_inner = banks[:, 1, :], banks[:, 2, 0:2 * FF1]
        b_turn, b_out = banks[0:HF1, 3, 0:2 * P], banks[:, 3, H:2 * H]
        wparts_g = wparts[:, :, :, :].rearrange("p t (n e) c -> p t n (e c)", e=GE)
        b_sh = acc[:, :, :].rearrange("p (b s) h -> p b (s h)", s=2)

        @block.sync
        def _(sp):
            for to, name in ((router[:, :, :], "router1"), (ranks1[:, :], "before"), (slot1[:, :], "slot1"),
                             (own[:, :], "own")):
                sp.dma_start(to, d[name]).then_inc(c["loaded"].sem, 16)
            sp.dma_start(shgu[:, :, :, :], d["shared1_gu"].rearrange("p a c n -> p a c n")).then_inc(c["shared_w"].sem, 16)
            sp.dma_start(shd[:, :, :], d["shared1_d"]).then_inc(c["shared_w"].sem, 16)
            with sp.Fori(0, NG1 // BODY) as i:
                for k in range(BODY):
                    at = bass.ds(BODY * i + k, 1)
                    wait(sp, c["inner"], k - 1, i, BODY)
                    sp.dma_start(wgu[:, k], d["w1_gu"][at].rearrange("o p e c n -> p (o e) c n")) \
                        .then_inc(gu_full[k].sem, 16)
                    wait(sp, c["down"], k - 1, i, BODY)
                    sp.dma_start(wd[:, k], d["w1_d"][at].rearrange("o p e c n -> p (o e) c n")) \
                        .then_inc(d_full[k].sem, 16)

        def live(i, m):
            return not isinstance(i, int) or 0 <= i * BODY + m < NG1

        @block.tensor
        def _(pe):
            for n in ("inner", "down", "gathered", "spread0", "spread1", "turned", "summed"):
                pe.sem_inc(c[n].sem, c[n].prime)
            pe.wait_ge(c["loaded"].sem, 64)
            for t in range(NT):
                for kc in range(NC):
                    last = pe.matmul(banks[:, 0, t * NE1:(t + 1) * NE1], g.xt[:, kc, t * P:(t + 1) * P],
                                     router[:, kc, :], start=(kc == 0), stop=(kc == NC - 1))
            last.then_inc(c["logits"].sem, 1)
            def count_places():
                pe.wait_ge(c["masked"].sem, 1)
                for t in range(NT):
                    pe.matmul(banks[:, 1, t * NE1:(t + 1) * NE1], ranks[:, 0:P], maskb[:, t, :], start=True, stop=False)
                    last = pe.matmul(banks[:, 1, t * NE1:(t + 1) * NE1], ranks[:, P:], prior[:, t, :],
                                     start=False, stop=True)
                last.then_inc(c["places"].sem, 1)

            pe.wait_ge(c["shared_w"].sem, 32)
            for j in range(NSH):
                for s in range(NSEQ):
                    n = j * NSEQ + s
                    if n == 4:
                        count_places()
                    wait(pe, c["sprod"], n - 1)
                    for which in range(2):
                        for kc in range(NC):
                            last = pe.matmul(b_sh[0:HF1, (n % 2) * 2 + which, :],
                                             shgu[:, which, kc, j * HF1:(j + 1) * HF1],
                                             g.xt[:, kc, s * SEQ:(s + 1) * SEQ], start=(kc == 0), stop=(kc == NC - 1))
                    last.then_inc(c["sinner"].sem, 1)
            wait(pe, c["sprod"], NSH * NSEQ)
            for t in range(NT):
                for j in range(NSH):
                    pe.matmul(acc[:, t, :], shinner[:, j, t * P:(t + 1) * P], shd[:, j, :],
                              start=(j == 0 and t % 2 == 0), stop=True, skip_group_check=True)
            pe.wait_ge(c["parted"].sem, 1)

            def gather(i, m):
                k = m % 2
                wait(pe, c["picked"], m + 1, i, BODY)
                wait(pe, c["buffered"], m, i, BODY)
                wait(pe, c["sloted"], m, i, BODY)
                for hc in range(NC):
                    for t in range(NT):
                        for part in range(3):
                            pe.matmul(b_gather[:, hc * P:(hc + 1) * P], xparts[:, part, t, hc * P:(hc + 1) * P],
                                      pick[:, k, t, :], start=(t == 0 and part == 0),
                                      stop=(t == NT - 1 and part == 2))
                at = bass.ds(BODY * i + m, 1) if not isinstance(i, int) else slice(BODY * i + m, BODY * i + m + 1)
                for t in range(NT):
                    last = pe.matmul(b_weight, pick[:, k, t, :], wparts_g[:, t, at, :].rearrange("p o w -> p (o w)"),
                                     start=(t == 0), stop=(t == NT - 1))
                last.then_inc(c["gathered"].sem, 1)

            def spread(i, m, half):
                k = m % 2
                wait(pe, c["kept1" if half == 0 else "kept0"], m + half, i, BODY)
                for j in range(4):
                    t = 4 * half + j
                    last = pe.matmul(b_spread[:, j * P:(j + 1) * P], pick[:, k, t, :], g.identb[:, :],
                                     start=True, stop=True)
                last.then_inc(c[f"spread{half}"].sem, 1)

            def inner(i, n):
                k = n % 2
                wait(pe, gu_full[k], 16 * (n // 2) + 16, i, 16)
                wait(pe, c["buffered"], n + 1, i, BODY)
                wait(pe, c["acted"], n, i, BODY)
                for kc in range(NC):
                    for e in range(GE):
                        last = pe.matmul(b_inner[e * CAP:(e + 1) * CAP, :], buf[:, k, kc, e * CAP:(e + 1) * CAP],
                                         wgu[:, k, e, kc, :], start=(kc == 0), stop=(kc == NC - 1),
                                         tile_position=(0, e * CAP))
                last.then_inc(c["inner"].sem, 1)

            def turn(i, n):
                wait(pe, c["acted"], n + 1, i, BODY)
                wait(pe, c["split"], n, i, BODY)
                for j in range(2):
                    last = pe.transpose(b_turn[:, j * P:(j + 1) * P], acted[:, j * HF1:(j + 1) * HF1], g.ident[:, :])
                last.then_inc(c["turned"].sem, 1)

            def down(i, n):
                k = n % 2
                wait(pe, d_full[k], 16 * (n // 2) + 16, i, 16)
                wait(pe, c["moved"], n + 1, i, BODY)
                for j in range(2):
                    for e in range(GE):
                        last = pe.matmul(b_out[e * CAP:(e + 1) * CAP, :], actt[:, j, e * CAP:(e + 1) * CAP],
                                         wd[:, k, e, j, :], start=(j == 0), stop=(j == 1),
                                         tile_position=(0, e * CAP))
                last.then_inc(c["down"].sem, 1)

            def sum_up(i, n):
                k = n % 2
                wait(pe, c["split"], n + 1, i, BODY)
                wait(pe, c["kept0"], n + 1, i, BODY)
                wait(pe, c["kept1"], n + 1, i, BODY)
                for t in range(NT):
                    for part in range(3):
                        last = pe.matmul(acc[:, t, :], pickt[:, k, t * P:(t + 1) * P], yparts[:, k, part, :],
                                         start=False, stop=True, skip_group_check=True)
                last.then_inc(c["summed"].sem, 1)

            def slot(i, n):
                if live(i, n + 1):
                    gather(i, n + 1)
                if live(i, n):
                    inner(i, n)
                if live(i, n - 1):
                    sum_up(i, n - 1)
                if live(i, n + 1):
                    spread(i, n + 1, 0)
                if live(i, n):
                    turn(i, n)
                if live(i, n + 1):
                    spread(i, n + 1, 1)
                if live(i, n):
                    down(i, n)

            slot(0, -1)
            slot(0, 0)
            slot(0, 1)
            with pe.Fori(1, LOOPS) as i:
                for n in range(BODY):
                    slot(i, n)
            for n in range(BODY + 1):
                slot(LOOPS, n)

        @block.scalar
        def _(act):
            for n in ("buffered", "silu", "moved", "kept1"):
                act.sem_inc(c[n].sem, c[n].prime)
            act.wait_ge(c["peak"].sem, 1)
            for t in range(NT):
                last = act.activation(score[:, t, 0:NE1], banks[:, 0, t * NE1:(t + 1) * NE1], ACT.Exp,
                                      bias=peak[:, t:t + 1], accum_out=sums[:, t:t + 1])
            last.then_inc(c["expd"].sem, 1)
            for n in range(NSH * NSEQ):
                act.wait_ge(c["sinner"].sem, n + 1)
                wait(act, c["sprod"], n - 1)
                act.activation(shsilu[:, n % 2, :], b_sh[0:HF1, (n % 2) * 2, :], ACT.Silu).then_inc(c["ssilu"].sem, 1)

            def slot(i, n):
                if live(i, n + 1):
                    m = n + 1
                    wait(act, c["gathered"], m + 1, i, BODY)
                    wait(act, c["inner"], m - 1, i, BODY)
                    act.activation(buf[:, m % 2].rearrange("p c s -> p (c s)"), b_gather, ACT.Copy) \
                        .then_inc(c["buffered"].sem, 1)
                if live(i, n):
                    wait(act, c["inner"], n + 1, i, BODY)
                    wait(act, c["acted"], n, i, BODY)
                    act.activation(silu[:, :], b_inner[:, 0:FF1], ACT.Silu).then_inc(c["silu"].sem, 1)
                    wait(act, c["turned"], n + 1, i, BODY)
                    wait(act, c["down"], n, i, BODY)
                    act.activation(actt[:, :, :].rearrange("p c s -> p (c s)"), b_turn, ACT.Copy) \
                        .then_inc(c["moved"].sem, 1)
                if live(i, n + 1):
                    m = n + 1
                    wait(act, c["spread1"], m + 1, i, BODY)
                    wait(act, c["summed"], m - 1, i, BODY)
                    act.activation(pickt[:, m % 2, SEQ:T], b_spread, ACT.Copy).then_inc(c["kept1"].sem, 1)

            slot(0, -1)
            slot(0, 0)
            slot(0, 1)
            with act.Fori(1, LOOPS) as i:
                for n in range(BODY):
                    slot(i, n)
            for n in range(BODY):
                slot(LOOPS, n)

        @block.vector
        def _(dve):
            for n in ("picked", "sloted", "kept0", "acted", "split"):
                dve.sem_inc(c[n].sem, c[n].prime)
            done = [0]

            def link(op):
                done[0] += 1
                op.then_inc(c["own_v"].sem, 1)
                dve.wait_ge(c["own_v"].sem, done[0])

            dve.memset(score[:, :, NE1:], SENTINEL)
            dve.memset(prior[:, 0, :], 0.0)
            dve.wait_ge(c["loaded"].sem, 64)
            dve.tensor_copy(ranks[:, :], ranks1[:, :])
            dve.wait_ge(c["logits"].sem, 1)
            dve.reduce_max(peak[:, :], banks[:, 0, :].rearrange("p (t e) -> p t e", t=NT), axis=AX.X, negate=True) \
                .then_inc(c["peak"].sem, 1)
            dve.wait_ge(c["expd"].sem, 1)
            link(dve.reciprocal(sums[:, :], sums[:, :]))
            link(dve.tensor_tensor(score[:, :, 0:NE1], score[:, :, 0:NE1],
                                   sums[:, :].unsqueeze(2).broadcast_to([P, NT, NE1]), ALU.mult))
            for t in range(NT):
                op = dve.max(top[:, t, :], score[:, t, 0:NE1])
            link(op)
            link(dve.memset(top[:, :, TOP1:], SENTINEL))
            for t in range(NT):
                op = dve.match_replace(left[:, t, :], top[:, t, :], score[:, t, :], -1.0)
            link(op)
            dve.tensor_scalar(maskb[:, :, :], left[:, :, 0:NE1], 0.0, None, ALU.is_lt)
            link(dve.scalar_tensor_tensor(wrest[:, :, :], left[:, :, 0:NE1], 0.0, score[:, :, 0:NE1],
                                          ALU.is_lt, ALU.mult))
            for t in range(1, NT):
                op = dve.tensor_tensor(prior[:, t, :], prior[:, t - 1, :], maskb[:, t - 1, :], ALU.add)
                if t < NT - 1:
                    link(op)
            op.then_inc(c["masked"].sem, 1)

            def shared_product(n):
                j, s = n // NSEQ, n % NSEQ
                dve.wait_ge(c["ssilu"].sem, n + 1)
                dve.tensor_tensor(shinner[:, j, s * SEQ:(s + 1) * SEQ], shsilu[:, n % 2, :],
                                  b_sh[0:HF1, (n % 2) * 2 + 1, :], ALU.mult).then_inc(c["sprod"].sem, 1)

            shared_product(0)
            shared_product(1)
            link(dve.tensor_copy(wpart[:, :, :], wrest[:, :, :]))
            dve.tensor_copy(wparts[:, :, :, 0], wpart[:, :, :])
            link(dve.tensor_tensor(wrest[:, :, :], wrest[:, :, :], wpart[:, :, :], ALU.subtract))
            shared_product(2)
            link(dve.tensor_copy(wpart[:, :, :], wrest[:, :, :]))
            dve.tensor_copy(wparts[:, :, :, 1], wpart[:, :, :])
            link(dve.tensor_tensor(wrest[:, :, :], wrest[:, :, :], wpart[:, :, :], ALU.subtract))
            dve.tensor_copy(wparts[:, :, :, 2], wrest[:, :, :])
            shared_product(3)
            dve.wait_ge(c["places"].sem, 1)
            link(dve.tensor_scalar(place[:, :, :].rearrange("p t e -> p (t e)"), banks[:, 1, :], 1.0, 2.0 * CAP,
                                   ALU.add, ALU.min))
            link(dve.tensor_tensor(place[:, :, :], place[:, :, :], maskb[:, :, :], ALU.mult))
            shared_product(4)
            for part in range(3):
                src = xrest if part else g.xn
                link(dve.tensor_copy(xparts[:, part], src[:, :, :]))
                if part < 2:
                    op = dve.tensor_tensor(xrest[:, :, :], src[:, :, :], xparts[:, part], ALU.subtract)
                    link(op)
                shared_product(5 + part)
            dve.sem_inc(c["parted"].sem, 1)

            def picks(i, m):
                wait(dve, c["spread1"], m - 1, i, BODY)
                at = bass.ds((BODY * i + m) * GE, GE) if not isinstance(i, int) \
                    else slice((BODY * i + m) * GE, (BODY * i + m + 1) * GE)
                dve.tensor_tensor(pick[:, m % 2].rearrange("p t (e s) -> p t e s", s=CAP),
                                  place[:, :, at].unsqueeze(3).broadcast_to([P, NT, GE, CAP]),
                                  slot1[:, :].unsqueeze(1).unsqueeze(1).broadcast_to([P, NT, GE, CAP]),
                                  ALU.is_equal).then_inc(c["picked"].sem, 1)

            chained = [0]

            def slot(i, n):
                if live(i, n + 1):
                    m = n + 1
                    wait(dve, c["gathered"], m + 1, i, BODY)
                    wait(dve, c["buffered"], m + 1, i, BODY)
                    wait(dve, c["split"], m - 1, i, BODY)
                    dve.tensor_tensor_reduce(out=wtmp[:, m % 2, :], in0=b_weight, in1=own[:, :], scale=1.0, scalar=0.0,
                                             op0=ALU.mult, op1=ALU.add, accum_out=wslot[:, m % 2:m % 2 + 1]) \
                        .then_inc(c["sloted"].sem, 1)
                if live(i, n):
                    wait(dve, c["silu"], n + 1, i, BODY)
                    wait(dve, c["turned"], n, i, BODY)
                    dve.tensor_tensor(acted[:, :], silu[:, :], b_inner[:, FF1:2 * FF1], ALU.mult) \
                        .then_inc(c["acted"].sem, 1)
                if live(i, n + 1):
                    m = n + 1
                    wait(dve, c["spread0"], m + 1, i, BODY)
                    wait(dve, c["summed"], m - 1, i, BODY)
                    dve.tensor_copy(pickt[:, m % 2, 0:SEQ], b_spread).then_inc(c["kept0"].sem, 1)
                if live(i, n + 2):
                    picks(i, n + 2)
                if live(i, n):
                    k = n % 2
                    wait(dve, c["down"], n + 1, i, BODY)
                    wait(dve, c["sloted"], n + 1, i, BODY)
                    wait(dve, c["summed"], n - 1, i, BODY)
                    at = 4 * n if isinstance(i, int) else 4 * n
                    dve.tensor_scalar(y[:, :], b_out, wslot[:, k:k + 1], None, ALU.mult).then_inc(c["chain"].sem, 1)
                    wait(dve, c["chain"], at + 1, i, 4 * BODY)
                    dve.tensor_copy(yparts[:, k, 0, :], y[:, :]).then_inc(c["chain"].sem, 1)
                    wait(dve, c["chain"], at + 2, i, 4 * BODY)
                    dve.tensor_tensor(y[:, :], y[:, :], yparts[:, k, 0, :], ALU.subtract).then_inc(c["chain"].sem, 1)
                    wait(dve, c["chain"], at + 3, i, 4 * BODY)
                    dve.tensor_copy(yparts[:, k, 1, :], y[:, :]).then_inc(c["chain"].sem, 1)
                    wait(dve, c["chain"], at + 4, i, 4 * BODY)
                    dve.tensor_tensor(yparts[:, k, 2, :], y[:, :], yparts[:, k, 1, :], ALU.subtract) \
                        .then_inc(c["split"].sem, 1)

            picks(0, 0)
            slot(0, -1)
            slot(0, 0)
            slot(0, 1)
            with dve.Fori(1, LOOPS) as i:
                for n in range(BODY):
                    slot(i, n)
            for n in range(BODY):
                slot(LOOPS, n)
            wait(dve, c["summed"], NG1)
            for t in range(0, NT, 2):
                x2 = g.x[:, t:t + 2, :].rearrange("p a h -> p (a h)")
                dve.tensor_tensor(x2, x2, acc[:, t:t + 2, :].rearrange("p a h -> p (a h)"), ALU.add)
    finish(nc, c.values())


class Shared:
    pass


def hybrid_layers_kernel(nc, ins, out):
    g = Shared()
    with (
        nc.sbuf_tensor("x", [P, NT, H], F32) as g.x,
        nc.sbuf_tensor("xn", [P, NT, H], F32) as g.xn,
        nc.sbuf_tensor("xt", [P, NC, T], F32) as g.xt,
        nc.sbuf_tensor("xh", [P, NC, T], F32R) as g.xh,
        nc.sbuf_tensor("xl", [P, NC, T], F32R) as g.xl,
        nc.sbuf_tensor("ident", [P, P], F32) as g.ident,
        nc.sbuf_tensor("identb", [P, P], BF16) as g.identb,
        nc.sbuf_tensor("zeros", [P, SEQ], BF16) as g.zeros,
        nc.sbuf_tensor("eps", [P, 1], F32) as g.eps,
        nc.sbuf_tensor("one", [P, 1], F32) as g.one,
        nc.sbuf_tensor("gamma", [P, NC], F32) as g.gamma,
    ):
        loaded, = counts = [Count(nc, "loaded")]
        with nc.Block() as block:
            @block.sync
            def _(sp):
                sp.dma_start(g.x[:, :, :], ins["x"]).then_inc(loaded.sem, 16)
                sp.dma_start(g.ident[:, :], ins["ident"]).then_inc(loaded.sem, 16)
                sp.dma_start(g.gamma[:, :], ins["gamma"]).then_inc(loaded.sem, 16)
                sp.wait_ge(loaded.sem, 48)

            @block.vector
            def _(dve):
                dve.memset(g.zeros[:, :], 0.0)
                dve.memset(g.eps[:, :], EPS)
                dve.memset(g.one[:, :], 1.0)
                dve.wait_ge(loaded.sem, 48)
                dve.tensor_copy(g.identb[:, :], g.ident[:, :])
        finish(nc, counts)

        stages(nc, g, ins)

        stored, = counts = [Count(nc, "stored")]
        with nc.Block() as block:
            @block.sync
            def _(sp):
                sp.dma_start(out, g.x[:, :, :]).then_inc(stored.sem, 16)
                sp.wait_ge(stored.sem, 16)


def stages(nc, g, ins):
    layer_norm(nc, g)
    selective_scan(nc, g, ins)
    layer_norm(nc, g, split=True)
    mixture(nc, g, ins)
    layer_norm(nc, g, gamma=g.gamma, again=True, split=True)
    attention(nc, g, ins, "mqa", kv_every=HEADS, window=False)
    layer_norm(nc, g, split=True)
    mixture(nc, g, ins)
    layer_norm(nc, g, split=True)
    attention(nc, g, ins, "gqa", kv_every=4, window=False)
    layer_norm(nc, g)
    capacity_mixture(nc, g, ins)
    layer_norm(nc, g, split=True)
    attention(nc, g, ins, "mha", kv_every=1, window=True)
    layer_norm(nc, g)
    capacity_mixture(nc, g, ins)


def kernel(**inputs):
    import numpy as np
    import concourse.bacc as bacc
    from concourse.bass_utils import run_bass_kernel_spmd

    a = {k: np.asarray(v) for k, v in inputs.items()}

    def chunks(w):
        w = w.reshape(*w.shape[:-2], -1, P, w.shape[-1])
        return np.moveaxis(w, -3, -2)

    def heads(w):
        return np.moveaxis(chunks(w).reshape(P, NC, -1, P), 2, 0)

    def tokens(x):
        return x.reshape(NT, P, H).transpose(1, 0, 2)

    arrays = {}
    arrays["x"] = tokens(a["L0_attn_a_hidden_states"].reshape(T, H))
    arrays["ident"] = np.eye(P, dtype=np.float32)
    arrays["gamma"] = a["L0_attn_b_gamma"].reshape(NC, P).T

    w = a["L0_attn_a_x_proj_w"].T
    bc, dt = w[:, DT_RANK:], w[:, :DT_RANK]
    arrays["xw"] = chunks(np.concatenate([bc, bc, bc, dt], 1))
    dtw = np.zeros((XROWS, H), np.float32)
    dtw[XROWS - DT_RANK:] = a["L0_attn_a_dt_proj_w"].T
    arrays["dtw"] = dtw
    arrays["vecs"] = np.concatenate([
        a["L0_attn_a_dt_proj_b"].reshape(NC, P).T, a["L0_attn_a_D"].reshape(NC, P).T,
        a["L0_attn_a_A_log"].reshape(NC, P, N_STATE).transpose(1, 0, 2).reshape(P, -1)], 1)
    arrays["pick"] = np.tile(np.eye(2 * N_STATE, dtype=np.float32), (3, 1))

    gate, up, down = (a["L0_ffn_" + n] for n in ("Wg", "Wu", "Wd"))
    sgate, sup, sdown = (a["L0_ffn_s" + n] for n in ("Wg", "Wu", "Wd"))
    gate = np.concatenate([gate, sgate.reshape(H, 2, FF0).transpose(1, 0, 2)])
    up = np.concatenate([up, sup.reshape(H, 2, FF0).transpose(1, 0, 2)])
    down = np.concatenate([down, sdown.reshape(2, FF0, H)])
    arrays["w0"] = np.concatenate([chunks(gate).reshape(NU0, P, -1), chunks(up).reshape(NU0, P, -1), down], 2)
    arrays["router0"] = chunks(a["L0_ffn_gate_w"].T)

    inv = 1.0 / np.float32(10000.0) ** (np.arange(0, P, 2, dtype=np.float32) / np.float32(P))
    angle = np.arange(SEQ, dtype=np.float32)[None, :] * inv.astype(np.float32)[:, None]
    cos, sin = np.cos(angle), np.sin(angle)
    rope = np.stack([np.concatenate([cos, cos]), np.concatenate([-sin, sin])], 1)
    arrays["rope_k"] = rope
    arrays["rope_q"] = rope * np.float32(P ** -0.5)
    q, k = np.arange(P)[:, None], np.arange(P)[None, :]
    arrays["mask"] = np.concatenate([np.where(k > q, 0, 1), np.where(k > q, 1, 0)], 1).astype(np.float32)
    pairs = np.concatenate([np.arange(0, P, 2), np.arange(1, P, 2)])

    def unpaired(w):
        return w.T.reshape(H, -1, P)[:, :, pairs].reshape(H, -1)

    kv = a["L0_attn_b_Wkv"]
    weights = {
        "mqa": (a["L0_attn_b_Wq"], kv[:, :P], kv[:, P:], a["L0_attn_b_Wo"]),
        "gqa": (unpaired(a["L1_attn_a_Wq"]), unpaired(a["L1_attn_a_Wk"]), a["L1_attn_a_Wv"].T, a["L1_attn_a_Wo"].T),
        "mha": tuple(a["L1_attn_b_" + n] for n in ("wq", "wk", "wv", "wo")),
    }
    for n, (wq, wk, wv, wo) in weights.items():
        arrays[n + "_q"] = heads(wq)
        arrays[n + "_kv"] = np.stack([heads(wk), heads(wv)], 2)
        arrays[n + "_o"] = wo.reshape(HEADS, P, H).transpose(1, 0, 2)

    gu = chunks(np.concatenate([a["L1_ffn_w_gate"], a["L1_ffn_w_up"]], 2))
    arrays["w1_gu"] = gu.reshape(NG1, GE, P, NC, 2 * FF1).transpose(0, 2, 1, 3, 4)
    arrays["w1_d"] = a["L1_ffn_w_down"].reshape(NG1, GE, 2, HF1, H).transpose(0, 3, 1, 2, 4)
    arrays["shared1_gu"] = np.stack([chunks(a["L1_ffn_sw_gate"]), chunks(a["L1_ffn_sw_up"])], 1)
    arrays["shared1_d"] = a["L1_ffn_sw_down"].reshape(NSH, HF1, H).transpose(1, 0, 2)
    arrays["router1"] = chunks(a["L1_ffn_gate_w"].T)
    t = np.arange(P)
    arrays["before"] = np.concatenate([(t[:, None] < t[None, :]).astype(np.float32), np.ones((P, P), np.float32)], 1)
    arrays["slot1"] = np.tile(np.arange(1, CAP + 1, dtype=np.float32), (P, 1))
    arrays["own"] = np.repeat((t[:, None] // CAP == np.arange(GE)[None, :]).astype(np.float32)[:, None, :], 3, 1) \
        .transpose(0, 2, 1).reshape(P, GE * 3)

    nc = bacc.Bacc("TRN2", target_bir_lowering=False, num_devices=1)
    sent, ins = {}, {}
    for name, v in arrays.items():
        v = np.ascontiguousarray(v, dtype=np.float32)
        sent["in_" + name] = v
        ins[name] = nc.dram_tensor("in_" + name, v.shape, F32, kind="ExternalInput").ap()
    out = nc.dram_tensor("out", (P, NT, H), F32, kind="ExternalOutput").ap()
    hybrid_layers_kernel(nc, ins, out)
    r = run_bass_kernel_spmd(nc, [sent], core_ids=[0])
    got = r.results[0]["out"]
    return got.transpose(1, 0, 2).reshape(NSEQ, SEQ, H)
```

```python
from contextlib import ExitStack

import concourse.bass as bass
from concourse import mybir

F32 = mybir.dt.float32
BF16 = mybir.dt.bfloat16
F32R = mybir.dt.float32r
ALU = mybir.AluOpType
ACT = mybir.ActivationFunctionType
AX = mybir.AxisListType

P = 128
T, H = 1024, 256
SEQ = 512
NSEQ = T // SEQ
NT, NC = T // P, H // P
EPS = 1e-5

HEADS = 16
N_STATE, DT_RANK = 16, 16
XROWS = 3 * 2 * N_STATE + DT_RANK

NE0, TOP0, FF0 = 16, 8, 128
NU0 = NE0 + 2
ROUTED_SCALE = 2.5

NE1, TOP1, FF1 = 64, 6, 176
CAP = 32
HF1 = FF1 // 2
GE = P // CAP
NG1 = NE1 // GE
NSH = -(-2 * FF1 // P)
NEG = -1e30


class Count:

    def __init__(self, nc, name, prime=0):
        self.sem = nc.alloc_semaphore(f"{name}_{nc.next_id()}")
        self.prime = prime


def sbuf(nc, name, shape, dtype):
    return nc.sbuf_tensor(f"{name}_{nc.next_id()}", shape, dtype)


def psum(nc, name, shape, dtype):
    return nc.psum_tensor(f"{name}_{nc.next_id()}", shape, dtype)


def wait(eng, count, n, i=0, per=0):
    if isinstance(i, int):
        n += i * per
        if n > 0:
            eng.wait_ge(count.sem, n + count.prime)
    else:
        assert n + count.prime > 0, (count.sem, n)
        eng.wait_ge(count.sem, i * per + (n + count.prime))


def finish(nc, counts):
    nc.clear_and_free_semaphores([c.sem for c in counts])
    nc.all_engine_barrier(sem_only=True)


class Norm:

    def __init__(self, nc, g, turn, gamma=None, again=False, split=False):
        self.g, self.turn, self.gamma, self.split = g, turn, gamma, split
        self.rounds = 2 if again else 1
        self.stats, self.moments, self.rooted, self.over, self.normed, self.turned = (
            Count(nc, n) for n in ("stats", "moments", "rooted", "over", "normed", "turned"))
        self.kept = [Count(nc, "kept_first"), Count(nc, "kept_second")]
        self.high, self.low = Count(nc, "high"), Count(nc, "low")
        self.counts = [self.stats, self.moments, self.rooted, self.over, self.normed, self.turned,
                       *self.kept, self.high, self.low]

    def wait_xt(self, eng):
        for s in range(NSEQ):
            eng.wait_ge(self.kept[s].sem, NC)

    def wait_parts(self, eng, s=NSEQ - 1):
        eng.wait_ge(self.low.sem, NC * (s + 1))

    def wait_xn(self, eng):
        eng.wait_ge(self.normed.sem, NT * self.rounds)

    def vector(self, dve):
        g, half = self.g, NT // 2
        for r in range(self.rounds):
            src = g.xn if r else g.x
            for h in range(2):
                if r:
                    dve.wait_ge(self.normed.sem, NT + half * (h - 1))
                for t in range(h * half, (h + 1) * half):
                    dve.bn_stats(g.bn[:, t, :], src[:, t, :]).then_inc(self.stats.sem, 1)
                for t in range(h * half, (h + 1) * half):
                    dve.wait_ge(self.stats.sem, NT * r + t + 1)
                    dve.bn_aggr(g.mv[:, t, :], g.bn[:, t, :]).then_inc(self.moments.sem, 1)
            for h in range(2):
                cut = slice(h * half, (h + 1) * half)
                dve.wait_ge(self.rooted.sem, 2 * r + h + 1)
                dve.reciprocal(g.rstd[:, cut], g.std[:, cut]).then_inc(self.over.sem, 1)
                dve.wait_ge(self.over.sem, 2 * r + h + 1)
                dve.wait_ge(self.moments.sem, NT * r + (h + 1) * half)
                for t in range(h * half, (h + 1) * half):
                    dve.tensor_scalar(g.xn[:, t, :], src[:, t, :], g.mv[:, t, 0:1], g.rstd[:, t:t + 1],
                                      ALU.subtract, ALU.mult).then_inc(self.normed.sem, 1)
        for c in range(NC):
            self.keep(dve, 1, c)
        for j in range(NSEQ * NC if self.split else 0):
            s, c = j // NC, j % NC
            dve.wait_ge(self.high.sem, j + 1)
            cut = slice(s * SEQ, (s + 1) * SEQ)
            dve.tensor_tensor(g.xl[:, c, cut], g.xt[:, c, cut], g.xh[:, c, cut].bitcast(F32), ALU.subtract) \
                .then_inc(self.low.sem, 1)

    def keep(self, eng, s, c):
        src, dst = self.turn[:, c, s * SEQ:(s + 1) * SEQ], self.g.xt[:, c, s * SEQ:(s + 1) * SEQ]
        gamma = None if self.gamma is None else self.gamma[:, c:c + 1]
        eng.wait_ge(self.turned.sem, (s * NC + c + 1) * (NT // 2))
        if s == 0:
            op = eng.activation(dst, src, ACT.Copy) if gamma is None else \
                eng.activation(dst, src, ACT.Copy, scale=gamma)
        else:
            op = eng.tensor_copy(dst, src) if gamma is None else eng.tensor_scalar(dst, src, gamma, None, ALU.mult)
        op.then_inc(self.kept[s].sem, 1)

    def scalar(self, act):
        g, half = self.g, NT // 2
        for r in range(self.rounds):
            for h in range(2):
                cut = slice(h * half, (h + 1) * half)
                act.wait_ge(self.moments.sem, NT * r + (h + 1) * half)
                if r:
                    act.wait_ge(self.over.sem, h + 1)
                act.activation(g.std[:, cut], g.mv[:, cut, 1], ACT.Sqrt, bias=g.eps[:, 0:1]) \
                    .then_inc(self.rooted.sem, 1)
        for s in range(NSEQ):
            for c in range(NC):
                if s == 0:
                    self.keep(act, 0, c)
                if self.split:
                    act.wait_ge(self.kept[s].sem, c + 1)
                    cut = slice(s * SEQ, (s + 1) * SEQ)
                    act.activation(g.xh[:, c, cut], g.xt[:, c, cut], ACT.Copy).then_inc(self.high.sem, 1)

    def tensor(self, pe):
        g, half = self.g, NT // 2
        for s in range(NSEQ):
            for c in range(NC):
                for t in range(s * half, (s + 1) * half):
                    pe.wait_ge(self.normed.sem, NT * (self.rounds - 1) + t + 1)
                    pe.transpose(self.turn[:, c, t * P:(t + 1) * P], g.xn[:, t, c * P:(c + 1) * P],
                                 g.ident[:, :]).then_inc(self.turned.sem, 1)


def selective_scan(nc, g, d):
    c = {n: Count(nc, n, p) for n, p in (
        ("loaded", 0), ("projected", 0), ("rows", 0), ("split", 0), ("dt", 0), ("soft_v", 0),
        ("size", 0), ("relu", 0), ("nega", 0), ("e", 0), ("lg", 0), ("over", 0), ("main", 0),
        ("ready", 0), ("spread", 0), ("copied", 2), ("decay", 0), ("driven", 0), ("state", 4),
        ("read", 4), ("summed", 4), ("gated", 0), ("turned", 0), ("zeroed", 0), ("selected", 0), ("added", 0))}
    HALF = 2 * N_STATE
    with (
        sbuf(nc, "xw", [P, NC, XROWS], F32) as xw,
        sbuf(nc, "dtw", [XROWS, H], F32) as dtw,
        sbuf(nc, "vecs", [P, 2 * NC + NC * N_STATE], F32) as vecs,
        sbuf(nc, "pick1", [3 * HALF, HALF], F32) as pick1,
        sbuf(nc, "pick", [3 * HALF, HALF, P], BF16) as pick,
        sbuf(nc, "rows", [XROWS, T], F32) as rows,
        sbuf(nc, "rest", [3 * HALF, T], F32) as rest,
        sbuf(nc, "part", [3 * HALF, T], BF16) as part,
        sbuf(nc, "stack", [3 * HALF, T], BF16) as stack,
        sbuf(nc, "nega", [P, NC, N_STATE], F32) as nega,
        sbuf(nc, "delta", [P, NC, T], F32) as delta,
        sbuf(nc, "du", [P, NC, T], F32) as du,
        sbuf(nc, "decay", [P, 2, NC, T], F32) as decay,
        sbuf(nc, "drive", [P, 2, NC, T], F32) as drive,
        sbuf(nc, "state", [P, 2, NC, T], F32) as state,
        sbuf(nc, "term", [P, 2, NC, T], F32) as term,
        sbuf(nc, "bs", [P, 2, T], F32) as bs,
        sbuf(nc, "cs", [P, 2, T], F32) as cs,
        psum(nc, "acc", [P, NC, T], F32) as acc,
        psum(nc, "wide", [P, 2, T], F32) as wide,
        nc.Block() as block,
    ):
        norm = Norm(nc, g, wide)
        bias, dvec, alog = vecs[:, 0:NC], vecs[:, NC:2 * NC], vecs[:, 2 * NC:].rearrange("p (c n) -> p c n", c=NC)
        size, e, lg, relu, over, lost = decay[:, 0], decay[:, 1], drive[:, 0], drive[:, 1], state[:, 0], state[:, 1]

        @block.sync
        def _(sp):
            sp.dma_start(xw[:, :, :], d["xw"]).then_inc(c["loaded"].sem, 16)
            sp.dma_start(dtw[:, :], d["dtw"]).then_inc(c["loaded"].sem, 16)
            sp.dma_start(vecs[:, :], d["vecs"]).then_inc(c["loaded"].sem, 16)
            sp.dma_start(pick1[:, :], d["pick"]).then_inc(c["loaded"].sem, 16)

        @block.gpsimd
        def _(pool):
            pool.wait_ge(c["loaded"].sem, 64)
            pool.tensor_copy(pick[:, :, :], pick1[:, :].unsqueeze(2).broadcast_to([3 * HALF, HALF, P])) \
                .then_inc(c["selected"].sem, 1)
            for dc in range(NC):
                pool.wait_ge(c["relu"].sem, dc + 1)
                pool.wait_ge(c["lg"].sem, dc + 1)
                pool.tensor_tensor(relu[:, dc, :], relu[:, dc, :], lg[:, dc, :], ALU.add).then_inc(c["main"].sem, 1)
            pool.sem_inc(c["read"].sem, c["read"].prime)
            with pool.Fori(0, N_STATE // 2) as i:
                for k in range(2):
                    for dc in range(NC):
                        wait(pool, c["state"], 2 * k + dc + 1, i, 4)
                        wait(pool, c["copied"], 2 * (k + 1), i, 4)
                        wait(pool, c["summed"], 2 * k + dc - 3, i, 4)
                        pool.tensor_tensor(term[:, k, dc, :], state[:, k, dc, :], cs[:, k, :], ALU.mult) \
                            .then_inc(c["read"].sem, 1)

        @block.tensor
        def _(pe):
            norm.tensor(pe)
            norm.wait_xt(pe)
            pe.wait_ge(c["loaded"].sem, 64)
            for s in range(NSEQ):
                for kc in range(NC):
                    last = pe.matmul(acc[0:XROWS, 0, s * SEQ:(s + 1) * SEQ], xw[:, kc, :],
                                     g.xt[:, kc, s * SEQ:(s + 1) * SEQ], start=(kc == 0), stop=(kc == NC - 1))
                last.then_inc(c["projected"].sem, 1)
            pe.wait_ge(c["rows"].sem, 2)
            for dc in range(NC):
                for s in range(NSEQ):
                    pe.matmul(wide[:, dc, s * SEQ:(s + 1) * SEQ], dtw[:, dc * P:(dc + 1) * P],
                              rows[:, s * SEQ:(s + 1) * SEQ], start=True, stop=True).then_inc(c["dt"].sem, 1)
            for dc in range(NC):
                for s in range(NSEQ):
                    pe.matmul(acc[:, dc, s * SEQ:(s + 1) * SEQ], g.zeros[:, 0:P], g.zeros[:, :],
                              start=True, stop=True)
            pe.sem_inc(c["summed"].sem, c["summed"].prime)
            pe.wait_ge(c["split"].sem, 1)
            pe.wait_ge(c["selected"].sem, 1)

            def spread(i, k):
                for which in range(2):
                    wait(pe, c["copied"], 2 * k - 1 + which, i, 4)
                    for s in range(NSEQ):
                        n = 2 * i + (k + which * N_STATE)
                        at = slice(n, n + 1) if isinstance(i, int) else bass.ds(n, 1)
                        lhs = pick[:, at, :].rearrange("p o m -> p (o m)")
                        last = pe.matmul(wide[:, which, s * SEQ:(s + 1) * SEQ], lhs,
                                         stack[:, s * SEQ:(s + 1) * SEQ], start=True, stop=True)
                    last.then_inc(c["spread"].sem, 1)

            def add_terms(i, k):
                for dc in range(NC):
                    wait(pe, c["read"], 2 * k + dc + 1, i, 4)
                    for s in range(NSEQ):
                        last = pe.matmul(acc[:, dc, s * SEQ:(s + 1) * SEQ], g.ident[:, :],
                                         term[:, k, dc, s * SEQ:(s + 1) * SEQ], start=False, stop=True,
                                         skip_group_check=True)
                    last.then_inc(c["summed"].sem, 1)

            pe.wait_ge(c["relu"].sem, 2)
            spread(0, 0)
            spread(0, 1)
            with pe.Fori(0, N_STATE // 2 - 1) as i:
                for k in range(2):
                    spread(i, k + 2)
                    add_terms(i, k)
            add_terms(N_STATE // 2 - 1, 0)
            add_terms(N_STATE // 2 - 1, 1)
            for t in range(NT):
                for dc in range(NC):
                    if dc == 0:
                        pe.wait_ge(c["gated"].sem, NSEQ * NC)
                    last = pe.transpose(wide[:, t // 4, (t % 4) * H + dc * P:(t % 4) * H + (dc + 1) * P],
                                        state[:, 0, dc, t * P:(t + 1) * P], g.ident[:, :])
                last.then_inc(c["turned"].sem, 1)

        @block.scalar
        def _(act):
            norm.scalar(act)
            for s in range(NSEQ):
                act.wait_ge(c["projected"].sem, s + 1)
                act.activation(rows[:, s * SEQ:(s + 1) * SEQ], acc[0:XROWS, 0, s * SEQ:(s + 1) * SEQ],
                               ACT.Copy).then_inc(c["rows"].sem, 1)
            act.wait_ge(c["loaded"].sem, 64)
            for dc in range(NC):
                act.wait_ge(c["dt"].sem, 2 * dc + 2)
                act.activation(size[:, dc, :], wide[:, dc, :], ACT.Abs, bias=bias[:, dc:dc + 1]) \
                    .then_inc(c["size"].sem, 1)
                act.activation(relu[:, dc, :], wide[:, dc, :], ACT.Relu, bias=bias[:, dc:dc + 1]) \
                    .then_inc(c["relu"].sem, 1)
            act.activation(nega[:, :, :], alog, ACT.Exp).then_inc(c["nega"].sem, 1)
            for dc in range(NC):
                act.wait_ge(c["size"].sem, dc + 1)
                act.activation(e[:, dc, :], size[:, dc, :], ACT.Exp, scale=-1.0).then_inc(c["e"].sem, 1)
            for dc in range(NC):
                act.wait_ge(c["e"].sem, dc + 1)
                act.activation(lg[:, dc, :], e[:, dc, :], ACT.Ln, bias=g.one[:, 0:1]).then_inc(c["lg"].sem, 1)
            for dc in range(NC):
                act.wait_ge(c["lg"].sem, dc + 1)
                act.activation(over[:, dc, :], lg[:, dc, :], ACT.Exp, scale=-1.0).then_inc(c["over"].sem, 1)
            act.wait_ge(c["ready"].sem, NC)
            act.sem_inc(c["copied"].sem, c["copied"].prime)
            with act.Fori(0, N_STATE // 2) as i:
                for k in range(2):
                    for dc in range(NC):
                        wait(act, c["state"], 2 * k + dc - 3, i, 4)
                        act.activation(decay[:, k, dc, :], delta[:, dc, :], ACT.Exp,
                                       scale=nega[:, dc, bass.ds(2 * i + k, 1)]).then_inc(c["decay"].sem, 1)
                    for which, to in enumerate((bs, cs)):
                        wait(act, c["spread"], 2 * k + which + 1, i, 4)
                        if which == 0:
                            wait(act, c["state"], 2 * k - 2, i, 4)
                        else:
                            wait(act, c["read"], 2 * k - 2, i, 4)
                        act.activation(to[:, k, :], wide[:, which, :], ACT.Copy).then_inc(c["copied"].sem, 1)

        @block.vector
        def _(dve):
            norm.vector(dve)
            norm.wait_xt(dve)
            n = [0]

            def link(op):
                n[0] += 1
                op.then_inc(c["soft_v"].sem, 1)
                dve.wait_ge(c["soft_v"].sem, n[0])

            A3 = 3 * HALF
            dve.wait_ge(c["rows"].sem, 2)
            link(dve.tensor_copy(part[:, :], rows[0:A3, :]))
            dve.tensor_copy(stack[0:HALF, :], part[0:HALF, :])
            link(dve.tensor_tensor(rest[:, :], rows[0:A3, :], part[:, :], ALU.subtract))
            link(dve.tensor_copy(part[:, :], rest[:, :]))
            dve.tensor_copy(stack[HALF:2 * HALF, :], part[HALF:2 * HALF, :])
            link(dve.tensor_tensor(rest[:, :], rest[:, :], part[:, :], ALU.subtract))
            dve.tensor_copy(stack[2 * HALF:A3, :], rest[2 * HALF:A3, :]).then_inc(c["split"].sem, 1)
            dve.wait_ge(c["nega"].sem, 1)
            link(dve.tensor_scalar(nega[:, :, :], nega[:, :, :], -1.0, None, ALU.mult))
            for dc in range(NC):
                dve.wait_ge(c["e"].sem, dc + 1)
                link(dve.tensor_scalar(lost[:, dc, :], e[:, dc, :], 1.0, 1.0, ALU.add, ALU.subtract))
                link(dve.tensor_tensor(lost[:, dc, :], e[:, dc, :], lost[:, dc, :], ALU.subtract))
            for dc in range(NC):
                dve.wait_ge(c["over"].sem, dc + 1)
                link(dve.tensor_tensor(lost[:, dc, :], lost[:, dc, :], over[:, dc, :], ALU.mult))
                dve.wait_ge(c["main"].sem, dc + 1)
                link(dve.tensor_tensor(delta[:, dc, :], relu[:, dc, :], lost[:, dc, :], ALU.add))
                dve.tensor_tensor(du[:, dc, :], delta[:, dc, :], g.xt[:, dc, :], ALU.mult).then_inc(c["ready"].sem, 1)
            dve.wait_ge(c["ready"].sem, NC)
            dve.sem_inc(c["state"].sem, c["state"].prime)
            with dve.Fori(0, N_STATE // 2) as i:
                for k in range(2):
                    wait(dve, c["decay"], 2 * (k + 1), i, 4)
                    dve.memset(decay[:, k, :, 0:T:SEQ], 0.0).then_inc(c["zeroed"].sem, 1)
                    wait(dve, c["copied"], 2 * k + 1, i, 4)
                    for dc in range(NC):
                        wait(dve, c["state"], 2 * k + dc - 3, i, 4)
                        dve.tensor_tensor(drive[:, k, dc, :], du[:, dc, :], bs[:, k, :], ALU.mult) \
                            .then_inc(c["driven"].sem, 1)
                    wait(dve, c["zeroed"], k + 1, i, 2)
                    for dc in range(NC):
                        wait(dve, c["driven"], 2 * k + dc + 1, i, 4)
                        wait(dve, c["read"], 2 * k + dc - 3, i, 4)
                        dve.tensor_tensor_scan(state[:, k, dc, :], decay[:, k, dc, :], drive[:, k, dc, :], 0.0,
                                               ALU.mult, ALU.add).then_inc(c["state"].sem, 1)
            for dc in range(NC):
                wait(dve, c["summed"], 2 * N_STATE - NC + dc + 1)
                wait(dve, c["read"], 2 * N_STATE)
                for s in range(NSEQ):
                    cut = slice(s * SEQ, (s + 1) * SEQ)
                    dve.scalar_tensor_tensor(state[:, 0, dc, cut], g.xt[:, dc, cut], dvec[:, dc:dc + 1],
                                             acc[:, dc, cut], ALU.mult, ALU.add).then_inc(c["gated"].sem, 1)
            for t in range(0, NT, 2):
                dve.wait_ge(c["turned"].sem, t + 2)
                x2 = g.x[:, t:t + 2, :].rearrange("p a h -> p (a h)")
                dve.tensor_tensor(x2, x2, wide[:, t // 4, (t % 4) * H:(t % 4 + 2) * H], ALU.add)
    finish(nc, [*c.values(), *norm.counts])


def mixture(nc, g, d):
    c = {n: Count(nc, n, p) for n, p in (
        ("loaded", 0), ("gu_even", 0), ("gu_odd", 0), ("d_even", 0), ("d_odd", 0), ("logits", 0), ("gates", 0),
        ("own", 0), ("gu_high", 2), ("gu_low", 2), ("d_high", 2), ("d_low", 2),
        ("inner", 4), ("silu", 4), ("prod", 4), ("high", 4), ("low", 4), ("down", 4), ("added", 4))}
    gu_full, d_full = (c["gu_even"], c["gu_odd"]), (c["d_even"], c["d_odd"])
    GU = 2 * NC * FF0
    LAST = NU0 // 2 - 1
    with (
        sbuf(nc, "router", [P, NC, NE0], F32) as router,
        sbuf(nc, "gu", [P, 2, GU], F32) as gu,
        sbuf(nc, "gu_hi", [P, 2, GU], F32R) as gu_hi,
        sbuf(nc, "gu_lo", [P, 2, GU], F32R) as gu_lo,
        sbuf(nc, "wd", [P, 2, H], F32) as wd,
        sbuf(nc, "wd_hi", [P, 2, H], F32R) as wd_hi,
        sbuf(nc, "wd_lo", [P, 2, H], F32R) as wd_lo,
        sbuf(nc, "score", [P, NT, NE0], F32) as score,
        sbuf(nc, "left", [P, NT, NE0], F32) as left,
        sbuf(nc, "top", [P, NT, 8], F32) as top,
        sbuf(nc, "total", [P, NT], F32) as total,
        sbuf(nc, "weight", [P, NT, NU0], F32) as weight,
        sbuf(nc, "silu", [P, NSEQ, SEQ], F32) as silu,
        sbuf(nc, "inner", [P, NSEQ, SEQ], F32) as inner,
        sbuf(nc, "inner_hi", [P, 2, T], F32R) as inner_hi,
        sbuf(nc, "inner_lo", [P, 2, T], F32R) as inner_lo,
        psum(nc, "gate", [P, NSEQ, SEQ], F32) as gate,
        psum(nc, "up", [P, NSEQ, SEQ], F32) as up,
        psum(nc, "outs", [P, NT, H], F32) as outs,
        nc.Block() as block,
    ):
        norm = Norm(nc, g, outs[:, :, :].rearrange("p (c a) h -> p c (a h)", c=NC), split=True)

        @block.sync
        def _(sp):
            sp.dma_start(router[:, :, :], d["router0"]).then_inc(c["loaded"].sem, 16)
            with sp.Fori(0, NU0 // 2) as i:
                for k in range(2):
                    src = d["w0"][bass.ds(2 * i + k, 1)].rearrange("o p n -> p (o n)")
                    wait(sp, c["gu_low"], k - 1, i, 2)
                    sp.dma_start(gu[:, k, :], src[:, 0:GU]).then_inc(gu_full[k].sem, 16)
                    wait(sp, c["d_low"], k - 1, i, 2)
                    sp.dma_start(wd[:, k, :], src[:, GU:]).then_inc(d_full[k].sem, 16)

        @block.tensor
        def _(pe):
            pe.sem_inc(c["down"].sem, c["down"].prime)
            pe.sem_inc(c["inner"].sem, c["inner"].prime)
            norm.tensor(pe)
            pe.wait_ge(c["loaded"].sem, 16)
            norm.wait_xt(pe)
            for t in range(NT):
                for kc in range(NC):
                    last = pe.matmul(outs[:, 0, t * NE0:(t + 1) * NE0], g.xt[:, kc, t * P:(t + 1) * P],
                                     router[:, kc, :], start=(kc == 0), stop=(kc == NC - 1))
            last.then_inc(c["logits"].sem, 1)

            def gate_up(i, n):
                k = n % 2
                wait(pe, c["gu_low"], n + 1, i, 2)
                for s in range(NSEQ):
                    if isinstance(i, int) and i == n == 0:
                        norm.wait_parts(pe, s)
                    wait(pe, c["prod"], 2 * n - 1 + s, i, 4)
                    cut = slice(s * SEQ, (s + 1) * SEQ)
                    for which, to in enumerate((gate, up)):
                        for kc in range(NC):
                            col = slice((which * NC + kc) * FF0, (which * NC + kc + 1) * FF0)
                            pe.matmul(to[:, s, :], gu_hi[:, k, col], g.xh[:, kc, cut], start=(kc == 0), stop=False)
                            pe.matmul(to[:, s, :], gu_hi[:, k, col], g.xl[:, kc, cut], start=False, stop=False)
                            last = pe.matmul(to[:, s, :], gu_lo[:, k, col], g.xh[:, kc, cut],
                                             start=False, stop=(kc == NC - 1))
                    last.then_inc(c["inner"].sem, 1)

            def down(i, n):
                k = n % 2
                wait(pe, c["d_low"], n + 1, i, 2)
                for t in range(NT):
                    if t % 4 == 0:
                        wait(pe, c["low"], 2 * n + t // 4 + 1, i, 4)
                    if t % 2 == 0:
                        wait(pe, c["added"], 4 * n - 3 + t // 2, i, 8)
                    cut = slice(t * P, (t + 1) * P)
                    pe.matmul(outs[:, t, :], inner_hi[:, k, cut], wd_hi[:, k, :], start=True, stop=False)
                    pe.matmul(outs[:, t, :], inner_hi[:, k, cut], wd_lo[:, k, :], start=False, stop=False)
                    last = pe.matmul(outs[:, t, :], inner_lo[:, k, cut], wd_hi[:, k, :], start=False, stop=True)
                    if t % 4 == 3:
                        last.then_inc(c["down"].sem, 1)

            gate_up(0, 0)
            pe.wait_ge(c["gates"].sem, 1)
            with pe.Fori(0, LAST) as i:
                for n in range(2):
                    gate_up(i, n + 1)
                    down(i, n)
            gate_up(LAST, 1)
            down(LAST, 0)
            down(LAST, 1)

        @block.scalar
        def _(act):
            for n in ("silu", "high", "gu_high", "d_high"):
                act.sem_inc(c[n].sem, c[n].prime)

            def split_gu(i, n):
                wait(act, gu_full[n % 2], 16 * (n // 2) + 16, i, 16)
                wait(act, c["inner"], 2 * n - 2, i, 4)
                act.activation(gu_hi[:, n % 2, :], gu[:, n % 2, :], ACT.Copy).then_inc(c["gu_high"].sem, 1)

            def split_d(i, n):
                wait(act, d_full[n % 2], 16 * (n // 2) + 16, i, 16)
                wait(act, c["down"], 2 * n - 2, i, 4)
                act.activation(wd_hi[:, n % 2, :], wd[:, n % 2, :], ACT.Copy).then_inc(c["d_high"].sem, 1)

            def inner_values(i, n):
                for s in range(NSEQ):
                    wait(act, c["inner"], 2 * n + s + 1, i, 4)
                    wait(act, c["prod"], 2 * n - 1 + s, i, 4)
                    act.activation(silu[:, s, :], gate[:, s, :], ACT.Silu).then_inc(c["silu"].sem, 1)
                for s in range(NSEQ):
                    wait(act, c["prod"], 2 * n + s + 1, i, 4)
                    wait(act, c["down"], 2 * n - 3 + s, i, 4)
                    act.activation(inner_hi[:, n % 2, s * SEQ:(s + 1) * SEQ], inner[:, s, :], ACT.Copy) \
                        .then_inc(c["high"].sem, 1)

            norm.scalar(act)
            split_gu(0, 0)
            act.wait_ge(c["logits"].sem, 1)
            act.activation(score[:, :, :].rearrange("p t e -> p (t e)"), outs[:, 0, 0:NT * NE0],
                           ACT.Sigmoid).then_inc(c["gates"].sem, 1)
            split_gu(0, 1)
            split_d(0, 0)
            inner_values(0, 0)
            with act.Fori(0, LAST) as i:
                for n in range(2):
                    split_gu(i, n + 2)
                    split_d(i, n + 1)
                    inner_values(i, n + 1)
            split_d(LAST, 1)
            inner_values(LAST, 1)

        @block.gpsimd
        def _(pool):
            pool.sem_inc(c["gu_low"].sem, c["gu_low"].prime)
            pool.sem_inc(c["d_low"].sem, c["d_low"].prime)

            def split_gu(i, n):
                wait(pool, c["gu_high"], n + 1, i, 2)
                pool.tensor_tensor(gu_lo[:, n % 2, :], gu[:, n % 2, :], gu_hi[:, n % 2, :].bitcast(F32),
                                   ALU.subtract).then_inc(c["gu_low"].sem, 1)

            def split_d(i, n):
                wait(pool, c["d_high"], n + 1, i, 2)
                pool.tensor_tensor(wd_lo[:, n % 2, :], wd[:, n % 2, :], wd_hi[:, n % 2, :].bitcast(F32),
                                   ALU.subtract).then_inc(c["d_low"].sem, 1)

            split_gu(0, 0)
            split_gu(0, 1)
            split_d(0, 0)
            with pool.Fori(0, LAST) as i:
                for n in range(2):
                    split_gu(i, n + 2)
                    split_d(i, n + 1)
            split_d(LAST, 1)

        @block.vector
        def _(dve):
            for n in ("prod", "low", "added"):
                dve.sem_inc(c[n].sem, c[n].prime)

            norm.vector(dve)

            def inner_values(i, n):
                for s in range(NSEQ):
                    wait(dve, c["silu"], 2 * n + s + 1, i, 4)
                    wait(dve, c["low"], 2 * n - 1 + s, i, 4)
                    dve.tensor_tensor(inner[:, s, :], silu[:, s, :], up[:, s, :], ALU.mult) \
                        .then_inc(c["prod"].sem, 1)

            def inner_low(i, n, s):
                wait(dve, c["high"], 2 * n + s + 1, i, 4)
                cut = slice(s * SEQ, (s + 1) * SEQ)
                dve.tensor_tensor(inner_lo[:, n % 2, cut], inner[:, s, :], inner_hi[:, n % 2, cut].bitcast(F32),
                                  ALU.subtract).then_inc(c["low"].sem, 1)

            def add(i, n, half):
                for t in range(4 * half, 4 * half + 4):
                    if t % 4 == 0:
                        wait(dve, c["down"], 2 * n + t // 4 + 1, i, 4)
                    if t % 2 == 0:
                        wait(dve, c["added"], 4 * n - 3 + t // 2, i, 8)
                    e = bass.ds(2 * i + n, 1)
                    last = dve.scalar_tensor_tensor(g.x[:, t, :], outs[:, t, :], weight[:, t, e],
                                                    g.x[:, t, :], ALU.mult, ALU.add)
                    if t % 2 == 1:
                        last.then_inc(c["added"].sem, 1)

            own = [0]

            def link(op):
                own[0] += 1
                op.then_inc(c["own"].sem, 1)
                dve.wait_ge(c["own"].sem, own[0])

            dve.memset(weight[:, :, NE0:], 1.0)
            dve.wait_ge(c["gates"].sem, 1)
            for t in range(NT):
                op = dve.max(top[:, t, :], score[:, t, :])
                if t == NT - 1:
                    link(op)
            for t in range(NT):
                op = dve.match_replace(left[:, t, :], top[:, t, :], score[:, t, :], -1.0)
                if t == NT - 1:
                    link(op)
            link(dve.scalar_tensor_tensor(left[:, :, :], left[:, :, :], 0.0, score[:, :, :], ALU.is_lt, ALU.mult))
            link(dve.reduce_sum(total[:, :], left[:, :, :], axis=AX.X))
            link(dve.tensor_scalar(total[:, :], total[:, :], 1e-6, None, ALU.add))
            link(dve.reciprocal(total[:, :], total[:, :]))
            link(dve.tensor_scalar(total[:, :], total[:, :], ROUTED_SCALE, None, ALU.mult))
            link(dve.tensor_tensor(weight[:, :, 0:NE0], left[:, :, :],
                                   total[:, :].unsqueeze(2).broadcast_to([P, NT, NE0]), ALU.mult))
            inner_values(0, 0)
            inner_low(0, 0, 0)
            inner_low(0, 0, 1)
            with dve.Fori(0, LAST) as i:
                for n in range(2):
                    inner_values(i, n + 1)
                    inner_low(i, n + 1, 0)
                    inner_low(i, n + 1, 1)
                    add(i, n, 0)
                    add(i, n, 1)
            inner_values(LAST, 1)
            inner_low(LAST, 1, 0)
            inner_low(LAST, 1, 1)
            for n in range(2):
                add(LAST, n, 0)
                add(LAST, n, 1)
    finish(nc, [*c.values(), *norm.counts])


def attention(nc, g, d, name, kv_every, window, gamma=None, again=False):
    UNITS = HEADS * NSEQ
    U = 4 if kv_every == 4 else 2
    BODY = U * NSEQ
    LOOPS = HEADS // U - 1
    KVSLOTS = 2 if kv_every == 1 else 1
    NQ = SEQ // P
    groups = [[0, 1], [2, 3]] if window else [[0, 1], [2], [3]]
    NG = len(groups)
    keys = [list(range(max(0, t - 1) if window else 0, t + 1)) for t in range(NQ)]
    cols, psum_col, width = [], [], []
    for gr in groups:
        at = 0
        for t in gr:
            cols.append(sum(len(keys[s]) for s in range(t)) * P)
            psum_col.append(at)
            at += len(keys[t]) * P
        width.append(at)
    WIDTH = sum(width)

    def has_kv(m):
        return (m // NSEQ) % kv_every == 0

    def before(m, kind):
        if m < 0 and kv_every < HEADS:
            return before(m + BODY, kind) - before(BODY, kind)
        if m < 0:
            return m + NSEQ if kind == "rope" else NSEQ
        kv = sum(has_kv(j) for j in range(m))
        return kv if kind == "v" else m + kv

    per_rope = BODY if kv_every == HEADS else before(BODY, "rope")
    per_v = 0 if kv_every == HEADS else before(BODY, "v")

    c = {n: Count(nc, n, p) for n, p in (
        ("loaded", 0), ("wo_even", 0), ("wo_odd", 0), ("wo_high", 0), ("wo_low", 2), ("o_high", 0), ("o_low", 0),
        ("o_used", 0), ("wq_even", 0), ("wq_odd", 0), ("kv_even", 0), ("kv_odd", 0), ("ready", 0), ("turns", 0),
        ("wq_high", 2), ("wq_low", 2), ("wk_high", 2), ("wk_low", 2),
        ("proj", 8), ("swapped", 4), ("cosed", 6), ("sined", 4), ("rotated", 6), ("part_high", 6), ("part_low", 6),
        ("vproj", 4), ("vkept", 4), ("scores", 8), ("peak", 0), ("expd", 8), ("recip", 0), ("normed", 0), ("normed_v", 0),
        ("turned", 8), ("pt_v", 8), ("pt_a", 8), ("values", 6), ("okept", 4))}
    wq_full, kv_full = (c["wq_even"], c["wq_odd"]), (c["kv_even"], c["kv_odd"])
    VBANK = window

    with ExitStack() as ctx:
        def sb(name, shape, dtype):
            return ctx.enter_context(sbuf(nc, name, shape, dtype))

        wo = sb("wo", [P, 2, H], F32)
        wo_hi = sb("wo_hi", [P, HEADS, H], F32R)
        wo_lo = sb("wo_lo", [P, HEADS, H], F32R)
        wq = sb("wq", [P, 2, NC, P], F32)
        wkv = sb("wkv", [P, KVSLOTS, 2, NC, P], F32)
        wq_hi = sb("wq_hi", [P, 2, NC, P], F32R)
        wq_lo = sb("wq_lo", [P, 2, NC, P], F32R)
        wk_hi = sb("wk_hi", [P, KVSLOTS, NC, P], F32R)
        wk_lo = sb("wk_lo", [P, KVSLOTS, NC, P], F32R)
        ropes = sb("ropes", [P, 2, 2, SEQ], F32)
        mask1 = sb("mask1", [P, 2, P], F32)
        mask = sb("mask", [P, 2, P], BF16)
        q_parts = [sb("q_" + n, [P, NSEQ, SEQ], F32R) for n in ("hi", "lo")]
        k_parts = [sb("k_" + n, [P, NSEQ, SEQ], F32R) for n in ("hi", "lo")]
        v = sb("v", [P, NSEQ, NQ, P], F32)
        prob = sb("prob", [P, NSEQ, WIDTH], F32)
        pt = sb("pt", [P, NSEQ, NQ, SEQ], F32)
        peak = sb("peak", [P, NSEQ, NQ], F32)
        sums = sb("sums", [P, NSEQ, NQ], F32)
        recip = sb("recip", [P, NSEQ, NQ], F32)
        o = sb("o", [P, HEADS, T], F32)
        banks = ctx.enter_context(psum(nc, "banks", [P, 8, SEQ], F32))
        block = ctx.enter_context(nc.Block())

        norm = Norm(nc, g, banks[:, 0:4, :].rearrange("p (c s) n -> p c (s n)", c=NC), gamma=gamma, again=again,
                    split=True)
        wo_full = (c["wo_even"], c["wo_odd"])
        WO = HEADS // 2
        o_stage = [part[:, :, :].rearrange("p k (h n) -> p k h n", n=P) for part in (g.xh, g.xl)]
        swap, cosed = (g.xn[:, 4 * a:4 * a + 4, :].rearrange("p (b t) h -> p b (t h)", b=2) for a in range(2))
        s_bank = [banks[:, j, :] for j in range(NG)]
        t_bank = [banks[:, 3 + j, :] for j in range(2)]
        p_bank = [banks[:, 5 + j, :] for j in range(2)]
        o_bank = banks[:, 7, :]
        v_bank = banks[:, 2, :] if VBANK else o_bank
        NPOOL = 2
        mover = ["v", "a"] if window else ["v", "v", "a"]

        def turned_by(n, gi):
            own = [j for j in range(NG) if mover[j] == mover[gi]]
            return c["pt_" + mover[gi]], n * len(own) + own.index(gi) + 1, BODY * len(own)

        @block.sync
        def _(sp):
            sp.dma_start(ropes[:, 0], d["rope_q"]).then_inc(c["loaded"].sem, 16)
            sp.dma_start(ropes[:, 1], d["rope_k"]).then_inc(c["loaded"].sem, 16)
            sp.dma_start(mask1[:, :, :], d["mask"].rearrange("p (a n) -> p a n", a=2)).then_inc(c["loaded"].sem, 16)

            def load(i, h):
                at = bass.ds(i * U + h, 1) if not isinstance(i, int) else slice(i * U + h, i * U + h + 1)
                wait(sp, c["wq_low"], h - 1, i, U)
                sp.dma_start(wq[:, h % 2], d[name + "_q"][at].rearrange("o p c n -> p (o c) n")) \
                    .then_inc(wq_full[h % 2].sem, 16)
                wait(sp, c["wo_low"], h - 1, i, U)
                sp.dma_start(wo[:, h % 2:h % 2 + 1, :], d[name + "_o"][:, at, :]).then_inc(wo_full[h % 2].sem, 16)
                if has_kv(NSEQ * h) and kv_every < HEADS:
                    kvh = h // kv_every
                    at = bass.ds(i * (U // kv_every) + kvh, 1)
                    wait(sp, c["vproj"], NSEQ * (kvh + 1 - KVSLOTS), i, per_v)
                    sp.dma_start(wkv[:, kvh % KVSLOTS].rearrange("p a c n -> p (a c) n"),
                                 d[name + "_kv"][at].rearrange("o p a c n -> p (o a c) n")) \
                        .then_inc(kv_full[kvh % KVSLOTS].sem, 16)

            if kv_every == HEADS:
                sp.dma_start(wkv[:, 0].rearrange("p a c n -> p (a c) n"),
                             d[name + "_kv"][0:1].rearrange("o p a c n -> p (o a c) n")).then_inc(kv_full[0].sem, 16)
            with sp.Fori(0, HEADS // U) as i:
                for h in range(U):
                    load(i, h)

        @block.tensor
        def _(pe):
            for n in ("proj", "vproj", "scores", "turned", "values"):
                pe.sem_inc(c[n].sem, c[n].prime)
            norm.tensor(pe)
            norm.wait_parts(pe)
            pe.wait_ge(c["ready"].sem, 1)

            def rope_unit(i, m, which):
                s = m % NSEQ
                r = before(m, "rope") + which
                wait(pe, c["cosed"], r - 1, i, per_rope)
                if which == 0:
                    h = m // NSEQ
                    wait(pe, c["wq_low"], h + 1, i, U)
                    hi, lo = wq_hi[:, h % 2], wq_lo[:, h % 2]
                else:
                    kvh = m // NSEQ // kv_every
                    wait(pe, c["wk_low"], kvh + 1, i, U // kv_every)
                    hi, lo = wk_hi[:, kvh % KVSLOTS], wk_lo[:, kvh % KVSLOTS]
                cut = slice(s * SEQ, (s + 1) * SEQ)
                for kc in range(NC):
                    pe.matmul(p_bank[r % 2], hi[:, kc, :], g.xh[:, kc, cut], start=(kc == 0), stop=False)
                    pe.matmul(p_bank[r % 2], hi[:, kc, :], g.xl[:, kc, cut], start=False, stop=False)
                    last = pe.matmul(p_bank[r % 2], lo[:, kc, :], g.xh[:, kc, cut], start=False, stop=(kc == NC - 1))
                last.then_inc(c["proj"].sem, 1)

            def value_unit(i, m):
                s = m % NSEQ
                kvh = m // NSEQ // kv_every
                wait(pe, kv_full[kvh % KVSLOTS], 16 * (kvh // KVSLOTS) + 16, i, 16 * (U // kv_every) // KVSLOTS)
                wait(pe, c["vkept"], before(m, "v"), i, per_v)
                if not VBANK:
                    wait(pe, c["okept"], m - 1, i, BODY)
                for t in range(NQ):
                    for kc in range(NC):
                        last = pe.matmul(v_bank[:, t * P:(t + 1) * P],
                                         g.xt[:, kc, s * SEQ + t * P:s * SEQ + (t + 1) * P],
                                         wkv[:, kvh % KVSLOTS, 1, kc, :], start=(kc == 0), stop=(kc == NC - 1))
                last.then_inc(c["vproj"].sem, 1)

            def score(i, m, gi):
                s = m % NSEQ
                if gi == 0:
                    r = before(m + 1, "rope") if m >= 0 else 0
                    wait(pe, c["part_low"], r, i, per_rope)
                wait(pe, c["expd"], NG * (m - 1) + gi + 1, i, NG * BODY)
                for t in groups[gi]:
                    out = s_bank[gi][:, psum_col[t]:psum_col[t] + len(keys[t]) * P]
                    n = max(len(keys[t]), 2) * P
                    wide = s_bank[gi][:, psum_col[t]:psum_col[t] + n]
                    q_hi, q_lo = (part[:, s, t * P:(t + 1) * P] for part in q_parts)
                    k_hi, k_lo = (part[:, s, keys[t][0] * P:keys[t][0] * P + n] for part in k_parts)
                    pe.matmul(wide, q_hi, k_hi, start=True, stop=False)
                    pe.matmul(wide, q_hi, k_lo, start=False, stop=False)
                    pe.matmul(wide, q_lo, k_hi, start=False, stop=False)
                    lo = 0 if window and len(keys[t]) == 2 else 1
                    last = pe.matmul(out[:, (len(keys[t]) - 2 + lo) * P:], g.identb[:, :],
                                     mask[:, lo:, :].rearrange("p a n -> p (a n)"), start=False, stop=True)
                last.then_inc(c["scores"].sem, 1)

            def turn(i, n, gi):
                s = n % NSEQ
                if gi < NPOOL:
                    wait(pe, c["normed"], NPOOL * n + gi + 1, i, NPOOL * BODY)
                else:
                    wait(pe, c["normed_v"], n + 1, i, BODY)
                j = NG * n + gi - 2
                cnt, at, per = turned_by(j // NG, j % NG)
                wait(pe, cnt, at, i, per)
                at = 0
                for t in groups[gi]:
                    for x in range(len(keys[t])):
                        last = pe.transpose(t_bank[(NG * n + gi) % 2][:, at:at + P],
                                            prob[:, s, cols[t] + x * P:cols[t] + (x + 1) * P], g.ident[:, :])
                        at += P
                last.then_inc(c["turned"].sem, 1)

            def sum_values(i, n):
                s = n % NSEQ
                for e in ("v", "a"):
                    own = [j for j in range(NG) if mover[j] == e]
                    wait(pe, c["pt_" + e], (n + 1) * len(own), i, BODY * len(own))
                wait(pe, c["okept"], n, i, BODY)
                wait(pe, c["vkept"], before(n + 1, "v"), i, per_v)
                if not VBANK:
                    m = min(n + 2, UNITS - i * BODY) if isinstance(i, int) else n + 2
                    wait(pe, c["vkept"], before(m, "v"), i, per_v)
                order = [0, 2, 1, 3] if window else list(range(NQ))
                for j, x in enumerate(order):
                    to = min(x + 2, NQ) * P if window else SEQ
                    last = pe.matmul(o_bank[:, x * P:to], v[:, s, x, :], pt[:, s, x, x * P:to],
                                     start=(j == 0), stop=(j == NQ - 1))
                last.then_inc(c["values"].sem, 1)

            def slot(i, n):
                static = isinstance(i, int)
                live = lambda m: not static or 0 <= i * BODY + m < UNITS
                kv = lambda m: has_kv(m) and (kv_every < HEADS or static and i * BODY + m < NSEQ)
                for gi in range(NG):
                    if live(n + 1):
                        score(i, n + 1, gi)
                    if live(n):
                        turn(i, n, gi)
                if live(n + 3):
                    rope_unit(i, n + 3, 0)
                    if kv(n + 3):
                        rope_unit(i, n + 3, 1)
                if live(n):
                    sum_values(i, n)
                if live(n + 2) and kv(n + 2):
                    value_unit(i, n + 2)

            for n in range(-3, 0):
                slot(0, n)
            with pe.Fori(0, LOOPS) as i:
                for n in range(BODY):
                    slot(i, n)
            for n in range(BODY):
                slot(LOOPS, n)
            for u in range(2 * NT):
                t, half = u // 2, u % 2
                wait(pe, c["wo_low"], HEADS)
                wait(pe, c["o_low"], u + 1)
                to = banks[:, t // 2, (t % 2) * H:(t % 2 + 1) * H]
                for h in range(WO):
                    o_hi, o_lo = (part[:, half, h, :] for part in o_stage)
                    hi, lo = (w[:, half * WO + h, :] for w in (wo_hi, wo_lo))
                    pe.matmul(to, o_hi, hi, start=(half == h == 0), stop=False)
                    pe.matmul(to, o_hi, lo, start=False, stop=False)
                    last = pe.matmul(to, o_lo, hi, start=False, stop=(half == 1 and h == WO - 1))
                last.then_inc(c["o_used"].sem, 1)

        def o_half(u):
            return o[:, (u % 2) * WO:(u % 2 + 1) * WO, u // 2 * P:(u // 2 + 1) * P]

        def head_at(i, h):
            return bass.ds(i * U + h, 1) if not isinstance(i, int) else slice(i * U + h, i * U + h + 1)

        def move_turned(eng, i, n, gi):
            s = n % NSEQ
            wait(eng, c["turned"], NG * n + gi + 1, i, NG * BODY)
            wait(eng, c["values"], n - 1, i, BODY)
            at = 0
            for t in groups[gi]:
                m = len(keys[t])
                src = t_bank[(NG * n + gi) % 2][:, at:at + m * P].rearrange("p (k q) -> p k q", q=P)
                dst = pt[:, s, keys[t][0]:keys[t][-1] + 1, t * P:(t + 1) * P]
                if mover[gi] == "v":
                    last = eng.tensor_copy(dst, src)
                else:
                    last = eng.activation(dst, src, ACT.Copy)
                at += m * P
            last.then_inc(c["pt_" + mover[gi]].sem, 1)

        @block.scalar
        def _(act):
            for n in ("swapped", "part_high", "expd", "pt_a", "okept", "vkept", "wq_high", "wk_high"):
                act.sem_inc(c[n].sem, c[n].prime)

            def weights_high(i, m):
                h = m // NSEQ
                wait(act, wq_full[h % 2], 16 * (h // 2) + 16, i, 16 * U // 2)
                wait(act, c["proj"], before(m - 3, "rope") + 1, i, per_rope)
                act.activation(wq_hi[:, h % 2], wq[:, h % 2], ACT.Copy).then_inc(c["wq_high"].sem, 1)
                wait(act, wo_full[h % 2], 16 * (h // 2) + 16, i, 16 * U // 2)
                act.activation(wo_hi[:, head_at(i, h), :], wo[:, h % 2:h % 2 + 1, :], ACT.Copy) \
                    .then_inc(c["wo_high"].sem, 1)
                if has_kv(m) and (kv_every < HEADS or m == 0):
                    kvh = h // kv_every
                    wait(act, kv_full[kvh % KVSLOTS], 16 * (kvh // KVSLOTS) + 16, i, 16 * (U // kv_every) // KVSLOTS)
                    wait(act, c["proj"], before((kvh - KVSLOTS) * kv_every * NSEQ + 1, "rope") + 2, i, per_rope)
                    act.activation(wk_hi[:, kvh % KVSLOTS], wkv[:, kvh % KVSLOTS, 0], ACT.Copy) \
                        .then_inc(c["wk_high"].sem, 1)

            def swap_halves(i, m, which):
                r = before(m, "rope") + which
                wait(act, c["proj"], r + 1, i, per_rope)
                wait(act, c["rotated"], r - 1, i, per_rope)
                act.activation(swap[0:P // 2, r % 2, :], p_bank[r % 2][P // 2:P, :], ACT.Copy)
                act.activation(swap[P // 2:P, r % 2, :], p_bank[r % 2][0:P // 2, :], ACT.Copy) \
                    .then_inc(c["swapped"].sem, 1)

            def rope_high(i, m, which):
                r = before(m, "rope") + which
                wait(act, c["rotated"], r + 1, i, per_rope)
                wait(act, c["scores"], NG * (m - 1), i, NG * BODY)
                act.activation((k_parts if which else q_parts)[0][:, m % NSEQ, :], cosed[:, r % 2, :], ACT.Copy) \
                    .then_inc(c["part_high"].sem, 1)

            def exps(i, m, gi):
                s = m % NSEQ
                wait(act, c["peak"], NG * m + gi + 1, i, NG * BODY)
                wait(act, c["turned"], NG * (m - 2) + gi + 1, i, NG * BODY)
                for t in groups[gi]:
                    n = len(keys[t]) * P
                    last = act.activation(prob[:, s, cols[t]:cols[t] + n], s_bank[gi][:, psum_col[t]:psum_col[t] + n],
                                          ACT.Exp, bias=peak[:, s, t:t + 1], accum_out=sums[:, s, t:t + 1])
                last.then_inc(c["expd"].sem, 1)

            def slot(i, n):
                static = isinstance(i, int)
                live = lambda m: not static or 0 <= i * BODY + m < UNITS
                kv = lambda m: has_kv(m) and (kv_every < HEADS or static and i * BODY + m < NSEQ)
                if n % NSEQ == 0 and live(n + 4):
                    weights_high(i, n + 4)
                for gi in range(NG):
                    if gi == NG - 1 and live(n):
                        move_turned(act, i, n, NG - 1)
                    if live(n + 1):
                        exps(i, n + 1, gi)
                if live(n + 2):
                    rope_high(i, n + 2, 0)
                    if kv(n + 2):
                        rope_high(i, n + 2, 1)
                if live(n + 3):
                    swap_halves(i, n + 3, 0)
                    if kv(n + 3):
                        swap_halves(i, n + 3, 1)
                if live(n):
                    wait(act, c["values"], n + 1, i, BODY)
                    h = n // NSEQ
                    s = n % NSEQ
                    at = bass.ds(i * U + h, 1) if not static else slice(i * U + h, i * U + h + 1)
                    act.activation(o[:, at, s * SEQ:(s + 1) * SEQ].rearrange("p a n -> p (a n)"), o_bank,
                                   ACT.Copy).then_inc(c["okept"].sem, 1)
                if live(n + 2) and kv(n + 2):
                    m = n + 2
                    wait(act, c["vproj"], before(m, "v") + 1, i, per_v)
                    wait(act, c["values"], m - 1, i, BODY)
                    act.activation(v[:, m % NSEQ].rearrange("p t n -> p (t n)"), v_bank, ACT.Copy) \
                        .then_inc(c["vkept"].sem, 1)

            def o_high(u):
                wait(act, c["proj"], before(BODY, "rope") + LOOPS * per_rope)
                wait(act, c["okept"], UNITS - 1 if u < NT else UNITS)
                wait(act, c["o_used"], u - 1)
                act.activation(o_stage[0][:, u % 2], o_half(u), ACT.Copy).then_inc(c["o_high"].sem, 1)

            norm.scalar(act)
            weights_high(0, 0)
            for n in range(-3, 0):
                slot(0, n)
            with act.Fori(0, LOOPS) as i:
                for n in range(BODY):
                    slot(i, n)
            for n in range(BODY):
                slot(LOOPS, n)
                if n == BODY - 2:
                    for u in range(2):
                        o_high(u)
            for u in range(2, 2 * NT):
                o_high(u)

        @block.vector
        def _(dve):
            norm.vector(dve)
            dve.wait_ge(c["loaded"].sem, 48)
            dve.tensor_scalar(mask[:, :, :], mask1[:, :, :], NEG, None, ALU.mult) \
                .then_inc(c["ready"].sem, 1)
            for n in ("cosed", "sined", "part_low", "pt_v", "wo_low"):
                dve.sem_inc(c[n].sem, c[n].prime)

            def peaks(i, m, gi):
                s = m % NSEQ
                wait(dve, c["scores"], NG * m + gi + 1, i, NG * BODY)
                wait(dve, c["expd"], NG * (m - 2) + gi + 1, i, NG * BODY)
                for t in groups[gi]:
                    last = dve.reduce_max(peak[:, s, t:t + 1],
                                          s_bank[gi][:, psum_col[t]:psum_col[t] + len(keys[t]) * P],
                                          axis=AX.X, negate=True)
                last.then_inc(c["peak"].sem, 1)

            def recips(i, m, gi):
                s = m % NSEQ
                wait(dve, c["expd"], NG * m + gi + 1, i, NG * BODY)
                cut = slice(groups[gi][0], groups[gi][-1] + 1)
                dve.reciprocal(recip[:, s, cut], sums[:, s, cut]).then_inc(c["recip"].sem, 1)

            def rope_low(i, m, which):
                s = m % NSEQ
                r = before(m, "rope") + which
                hi, lo = k_parts if which else q_parts
                wait(dve, c["part_high"], r + 1, i, per_rope)
                dve.tensor_tensor(lo[:, s, :], cosed[:, r % 2, :], hi[:, s, :].bitcast(F32), ALU.subtract) \
                    .then_inc(c["part_low"].sem, 1)

            def rotate(i, m, which):
                r = before(m, "rope") + which
                wait(dve, c["swapped"], r + 1, i, per_rope)
                wait(dve, c["part_low"], r - 1, i, per_rope)
                dve.tensor_tensor(cosed[:, r % 2, :], p_bank[r % 2], ropes[:, which, 0, :], ALU.mult) \
                    .then_inc(c["cosed"].sem, 1)
                dve.tensor_tensor(swap[:, r % 2, :], swap[:, r % 2, :], ropes[:, which, 1, :], ALU.mult) \
                    .then_inc(c["sined"].sem, 1)

            def slot(i, n):
                static = isinstance(i, int)
                live = lambda m: not static or 0 <= i * BODY + m < UNITS
                kv = lambda m: has_kv(m) and (kv_every < HEADS or static and i * BODY + m < NSEQ)
                for gi in range(NG):
                    if live(n + 1):
                        peaks(i, n + 1, gi)
                        if gi:
                            recips(i, n + 1, gi - 1)
                    if live(n) and mover[gi] == "v":
                        move_turned(dve, i, n, gi)
                if live(n + 1):
                    recips(i, n + 1, NG - 1)
                    if NG > NPOOL:
                        m, s = n + 1, (n + 1) % NSEQ
                        wait(dve, c["recip"], NG * (m + 1), i, NG * BODY)
                        for t in groups[-1]:
                            row = prob[:, s, cols[t]:cols[t] + len(keys[t]) * P]
                            dve.tensor_scalar(row, row, recip[:, s, t:t + 1], None, ALU.mult) \
                                .then_inc(c["normed_v"].sem, 1)
                if live(n + 2):
                    rope_low(i, n + 2, 0)
                    if kv(n + 2):
                        rope_low(i, n + 2, 1)
                if live(n + 3):
                    rotate(i, n + 3, 0)
                    if kv(n + 3):
                        rotate(i, n + 3, 1)
                if n % NSEQ == 0 and live(n + 4):
                    out_low(i, n + 4)

            def out_low(i, m):
                h = m // NSEQ
                wait(dve, c["wo_high"], h + 1, i, U)
                dve.tensor_tensor(wo_lo[:, head_at(i, h), :], wo[:, h % 2:h % 2 + 1, :],
                                  wo_hi[:, head_at(i, h), :].bitcast(F32), ALU.subtract).then_inc(c["wo_low"].sem, 1)

            def o_low(u):
                wait(dve, c["o_high"], u + 1)
                dve.tensor_tensor(o_stage[1][:, u % 2], o_half(u), o_stage[0][:, u % 2].bitcast(F32), ALU.subtract) \
                    .then_inc(c["o_low"].sem, 1)

            out_low(0, 0)
            for n in range(-3, 0):
                slot(0, n)
            with dve.Fori(0, LOOPS) as i:
                for n in range(BODY):
                    slot(i, n)
            for n in range(BODY):
                slot(LOOPS, n)
                if n == BODY - 2:
                    for u in range(2):
                        o_low(u)

            def add_out(pair):
                dve.wait_ge(c["o_used"].sem, 4 * (pair + 1))
                x2 = g.x[:, 2 * pair:2 * pair + 2, :].rearrange("p a h -> p (a h)")
                dve.tensor_tensor(x2, x2, banks[:, pair, :], ALU.add)

            for u in range(2, 2 * NT):
                o_low(u)
                if u >= 5 and u % 4 == 1:
                    add_out(u // 4 - 1)
            add_out(NT // 2 - 1)

        @block.gpsimd
        def _(pool):
            for n in ("rotated", "wq_low", "wk_low"):
                pool.sem_inc(c[n].sem, c[n].prime)

            def weights_low(i, m):
                h = m // NSEQ
                wait(pool, c["wq_high"], h + 1, i, U)
                pool.tensor_tensor(wq_lo[:, h % 2], wq[:, h % 2], wq_hi[:, h % 2].bitcast(F32), ALU.subtract) \
                    .then_inc(c["wq_low"].sem, 1)
                if has_kv(m) and (kv_every < HEADS or m == 0):
                    kvh = h // kv_every
                    k = kvh % KVSLOTS
                    wait(pool, c["wk_high"], kvh + 1, i, U // kv_every)
                    pool.tensor_tensor(wk_lo[:, k], wkv[:, k, 0], wk_hi[:, k].bitcast(F32), ALU.subtract) \
                        .then_inc(c["wk_low"].sem, 1)

            def norms(i, m, gi):
                s = m % NSEQ
                wait(pool, c["recip"], NG * m + gi + 1, i, NG * BODY)
                pool.sem_inc(c["turns"].sem, 1)
                for t in groups[gi]:
                    part = prob[:, s, cols[t]:cols[t] + len(keys[t]) * P]
                    last = pool.tensor_scalar(part, part, recip[:, s, t:t + 1], None, ALU.mult)
                last.then_inc(c["normed"].sem, 1)

            def rotated(i, m, which):
                r = before(m, "rope") + which
                wait(pool, c["sined"], r + 1, i, per_rope)
                wait(pool, c["cosed"], r + 1, i, per_rope)
                pool.tensor_tensor(cosed[:, r % 2, :], cosed[:, r % 2, :], swap[:, r % 2, :], ALU.add) \
                    .then_inc(c["rotated"].sem, 1)

            def slot(i, n):
                static = isinstance(i, int)
                live = lambda m: not static or 0 <= i * BODY + m < UNITS
                kv = lambda m: has_kv(m) and (kv_every < HEADS or static and i * BODY + m < NSEQ)
                if n % NSEQ == 0 and live(n + 4):
                    weights_low(i, n + 4)
                if live(n + 1):
                    for gi in range(NPOOL):
                        norms(i, n + 1, gi)
                if live(n + 3):
                    rotated(i, n + 3, 0)
                    if kv(n + 3):
                        rotated(i, n + 3, 1)

            weights_low(0, 0)
            for n in range(-3, 0):
                slot(0, n)
            with pool.Fori(0, LOOPS) as i:
                for n in range(BODY):
                    slot(i, n)
            for n in range(BODY):
                slot(LOOPS, n)
    finish(nc, [*c.values(), *norm.counts])


def capacity_mixture(nc, g, d):
    c = {n: Count(nc, n, p) for n, p in (
        ("loaded", 0), ("own_v", 0), ("logits", 0), ("shared_w", 0), ("peak", 0), ("expd", 0), ("masked", 0),
        ("places", 0), ("sparts", 0), ("routed", 0), ("sinner", 0), ("ssilu", 0), ("sprod", 0), ("shigh", 0), ("slow", 0),
        ("sw_high", 0), ("sw_low", 0), ("xpart", 0), ("xrest", 0),
        ("gu_even", 0), ("gu_odd", 0), ("d_even", 0), ("d_odd", 0),
        ("picked", 4), ("paired", 4), ("gathered", 4), ("weighed", 4), ("buffered", 4), ("sloted", 4), ("spread0", 4), ("spread1", 4),
        ("kept0", 4), ("kept1", 4), ("inner", 4), ("silu", 4), ("acted", 4), ("turned", 4), ("moved", 4),
        ("down", 4), ("split", 4), ("summed", 4), ("chain", 0), ("parted", 0))}
    gu_full, d_full = (c["gu_even"], c["gu_odd"]), (c["d_even"], c["d_odd"])
    SENTINEL = 2.0
    BODY = 2
    LOOPS = NG1 // BODY - 1
    with ExitStack() as ctx:
        def sb(name, shape, dtype):
            return ctx.enter_context(sbuf(nc, name, shape, dtype))

        router = sb("router", [P, NC, NE1], F32)
        ranks1 = sb("ranks", [P, 2 * P], F32)
        ranks = sb("ranks_b", [P, 2 * P], BF16)
        slot1 = sb("slot1", [P, CAP], F32)
        own = sb("own", [P, GE * 3], F32)
        peak = sb("peak", [P, NT], F32)
        sums = sb("sums", [P, NT], F32)
        score = sb("score", [P, NT, NE1 + 2], F32)
        left = sb("left", [P, NT, NE1 + 2], F32)
        top = sb("top", [P, NT, 8], F32)
        maskb = sb("maskb", [P, NT, NE1], BF16)
        prior = sb("prior", [P, NT, NE1], BF16)
        place = sb("place", [P, NT, NE1], F32)
        wrest = sb("wrest", [P, NT, NE1], F32)
        wpart = sb("wpart", [P, NT, NE1], BF16)
        wparts = sb("wparts", [P, NT, NE1, 3], BF16)
        x_hi = sb("x_hi", [P, NT, H], F32R)
        x_lo = sb("x_lo", [P, NT, H], F32R)
        shgu, shgu_hi, shgu_lo = (sb("shgu", [P, 2, NC, NSH * P], dt) for dt in (F32, F32R, F32R))
        shd, shd_hi, shd_lo = (sb("shd", [P, NSH, H], dt) for dt in (F32, F32R, F32R))
        shsilu = sb("shsilu", [P, 2, SEQ], F32)
        shinner = sb("shinner", [P, 2, SEQ], F32)
        shin_hi = sb("shin_hi", [P, NSH, T], F32R)
        shin_lo = sb("shin_lo", [P, NSH, T], F32R)
        wgu = sb("wgu", [P, 2, GE, NC, 2 * FF1], F32)
        wd = sb("wd", [HF1, 2, GE, 2, H], F32)
        pick = sb("pick", [P, 2, NT, P], BF16)
        pair = sb("pair", [P, NT, 2 * P], F32R)
        pickt = sb("pickt", [P, 2, T], F32R)
        buf = sb("buf", [P, NC, 2 * P], F32)
        wtmp = sb("wtmp", [P, 2, GE * 3], F32)
        wslot = sb("wslot", [P, 2], F32)
        silu = sb("silu", [P, FF1], F32)
        acted = sb("acted", [P, FF1], F32)
        actt = sb("actt", [HF1, 2, P], F32)
        y = sb("y", [P, H], F32)
        yparts = sb("yparts", [P, 2, 2, H], F32R)
        acc = ctx.enter_context(psum(nc, "acc", [P, NT, H], F32))
        banks = ctx.enter_context(psum(nc, "banks", [P, 4, SEQ], F32))
        block = ctx.enter_context(nc.Block())
        b_gather, b_spread = banks[:, 0, :], banks[:, 1, :]
        b_inner, b_weight = banks[:, 2, 0:2 * FF1], banks[:, 2, 2 * FF1:2 * FF1 + GE * 3]
        b_turn, b_out = banks[0:HF1, 3, 0:2 * P], banks[:, 3, H:2 * H]
        norm = Norm(nc, g, banks[:, :, :].rearrange("p (c s) n -> p c (s n)", c=NC), split=True)
        wparts_g = wparts[:, :, :, :].rearrange("p t (n e) c -> p t n (e c)", e=GE)
        b_sh = acc[:, :, :].rearrange("p (b s) h -> p b (s h)", s=2)

        @block.sync
        def _(sp):
            for to, name in ((router[:, :, :], "router1"), (ranks1[:, :], "before"), (slot1[:, :], "slot1"),
                             (own[:, :], "own")):
                sp.dma_start(to, d[name]).then_inc(c["loaded"].sem, 16)
            sp.dma_start(shgu[:, :, :, :], d["shared1_gu"].rearrange("p a c n -> p a c n")).then_inc(c["shared_w"].sem, 16)
            sp.dma_start(shd[:, :, :], d["shared1_d"]).then_inc(c["shared_w"].sem, 16)
            with sp.Fori(0, NG1 // BODY) as i:
                for k in range(BODY):
                    at = bass.ds(BODY * i + k, 1)
                    wait(sp, c["inner"], k - 1, i, BODY)
                    sp.dma_start(wgu[:, k], d["w1_gu"][at].rearrange("o p e c n -> p (o e) c n")) \
                        .then_inc(gu_full[k].sem, 16)
                    wait(sp, c["down"], k - 1, i, BODY)
                    sp.dma_start(wd[:, k], d["w1_d"][at].rearrange("o p e c n -> p (o e) c n")) \
                        .then_inc(d_full[k].sem, 16)

        def live(i, m):
            return not isinstance(i, int) or 0 <= i * BODY + m < NG1

        @block.tensor
        def _(pe):
            for n in ("inner", "down", "gathered", "weighed", "spread0", "spread1", "turned", "summed"):
                pe.sem_inc(c[n].sem, c[n].prime)
            norm.tensor(pe)
            norm.wait_xt(pe)
            pe.wait_ge(c["loaded"].sem, 64)
            for t in range(NT):
                for kc in range(NC):
                    last = pe.matmul(banks[:, 0, t * NE1:(t + 1) * NE1], g.xt[:, kc, t * P:(t + 1) * P],
                                     router[:, kc, :], start=(kc == 0), stop=(kc == NC - 1))
            last.then_inc(c["logits"].sem, 1)
            def count_places():
                pe.wait_ge(c["masked"].sem, 1)
                for t in range(NT):
                    pe.matmul(banks[:, 1, t * NE1:(t + 1) * NE1], ranks[:, 0:P], maskb[:, t, :], start=True, stop=False)
                    last = pe.matmul(banks[:, 1, t * NE1:(t + 1) * NE1], ranks[:, P:], prior[:, t, :],
                                     start=False, stop=True)
                last.then_inc(c["places"].sem, 1)

            norm.wait_parts(pe)
            pe.wait_ge(c["sw_low"].sem, 1)
            for j in range(NSH):
                for s in range(NSEQ):
                    n = j * NSEQ + s
                    if n == 4:
                        count_places()
                    wait(pe, c["sprod"], n - 1)
                    cut, col = slice(s * SEQ, (s + 1) * SEQ), slice(j * P, (j + 1) * P)
                    for which in range(2):
                        to = b_sh[:, (n % 2) * 2 + which, :]
                        for kc in range(NC):
                            hi, lo = shgu_hi[:, which, kc, col], shgu_lo[:, which, kc, col]
                            pe.matmul(to, hi, g.xh[:, kc, cut], start=(kc == 0), stop=False)
                            pe.matmul(to, hi, g.xl[:, kc, cut], start=False, stop=False)
                            last = pe.matmul(to, lo, g.xh[:, kc, cut], start=False, stop=(kc == NC - 1))
                    last.then_inc(c["sinner"].sem, 1)
            wait(pe, c["sprod"], NSH * NSEQ)
            pe.wait_ge(c["sw_low"].sem, 2)
            for t in range(NT):
                if t % (NT // NSEQ) == 0:
                    wait(pe, c["slow"], (NSH - 1) * NSEQ + t // (NT // NSEQ) + 1)
                cut = slice(t * P, (t + 1) * P)
                for j in range(NSH):
                    pe.matmul(acc[:, t, :], shin_hi[:, j, cut], shd_hi[:, j, :],
                              start=(j == 0 and t % 2 == 0), stop=True, skip_group_check=True)
                    pe.matmul(acc[:, t, :], shin_hi[:, j, cut], shd_lo[:, j, :], start=False, stop=True,
                              skip_group_check=True)
                    pe.matmul(acc[:, t, :], shin_lo[:, j, cut], shd_hi[:, j, :], start=False, stop=True,
                              skip_group_check=True)
            pe.wait_ge(c["parted"].sem, 1)

            def gather(i, q):
                wait(pe, c["paired"], 2 * q + 2, i, 2)
                wait(pe, c["buffered"], q, i, 1)
                for hc in range(NC):
                    for t in range(NT):
                        for part in (x_hi, x_lo):
                            last = pe.matmul(b_gather[:, hc * 2 * P:(hc + 1) * 2 * P], part[:, t, hc * P:(hc + 1) * P],
                                             pair[:, t, :], start=(t == 0 and part is x_hi),
                                             stop=(t == NT - 1 and part is x_lo))
                last.then_inc(c["gathered"].sem, 1)

            def weigh(i, m):
                k = m % 2
                wait(pe, c["sloted"], m, i, BODY)
                at = bass.ds(BODY * i + m, 1) if not isinstance(i, int) else slice(BODY * i + m, BODY * i + m + 1)
                for t in range(NT):
                    last = pe.matmul(b_weight, pick[:, k, t, :], wparts_g[:, t, at, :].rearrange("p o w -> p (o w)"),
                                     start=(t == 0), stop=(t == NT - 1))
                last.then_inc(c["weighed"].sem, 1)

            def spread(i, m, half):
                k = m % 2
                if half == 0:
                    wait(pe, c["picked"], m + 1, i, BODY)
                wait(pe, c["kept1" if half == 0 else "kept0"], m + half, i, BODY)
                for j in range(4):
                    t = 4 * half + j
                    last = pe.matmul(b_spread[:, j * P:(j + 1) * P], pick[:, k, t, :], g.identb[:, :],
                                     start=True, stop=True)
                last.then_inc(c[f"spread{half}"].sem, 1)

            def inner(i, n):
                k = n % 2
                wait(pe, gu_full[k], 16 * (n // 2) + 16, i, 16)
                wait(pe, c["buffered"], n // 2 + 1, i, 1)
                wait(pe, c["acted"], n, i, BODY)
                wait(pe, c["sloted"], n + 1, i, BODY)
                for kc in range(NC):
                    for e in range(GE):
                        last = pe.matmul(b_inner[e * CAP:(e + 1) * CAP, :], buf[:, kc, k * P + e * CAP:k * P + (e + 1) * CAP],
                                         wgu[:, k, e, kc, :], start=(kc == 0), stop=(kc == NC - 1),
                                         tile_position=(0, e * CAP))
                last.then_inc(c["inner"].sem, 1)

            def turn(i, n):
                wait(pe, c["acted"], n + 1, i, BODY)
                wait(pe, c["split"], n, i, BODY)
                for j in range(2):
                    last = pe.transpose(b_turn[:, j * P:(j + 1) * P], acted[:, j * HF1:(j + 1) * HF1], g.ident[:, :])
                last.then_inc(c["turned"].sem, 1)

            def down(i, n):
                k = n % 2
                wait(pe, d_full[k], 16 * (n // 2) + 16, i, 16)
                wait(pe, c["moved"], n + 1, i, BODY)
                for j in range(2):
                    for e in range(GE):
                        last = pe.matmul(b_out[e * CAP:(e + 1) * CAP, :], actt[:, j, e * CAP:(e + 1) * CAP],
                                         wd[:, k, e, j, :], start=(j == 0), stop=(j == 1),
                                         tile_position=(0, e * CAP))
                last.then_inc(c["down"].sem, 1)

            def sum_up(i, n):
                k = n % 2
                wait(pe, c["split"], n + 1, i, BODY)
                wait(pe, c["kept0"], n + 1, i, BODY)
                wait(pe, c["kept1"], n + 1, i, BODY)
                for t in range(NT):
                    for part in range(2):
                        last = pe.matmul(acc[:, t, :], pickt[:, k, t * P:(t + 1) * P], yparts[:, k, part, :],
                                         start=False, stop=True, skip_group_check=True)
                last.then_inc(c["summed"].sem, 1)

            def slot(i, n):
                if live(i, n):
                    inner(i, n)
                if live(i, n + 1):
                    spread(i, n + 1, 0)
                if live(i, n - 1):
                    sum_up(i, n - 1)
                if n % 2 == 1 and live(i, n + 1):
                    gather(i, (n + 1) // 2)
                if live(i, n):
                    turn(i, n)
                if live(i, n + 1):
                    weigh(i, n + 1)
                    spread(i, n + 1, 1)
                if live(i, n):
                    down(i, n)

            slot(0, -1)
            slot(0, 0)
            slot(0, 1)
            with pe.Fori(1, LOOPS) as i:
                for n in range(BODY):
                    slot(i, n)
            for n in range(BODY + 1):
                slot(LOOPS, n)

        @block.scalar
        def _(act):
            for n in ("buffered", "silu", "moved", "kept1"):
                act.sem_inc(c[n].sem, c[n].prime)
            norm.scalar(act)
            act.wait_ge(c["peak"].sem, 1)
            for t in range(NT):
                last = act.activation(score[:, t, 0:NE1], banks[:, 0, t * NE1:(t + 1) * NE1], ACT.Exp,
                                      bias=peak[:, t:t + 1], accum_out=sums[:, t:t + 1])
            last.then_inc(c["expd"].sem, 1)
            for n in range(NSH * NSEQ + 1):
                if n < NSH * NSEQ:
                    act.wait_ge(c["sinner"].sem, n + 1)
                    wait(act, c["sprod"], n - 1)
                    act.activation(shsilu[:, n % 2, :], b_sh[:, (n % 2) * 2, :], ACT.Silu).then_inc(c["ssilu"].sem, 1)
                if n == 0:
                    norm.wait_xn(act)
                    act.activation(x_hi[:, :, :], g.xn[:, :, :], ACT.Copy).then_inc(c["xpart"].sem, 1)
                if n:
                    j, s = (n - 1) // NSEQ, (n - 1) % NSEQ
                    act.wait_ge(c["sprod"].sem, n)
                    act.activation(shin_hi[:, j, s * SEQ:(s + 1) * SEQ], shinner[:, (n - 1) % 2, :], ACT.Copy) \
                        .then_inc(c["shigh"].sem, 1)

            def slot(i, n):
                if live(i, n):
                    wait(act, c["inner"], n + 1, i, BODY)
                    wait(act, c["acted"], n, i, BODY)
                    act.activation(silu[:, :], b_inner[:, 0:FF1], ACT.Silu).then_inc(c["silu"].sem, 1)
                if n % 2 == 1 and live(i, n + 1):
                    q = (n + 1) // 2
                    wait(act, c["gathered"], q + 1, i, 1)
                    wait(act, c["inner"], n + 1, i, BODY)
                    act.activation(buf[:, :, :].rearrange("p c s -> p (c s)"), b_gather, ACT.Copy) \
                        .then_inc(c["buffered"].sem, 1)
                if live(i, n):
                    wait(act, c["turned"], n + 1, i, BODY)
                    wait(act, c["down"], n, i, BODY)
                    act.activation(actt[:, :, :].rearrange("p c s -> p (c s)"), b_turn, ACT.Copy) \
                        .then_inc(c["moved"].sem, 1)
                if live(i, n + 1):
                    m = n + 1
                    wait(act, c["spread1"], m + 1, i, BODY)
                    wait(act, c["summed"], m - 1, i, BODY)
                    act.activation(pickt[:, m % 2, SEQ:T], b_spread, ACT.Copy).then_inc(c["kept1"].sem, 1)

            slot(0, -1)
            slot(0, 0)
            slot(0, 1)
            with act.Fori(1, LOOPS) as i:
                for n in range(BODY):
                    slot(i, n)
            for n in range(BODY):
                slot(LOOPS, n)

        @block.gpsimd
        def _(pool):
            pool.wait_ge(c["shared_w"].sem, 32)
            for n, (w, hi, lo) in enumerate(((shgu, shgu_hi, shgu_lo), (shd, shd_hi, shd_lo))):
                w, hi, lo = (a[tuple([slice(None)] * len(a.shape))] for a in (w, hi, lo))
                pool.tensor_copy(hi, w).then_inc(c["sw_high"].sem, 1)
                pool.wait_ge(c["sw_high"].sem, n + 1)
                pool.tensor_tensor(lo, w, hi.bitcast(F32), ALU.subtract).then_inc(c["sw_low"].sem, 1)
            for n in range(NSH * NSEQ):
                pool.wait_ge(c["shigh"].sem, n + 1)
                j, s = n // NSEQ, n % NSEQ
                cut = slice(s * SEQ, (s + 1) * SEQ)
                pool.tensor_tensor(shin_lo[:, j, cut], shinner[:, n % 2, :], shin_hi[:, j, cut].bitcast(F32),
                                   ALU.subtract).then_inc(c["slow"].sem, 1)

        @block.vector
        def _(dve):
            for n in ("picked", "paired", "sloted", "kept0", "acted", "split"):
                dve.sem_inc(c[n].sem, c[n].prime)
            done = [0]

            def link(op):
                done[0] += 1
                op.then_inc(c["own_v"].sem, 1)
                dve.wait_ge(c["own_v"].sem, done[0])

            norm.vector(dve)
            norm.wait_xn(dve)
            dve.memset(score[:, :, NE1:], SENTINEL)
            dve.memset(prior[:, 0, :], 0.0)
            dve.wait_ge(c["loaded"].sem, 64)
            dve.tensor_copy(ranks[:, :], ranks1[:, :])
            dve.wait_ge(c["logits"].sem, 1)
            dve.reduce_max(peak[:, :], banks[:, 0, :].rearrange("p (t e) -> p t e", t=NT), axis=AX.X, negate=True) \
                .then_inc(c["peak"].sem, 1)
            dve.wait_ge(c["expd"].sem, 1)
            link(dve.reciprocal(sums[:, :], sums[:, :]))
            link(dve.tensor_tensor(score[:, :, 0:NE1], score[:, :, 0:NE1],
                                   sums[:, :].unsqueeze(2).broadcast_to([P, NT, NE1]), ALU.mult))
            for t in range(NT):
                op = dve.max(top[:, t, :], score[:, t, 0:NE1])
            link(op)
            link(dve.memset(top[:, :, TOP1:], SENTINEL))
            for t in range(NT):
                op = dve.match_replace(left[:, t, :], top[:, t, :], score[:, t, :], -1.0)
            link(op)
            dve.tensor_scalar(maskb[:, :, :], left[:, :, 0:NE1], 0.0, None, ALU.is_lt)
            link(dve.scalar_tensor_tensor(wrest[:, :, :], left[:, :, 0:NE1], 0.0, score[:, :, 0:NE1],
                                          ALU.is_lt, ALU.mult))
            for t in range(1, NT):
                op = dve.tensor_tensor(prior[:, t, :], prior[:, t - 1, :], maskb[:, t - 1, :], ALU.add)
                if t < NT - 1:
                    link(op)
            op.then_inc(c["masked"].sem, 1)

            def shared_product(n):
                dve.wait_ge(c["ssilu"].sem, n + 1)
                wait(dve, c["slow"], n - 1)
                dve.tensor_tensor(shinner[:, n % 2, :], shsilu[:, n % 2, :],
                                  b_sh[:, (n % 2) * 2 + 1, :], ALU.mult).then_inc(c["sprod"].sem, 1)

            shared_product(0)
            shared_product(1)
            dve.wait_ge(c["xpart"].sem, 1)
            dve.tensor_tensor(x_lo[:, :, :], g.xn[:, :, :], x_hi[:, :, :].bitcast(F32), ALU.subtract) \
                .then_inc(c["xrest"].sem, 1)
            link(dve.tensor_copy(wpart[:, :, :], wrest[:, :, :]))
            dve.tensor_copy(wparts[:, :, :, 0], wpart[:, :, :])
            link(dve.tensor_tensor(wrest[:, :, :], wrest[:, :, :], wpart[:, :, :], ALU.subtract))
            shared_product(2)
            link(dve.tensor_copy(wpart[:, :, :], wrest[:, :, :]))
            dve.tensor_copy(wparts[:, :, :, 1], wpart[:, :, :])
            link(dve.tensor_tensor(wrest[:, :, :], wrest[:, :, :], wpart[:, :, :], ALU.subtract))
            dve.tensor_copy(wparts[:, :, :, 2], wrest[:, :, :])
            shared_product(3)
            dve.wait_ge(c["places"].sem, 1)
            link(dve.tensor_scalar(place[:, :, :].rearrange("p t e -> p (t e)"), banks[:, 1, :], 1.0, 2.0 * CAP,
                                   ALU.add, ALU.min))
            link(dve.tensor_tensor(place[:, :, :], place[:, :, :], maskb[:, :, :], ALU.mult))
            shared_product(4)
            shared_product(5)
            dve.wait_ge(c["xrest"].sem, 1)
            dve.sem_inc(c["parted"].sem, 1)

            def picks(i, m):
                wait(dve, c["spread1"], m - 1, i, BODY)
                at = bass.ds((BODY * i + m) * GE, GE) if not isinstance(i, int) \
                    else slice((BODY * i + m) * GE, (BODY * i + m + 1) * GE)
                dve.tensor_tensor(pick[:, m % 2].rearrange("p t (e s) -> p t e s", s=CAP),
                                  place[:, :, at].unsqueeze(3).broadcast_to([P, NT, GE, CAP]),
                                  slot1[:, :].unsqueeze(1).unsqueeze(1).broadcast_to([P, NT, GE, CAP]),
                                  ALU.is_equal).then_inc(c["picked"].sem, 1)

            def pairs(i, q, half):
                if half == 0:
                    wait(dve, c["gathered"], q, i, 1)
                at = bass.ds((2 * i + 2 * q) * GE, 2 * GE) if not isinstance(i, int) \
                    else slice((2 * i + 2 * q) * GE, (2 * i + 2 * q + 2) * GE)
                cut = slice(half * NT // 2, (half + 1) * NT // 2)
                dve.tensor_tensor(pair[:, cut, :].rearrange("p t (e s) -> p t e s", s=CAP),
                                  place[:, cut, at].unsqueeze(3).broadcast_to([P, NT // 2, 2 * GE, CAP]),
                                  slot1[:, :].unsqueeze(1).unsqueeze(1)
                                  .broadcast_to([P, NT // 2, 2 * GE, CAP]), ALU.is_equal).then_inc(c["paired"].sem, 1)

            def slot(i, n):
                if n % 2 == 0 and live(i, n + 2):
                    pairs(i, (n + 2) // 2, 0)
                if live(i, n):
                    wait(dve, c["silu"], n + 1, i, BODY)
                    wait(dve, c["turned"], n, i, BODY)
                    dve.tensor_tensor(acted[:, :], silu[:, :], b_inner[:, FF1:2 * FF1], ALU.mult) \
                        .then_inc(c["acted"].sem, 1)
                if live(i, n + 1):
                    m = n + 1
                    wait(dve, c["spread0"], m + 1, i, BODY)
                    wait(dve, c["summed"], m - 1, i, BODY)
                    dve.tensor_copy(pickt[:, m % 2, 0:SEQ], b_spread).then_inc(c["kept0"].sem, 1)
                    wait(dve, c["weighed"], m + 1, i, BODY)
                    wait(dve, c["split"], m - 1, i, BODY)
                    dve.tensor_tensor_reduce(out=wtmp[:, m % 2, :], in0=b_weight, in1=own[:, :], scale=1.0, scalar=0.0,
                                             op0=ALU.mult, op1=ALU.add, accum_out=wslot[:, m % 2:m % 2 + 1]) \
                        .then_inc(c["sloted"].sem, 1)
                if live(i, n + 2):
                    picks(i, n + 2)
                if live(i, n):
                    k = n % 2
                    wait(dve, c["down"], n + 1, i, BODY)
                    wait(dve, c["sloted"], n + 1, i, BODY)
                    wait(dve, c["summed"], n - 1, i, BODY)
                    dve.tensor_scalar(y[:, :], b_out, wslot[:, k:k + 1], None, ALU.mult).then_inc(c["chain"].sem, 1)
                    dve.tensor_scalar(yparts[:, k, 0, :], b_out, wslot[:, k:k + 1], None, ALU.mult) \
                        .then_inc(c["chain"].sem, 1)
                    wait(dve, c["chain"], 2 * n + 2, i, 2 * BODY)
                    dve.tensor_tensor(yparts[:, k, 1, :], y[:, :], yparts[:, k, 0, :].bitcast(F32), ALU.subtract) \
                        .then_inc(c["split"].sem, 1)
                if n % 2 == 0 and live(i, n + 2):
                    pairs(i, (n + 2) // 2, 1)

            pairs(0, 0, 0)
            pairs(0, 0, 1)
            picks(0, 0)
            slot(0, -1)
            slot(0, 0)
            slot(0, 1)
            with dve.Fori(1, LOOPS) as i:
                for n in range(BODY):
                    slot(i, n)
            for n in range(BODY):
                slot(LOOPS, n)
            wait(dve, c["summed"], NG1)
            for t in range(0, NT, 2):
                x2 = g.x[:, t:t + 2, :].rearrange("p a h -> p (a h)")
                dve.tensor_tensor(x2, x2, acc[:, t:t + 2, :].rearrange("p a h -> p (a h)"), ALU.add)
    finish(nc, [*c.values(), *norm.counts])


class Shared:
    pass


def hybrid_layers_kernel(nc, ins, out):
    g = Shared()
    with (
        nc.sbuf_tensor("x", [P, NT, H], F32) as g.x,
        nc.sbuf_tensor("xn", [P, NT, H], F32) as g.xn,
        nc.sbuf_tensor("xt", [P, NC, T], F32) as g.xt,
        nc.sbuf_tensor("xh", [P, NC, T], F32R) as g.xh,
        nc.sbuf_tensor("xl", [P, NC, T], F32R) as g.xl,
        nc.sbuf_tensor("ident", [P, P], F32) as g.ident,
        nc.sbuf_tensor("identb", [P, P], BF16) as g.identb,
        nc.sbuf_tensor("zeros", [P, SEQ], BF16) as g.zeros,
        nc.sbuf_tensor("bn", [P, NT, 6], F32) as g.bn,
        nc.sbuf_tensor("mv", [P, NT, 2], F32) as g.mv,
        nc.sbuf_tensor("std", [P, NT], F32) as g.std,
        nc.sbuf_tensor("rstd", [P, NT], F32) as g.rstd,
        nc.sbuf_tensor("eps", [P, 1], F32) as g.eps,
        nc.sbuf_tensor("one", [P, 1], F32) as g.one,
        nc.sbuf_tensor("gamma", [P, NC], F32) as g.gamma,
    ):
        loaded, = counts = [Count(nc, "loaded")]
        with nc.Block() as block:
            @block.sync
            def _(sp):
                sp.dma_start(g.x[:, :, :], ins["x"]).then_inc(loaded.sem, 16)
                sp.dma_start(g.ident[:, :], ins["ident"]).then_inc(loaded.sem, 16)
                sp.dma_start(g.gamma[:, :], ins["gamma"]).then_inc(loaded.sem, 16)
                sp.wait_ge(loaded.sem, 48)

            @block.vector
            def _(dve):
                dve.memset(g.zeros[:, :], 0.0)
                dve.memset(g.eps[:, :], EPS)
                dve.memset(g.one[:, :], 1.0)
                dve.wait_ge(loaded.sem, 48)
                dve.tensor_copy(g.identb[:, :], g.ident[:, :])
        finish(nc, counts)

        stages(nc, g, ins)

        stored, = counts = [Count(nc, "stored")]
        with nc.Block() as block:
            @block.sync
            def _(sp):
                sp.dma_start(out, g.x[:, :, :]).then_inc(stored.sem, 16)
                sp.wait_ge(stored.sem, 16)


def stages(nc, g, ins):
    selective_scan(nc, g, ins)
    mixture(nc, g, ins)
    attention(nc, g, ins, "mqa", kv_every=HEADS, window=False, gamma=g.gamma, again=True)
    mixture(nc, g, ins)
    attention(nc, g, ins, "gqa", kv_every=4, window=False)
    capacity_mixture(nc, g, ins)
    attention(nc, g, ins, "mha", kv_every=1, window=True)
    capacity_mixture(nc, g, ins)


def kernel(**inputs):
    import numpy as np
    import concourse.bacc as bacc
    from concourse.bass_utils import run_bass_kernel_spmd

    a = {k: np.asarray(v) for k, v in inputs.items()}

    def chunks(w):
        w = w.reshape(*w.shape[:-2], -1, P, w.shape[-1])
        return np.moveaxis(w, -3, -2)

    def heads(w):
        return np.moveaxis(chunks(w).reshape(P, NC, -1, P), 2, 0)

    def tokens(x):
        return x.reshape(NT, P, H).transpose(1, 0, 2)

    arrays = {}
    arrays["x"] = tokens(a["L0_attn_a_hidden_states"].reshape(T, H))
    arrays["ident"] = np.eye(P, dtype=np.float32)
    arrays["gamma"] = a["L0_attn_b_gamma"].reshape(NC, P).T

    w = a["L0_attn_a_x_proj_w"].T
    bc, dt = w[:, DT_RANK:], w[:, :DT_RANK]
    arrays["xw"] = chunks(np.concatenate([bc, bc, bc, dt], 1))
    dtw = np.zeros((XROWS, H), np.float32)
    dtw[XROWS - DT_RANK:] = a["L0_attn_a_dt_proj_w"].T
    arrays["dtw"] = dtw
    arrays["vecs"] = np.concatenate([
        a["L0_attn_a_dt_proj_b"].reshape(NC, P).T, a["L0_attn_a_D"].reshape(NC, P).T,
        a["L0_attn_a_A_log"].reshape(NC, P, N_STATE).transpose(1, 0, 2).reshape(P, -1)], 1)
    arrays["pick"] = np.tile(np.eye(2 * N_STATE, dtype=np.float32), (3, 1))

    gate, up, down = (a["L0_ffn_" + n] for n in ("Wg", "Wu", "Wd"))
    sgate, sup, sdown = (a["L0_ffn_s" + n] for n in ("Wg", "Wu", "Wd"))
    gate = np.concatenate([gate, sgate.reshape(H, 2, FF0).transpose(1, 0, 2)])
    up = np.concatenate([up, sup.reshape(H, 2, FF0).transpose(1, 0, 2)])
    down = np.concatenate([down, sdown.reshape(2, FF0, H)])
    arrays["w0"] = np.concatenate([chunks(gate).reshape(NU0, P, -1), chunks(up).reshape(NU0, P, -1), down], 2)
    arrays["router0"] = chunks(a["L0_ffn_gate_w"].T)

    inv = 1.0 / np.float32(10000.0) ** (np.arange(0, P, 2, dtype=np.float32) / np.float32(P))
    angle = np.arange(SEQ, dtype=np.float32)[None, :] * inv.astype(np.float32)[:, None]
    cos, sin = np.cos(angle), np.sin(angle)
    rope = np.stack([np.concatenate([cos, cos]), np.concatenate([-sin, sin])], 1)
    arrays["rope_k"] = rope
    arrays["rope_q"] = rope * np.float32(P ** -0.5)
    q, k = np.arange(P)[:, None], np.arange(P)[None, :]
    arrays["mask"] = np.concatenate([np.where(k > q, 0, 1), np.where(k > q, 1, 0)], 1).astype(np.float32)
    pairs = np.concatenate([np.arange(0, P, 2), np.arange(1, P, 2)])

    def unpaired(w):
        return w.T.reshape(H, -1, P)[:, :, pairs].reshape(H, -1)

    kv = a["L0_attn_b_Wkv"]
    weights = {
        "mqa": (a["L0_attn_b_Wq"], kv[:, :P], kv[:, P:], a["L0_attn_b_Wo"]),
        "gqa": (unpaired(a["L1_attn_a_Wq"]), unpaired(a["L1_attn_a_Wk"]), a["L1_attn_a_Wv"].T, a["L1_attn_a_Wo"].T),
        "mha": tuple(a["L1_attn_b_" + n] for n in ("wq", "wk", "wv", "wo")),
    }
    for n, (wq, wk, wv, wo) in weights.items():
        arrays[n + "_q"] = heads(wq)
        arrays[n + "_kv"] = np.stack([heads(wk), heads(wv)], 2)
        arrays[n + "_o"] = wo.reshape(HEADS, P, H).transpose(1, 0, 2)

    gu = chunks(np.concatenate([a["L1_ffn_w_gate"], a["L1_ffn_w_up"]], 2))
    arrays["w1_gu"] = gu.reshape(NG1, GE, P, NC, 2 * FF1).transpose(0, 2, 1, 3, 4)
    arrays["w1_d"] = a["L1_ffn_w_down"].reshape(NG1, GE, 2, HF1, H).transpose(0, 3, 1, 2, 4)
    fill = NSH * P - 2 * FF1
    arrays["shared1_gu"] = np.stack([chunks(np.pad(a["L1_ffn_sw_" + n], ((0, 0), (0, fill)))) for n in ("gate", "up")], 1)
    arrays["shared1_d"] = np.pad(a["L1_ffn_sw_down"], ((0, fill), (0, 0))).reshape(NSH, P, H).transpose(1, 0, 2)
    arrays["router1"] = chunks(a["L1_ffn_gate_w"].T)
    t = np.arange(P)
    arrays["before"] = np.concatenate([(t[:, None] < t[None, :]).astype(np.float32), np.ones((P, P), np.float32)], 1)
    arrays["slot1"] = np.tile(np.arange(1, CAP + 1, dtype=np.float32), (P, 1))
    arrays["own"] = np.repeat((t[:, None] // CAP == np.arange(GE)[None, :]).astype(np.float32)[:, None, :], 3, 1) \
        .transpose(0, 2, 1).reshape(P, GE * 3)

    nc = bacc.Bacc("TRN2", target_bir_lowering=False, num_devices=1)
    sent, ins = {}, {}
    for name, v in arrays.items():
        v = np.ascontiguousarray(v, dtype=np.float32)
        sent["in_" + name] = v
        ins[name] = nc.dram_tensor("in_" + name, v.shape, F32, kind="ExternalInput").ap()
    out = nc.dram_tensor("out", (P, NT, H), F32, kind="ExternalOutput").ap()
    hybrid_layers_kernel(nc, ins, out)
    r = run_bass_kernel_spmd(nc, [sent], core_ids=[0])
    got = r.results[0]["out"]
    return got.transpose(1, 0, 2).reshape(NSEQ, SEQ, H)
```
